# Optimizing a Trainium2 kernel written in Bass

```python
import numpy as np
import jax
import jax.numpy as jnp

def _softmax(x, axis=-1):
    return jax.nn.softmax(x, axis=axis)

def _gelu(x):
    return jax.nn.gelu(x, approximate=True)

def _silu(x):
    return jax.nn.silu(x)

def _sigmoid(x):
    return jax.nn.sigmoid(x)

def _layernorm(x, axis=-1, eps=1e-05):
    m = jnp.mean(x, axis=axis, keepdims=True)
    v = jnp.var(x, axis=axis, keepdims=True)
    return (x - m) / jnp.sqrt(v + eps)

def _scatter_add(tgt, idx, src, axis=0):
    return tgt.at[idx].add(src)

def _segment_sum(src, seg, n):
    return jax.ops.segment_sum(src, seg, n)
kernel_name = 'mk_xattn_ffn_d2_seqx_r4_43a457'

def setup_inputs(seed: int=0):
    np.random.seed(seed)
    _w = jnp.asarray

    def _rec_inputs():
        import jax
        import jax.numpy as jnp
        _rk = jax.random.key(seed)
        x = -0.0002928 + 1 * jax.random.normal(jax.random.fold_in(_rk, 1), (16, 256, 256), jnp.float32)
        _lenS = 256 - jax.random.randint(jax.random.fold_in(_rk, 7), (16,), 0, max(1, 256 // 4) + 1, jnp.int32)
        _lenS2 = 256 - jax.random.randint(jax.random.fold_in(_rk, 8), (16,), 0, max(1, 256 // 4) + 1, jnp.int32)
        _ctx_1024P = jax.random.normal(jax.random.fold_in(_rk, 11), (16, 16, 256), jnp.float32)
        _ctx_1024c = jax.random.dirichlet(jax.random.fold_in(_rk, 511), 0.3 * jnp.ones((16,), jnp.float32), (16, 256))
        _ctx_1024t = jnp.einsum('bsk,bkd->bsd', _ctx_1024c, _ctx_1024P)
        _ctx_1024t = _ctx_1024t * jax.lax.rsqrt(jnp.mean(jnp.square(_ctx_1024t)) + 1e-12) * 0.953939
        ctx_1024 = -1.39393e-06 + 0.999914 * (_ctx_1024t + 0.3 * jax.random.normal(jax.random.fold_in(_rk, 611), (16, 256, 256), jnp.float32))
        return (x, ctx_1024)
    x, ctx_1024 = _rec_inputs()

    def _L0_xattn_setup():
        import jax, jax.numpy as jnp
        import numpy as np
        B, S, D, NH = (2, 512, 256, 8)
        DH = D // NH
        EPS = 1e-06
        LN_EPS = 1e-05

        def _mlstm_cell(q, k, v, igate_w, igate_b, fgate_w, fgate_b, ln_scale):
            Slen = q.shape[0]
            ifg = jnp.concatenate([q, k, v], axis=-1)
            ig = (ifg @ igate_w.T + igate_b).T
            fg = (ifg @ fgate_w.T + fgate_b).T
            qh = q.reshape(Slen, NH, DH).transpose(1, 0, 2)
            kh = k.reshape(Slen, NH, DH).transpose(1, 0, 2)
            vh = v.reshape(Slen, NH, DH).transpose(1, 0, 2)
            log_f = jax.nn.log_sigmoid(fg)
            cs = jnp.cumsum(log_f, axis=1)
            fg_mat = cs[:, :, None] - cs[:, None, :]
            mask = jnp.tril(jnp.ones((Slen, Slen), dtype=bool))
            log_fg_mat = jnp.where(mask, fg_mat, -jnp.inf)
            log_D = log_fg_mat + ig[:, None, :]
            max_log_D = jnp.max(log_D, axis=-1, keepdims=True)
            D_mat = jnp.exp(log_D - max_log_D)
            qk = jnp.einsum('hsd,htd->hst', qh, kh) / np.sqrt(DH)
            C = qk * D_mat
            normalizer = jnp.maximum(jnp.abs(C.sum(axis=-1, keepdims=True)), jnp.exp(-max_log_D))
            h = jnp.einsum('hst,htd->hsd', C / (normalizer + EPS), vh)
            h = h.transpose(1, 0, 2).reshape(Slen, D)
            mu = h.mean(axis=-1, keepdims=True)
            var = h.var(axis=-1, keepdims=True)
            return (h - mu) / jnp.sqrt(var + LN_EPS) * ln_scale
        key = jax.random.key(seed)
        ks = jax.random.split(key, 8)
        rnd = lambda k, sh, s=1.0: jax.random.normal(k, sh, dtype=jnp.float32) * s
        return {'q': rnd(ks[0], (B, S, D)), 'k': rnd(ks[1], (B, S, D)), 'v': rnd(ks[2], (B, S, D)), 'igate_w': rnd(ks[3], (NH, 3 * D), 0.02), 'igate_b': jnp.linspace(3.0, 6.0, NH, dtype=jnp.float32), 'fgate_w': rnd(ks[4], (NH, 3 * D), 0.02), 'fgate_b': rnd(ks[5], (NH,), 0.3162278), 'ln_scale': jnp.ones((D,), dtype=jnp.float32)}
    _L0_xattn_all = _L0_xattn_setup()
    _L0_xattn_in = {k: v for k, v in _L0_xattn_all.items() if k in ('igate_w', 'igate_b', 'fgate_w', 'fgate_b', 'ln_scale')}
    del _L0_xattn_all

    def _L0_ffn_setup():
        import jax, jax.numpy as jnp
        import numpy as np
        B, S, D = (4, 1024, 256)
        E, F_EXP = (16, 512)
        F_C = 2.0
        F_SH = 512
        key = jax.random.key(seed)
        ks = jax.random.split(key, 8)
        s = 0.02
        return {'hidden_states': jax.random.normal(ks[0], (B, S, D), jnp.float32), 'gate_w': jax.random.normal(ks[1], (E, D), jnp.float32) * s, 'Wg': jax.random.normal(ks[2], (E, F_EXP, D), jnp.float32) * s, 'Wu': jax.random.normal(ks[3], (E, F_EXP, D), jnp.float32) * s, 'Wd': jax.random.normal(ks[4], (E, D, F_EXP), jnp.float32) * s, 'Ws_g': jax.random.normal(ks[5], (F_SH, D), jnp.float32) * s, 'Ws_u': jax.random.normal(ks[6], (F_SH, D), jnp.float32) * s, 'Ws_d': jax.random.normal(ks[7], (D, F_SH), jnp.float32) * s}
    _L0_ffn_all = _L0_ffn_setup()
    _L0_ffn_in = {k: v for k, v in _L0_ffn_all.items() if k in ('gate_w', 'Wg', 'Wu', 'Wd', 'Ws_g', 'Ws_u', 'Ws_d')}
    del _L0_ffn_all

    def _L1_xattn_setup():
        import jax, jax.numpy as jnp
        import numpy as np
        B, L, D = (4, 1024, 256)
        key = jax.random.key(seed)
        k1, k2 = jax.random.split(key)
        Q = jax.random.normal(k1, (B, L, D), dtype=jnp.float32)
        K = jax.random.normal(k2, (B, L, D), dtype=jnp.float32)
        return {'Q': Q, 'K': K}
    _L1_xattn_all = _L1_xattn_setup()
    _L1_xattn_in = {k: v for k, v in _L1_xattn_all.items() if k in ()}
    del _L1_xattn_all

    def _L1_ffn_setup():
        import jax, jax.numpy as jnp
        import numpy as np
        D = 256
        H = 1024
        E = 8
        B = 2
        T = 512
        LN_EPS = 1e-05

        def _layer_norm(r, gamma, beta):
            mu = jnp.mean(r, axis=-1, keepdims=True)
            var = jnp.mean(jnp.square(r - mu), axis=-1, keepdims=True)
            return (r - mu) * jax.lax.rsqrt(var + LN_EPS) * gamma + beta
        key = jax.random.key(seed)
        ks = jax.random.split(key, 9)
        s_in = 1.0 / np.sqrt(D)
        s_hid = 1.0 / np.sqrt(H)
        x = jax.random.normal(ks[0], (B, T, D), dtype=jnp.float32)
        Wg = jax.random.uniform(ks[1], (D, E), jnp.float32, -s_in, s_in)
        bg = jax.random.uniform(ks[2], (E,), jnp.float32, -s_in, s_in)
        W1 = jax.random.uniform(ks[3], (E, D, H), jnp.float32, -s_in, s_in)
        b1 = jax.random.uniform(ks[4], (E, H), jnp.float32, -s_in, s_in)
        W2 = jax.random.uniform(ks[5], (E, H, D), jnp.float32, -s_hid, s_hid)
        b2 = jax.random.uniform(ks[6], (E, D), jnp.float32, -s_hid, s_hid)
        gamma = jnp.ones((D,), jnp.float32)
        beta = jnp.zeros((D,), jnp.float32)
        return {'x': x, 'Wg': Wg, 'bg': bg, 'W1': W1, 'b1': b1, 'W2': W2, 'b2': b2, 'gamma': gamma, 'beta': beta}
    _L1_ffn_all = _L1_ffn_setup()
    _L1_ffn_in = {k: v for k, v in _L1_ffn_all.items() if k in ('Wg', 'bg', 'W1', 'b1', 'W2', 'b2', 'gamma', 'beta')}
    del _L1_ffn_all
    return {'x': x, 'ctx_1024': ctx_1024, 'L0_xattn_igate_w': _L0_xattn_in['igate_w'], 'L0_xattn_igate_b': _L0_xattn_in['igate_b'], 'L0_xattn_fgate_w': _L0_xattn_in['fgate_w'], 'L0_xattn_fgate_b': _L0_xattn_in['fgate_b'], 'L0_xattn_ln_scale': _L0_xattn_in['ln_scale'], 'L0_ffn_gate_w': _L0_ffn_in['gate_w'], 'L0_ffn_Wg': _L0_ffn_in['Wg'], 'L0_ffn_Wu': _L0_ffn_in['Wu'], 'L0_ffn_Wd': _L0_ffn_in['Wd'], 'L0_ffn_Ws_g': _L0_ffn_in['Ws_g'], 'L0_ffn_Ws_u': _L0_ffn_in['Ws_u'], 'L0_ffn_Ws_d': _L0_ffn_in['Ws_d'], 'L1_ffn_Wg': _L1_ffn_in['Wg'], 'L1_ffn_bg': _L1_ffn_in['bg'], 'L1_ffn_W1': _L1_ffn_in['W1'], 'L1_ffn_b1': _L1_ffn_in['b1'], 'L1_ffn_W2': _L1_ffn_in['W2'], 'L1_ffn_b2': _L1_ffn_in['b2'], 'L1_ffn_gamma': _L1_ffn_in['gamma'], 'L1_ffn_beta': _L1_ffn_in['beta']}

def reference(x, ctx_1024, L0_xattn_igate_w, L0_xattn_igate_b, L0_xattn_fgate_w, L0_xattn_fgate_b, L0_xattn_ln_scale, L0_ffn_gate_w, L0_ffn_Wg, L0_ffn_Wu, L0_ffn_Wd, L0_ffn_Ws_g, L0_ffn_Ws_u, L0_ffn_Ws_d, L1_ffn_Wg, L1_ffn_bg, L1_ffn_W1, L1_ffn_b1, L1_ffn_W2, L1_ffn_b2, L1_ffn_gamma, L1_ffn_beta):
    import jax
    import jax.numpy as jnp

    def _L0_xattn_ref(q, k, v, igate_w, igate_b, fgate_w, fgate_b, ln_scale):
        import jax, jax.numpy as jnp
        import numpy as np
        B, S, D, NH = (2, 512, 256, 8)
        DH = D // NH
        EPS = 1e-06
        LN_EPS = 1e-05

        def _mlstm_cell(q, k, v, igate_w, igate_b, fgate_w, fgate_b, ln_scale):
            Slen = q.shape[0]
            ifg = jnp.concatenate([q, k, v], axis=-1)
            ig = (ifg @ igate_w.T + igate_b).T
            fg = (ifg @ fgate_w.T + fgate_b).T
            qh = q.reshape(Slen, NH, DH).transpose(1, 0, 2)
            kh = k.reshape(Slen, NH, DH).transpose(1, 0, 2)
            vh = v.reshape(Slen, NH, DH).transpose(1, 0, 2)
            log_f = jax.nn.log_sigmoid(fg)
            cs = jnp.cumsum(log_f, axis=1)
            fg_mat = cs[:, :, None] - cs[:, None, :]
            mask = jnp.tril(jnp.ones((Slen, Slen), dtype=bool))
            log_fg_mat = jnp.where(mask, fg_mat, -jnp.inf)
            log_D = log_fg_mat + ig[:, None, :]
            max_log_D = jnp.max(log_D, axis=-1, keepdims=True)
            D_mat = jnp.exp(log_D - max_log_D)
            qk = jnp.einsum('hsd,htd->hst', qh, kh) / np.sqrt(DH)
            C = qk * D_mat
            normalizer = jnp.maximum(jnp.abs(C.sum(axis=-1, keepdims=True)), jnp.exp(-max_log_D))
            h = jnp.einsum('hst,htd->hsd', C / (normalizer + EPS), vh)
            h = h.transpose(1, 0, 2).reshape(Slen, D)
            mu = h.mean(axis=-1, keepdims=True)
            var = h.var(axis=-1, keepdims=True)
            return (h - mu) / jnp.sqrt(var + LN_EPS) * ln_scale
        return jax.vmap(lambda qq, kk, vv: _mlstm_cell(qq, kk, vv, igate_w, igate_b, fgate_w, fgate_b, ln_scale))(q, k, v)

    def _L0_ffn_ref(hidden_states, gate_w, Wg, Wu, Wd, Ws_g, Ws_u, Ws_d):
        import jax, jax.numpy as jnp
        import numpy as np
        B, S, D = (4, 1024, 256)
        E, F_EXP = (16, 512)
        F_C = 2.0
        F_SH = 512
        b, s, d = hidden_states.shape
        e = gate_w.shape[0]
        cap = int(s * F_C / e)
        logits = jnp.einsum('bsd,ed->bse', hidden_states, gate_w)
        scores = jax.nn.softmax(logits, axis=-1).transpose(0, 2, 1)
        topk_w, topk_idx = jax.lax.top_k(scores, cap)
        x_tok = jnp.take_along_axis(hidden_states[:, None, :, :], topk_idx[..., None], axis=2)
        g = jnp.einsum('becd,efd->becf', x_tok, Wg)
        u = jnp.einsum('becd,efd->becf', x_tok, Wu)
        h = jax.nn.gelu(g, approximate=False) * u
        eo = jnp.einsum('becf,edf->becd', h, Wd) * topk_w[..., None]
        offs = (jnp.arange(b) * s)[:, None, None]
        flat_idx = (topk_idx + offs).reshape(-1)
        flat = jnp.zeros((b * s, d), hidden_states.dtype)
        flat = flat.at[flat_idx].add(eo.reshape(-1, d))
        out = flat.reshape(b, s, d)
        gs = jnp.einsum('bsd,fd->bsf', hidden_states, Ws_g)
        us = jnp.einsum('bsd,fd->bsf', hidden_states, Ws_u)
        shared = jnp.einsum('bsf,df->bsd', jax.nn.gelu(gs, approximate=False) * us, Ws_d)
        return out + shared

    def _L1_xattn_ref(Q, K):
        import jax, jax.numpy as jnp
        import numpy as np
        B, L, D = (4, 1024, 256)
        scores = jnp.einsum('btd,bsd->bts', K, K)
        Lq = Q.shape[1]
        mask = jnp.tril(jnp.ones((Lq, Lq), dtype=scores.dtype))
        scores = scores * mask[None, :, :]
        Q_proj = jnp.einsum('bts,bsd->btd', scores, Q)
        return Q + Q_proj

    def _L1_ffn_ref(x, Wg, bg, W1, b1, W2, b2, gamma, beta):
        import jax, jax.numpy as jnp
        import numpy as np
        D = 256
        H = 1024
        E = 8
        B = 2
        T = 512
        LN_EPS = 1e-05

        def _layer_norm(r, gamma, beta):
            mu = jnp.mean(r, axis=-1, keepdims=True)
            var = jnp.mean(jnp.square(r - mu), axis=-1, keepdims=True)
            return (r - mu) * jax.lax.rsqrt(var + LN_EPS) * gamma + beta
        logits = jnp.einsum('btd,de->bte', x, Wg) + bg
        top2_vals, top2_idx = jax.lax.top_k(logits, 2)
        scores = jax.nn.softmax(top2_vals, axis=-1)
        onehot = jax.nn.one_hot(top2_idx, E, dtype=x.dtype)
        combine = jnp.einsum('btk,btke->bte', scores, onehot)
        h = jnp.einsum('btd,edh->bteh', x, W1) + b1[None, None]
        h = jax.nn.gelu(h, approximate=False)
        y = jnp.einsum('bteh,ehd->bted', h, W2) + b2[None, None]
        out = jnp.einsum('bted,bte->btd', y, combine)
        return _layer_norm(x + out, gamma, beta)
    x = x + _L0_xattn_ref(_layernorm(x, axis=-1), ctx_1024, ctx_1024, L0_xattn_igate_w, L0_xattn_igate_b, L0_xattn_fgate_w, L0_xattn_fgate_b, L0_xattn_ln_scale)
    x = x + _L0_ffn_ref(_layernorm(x, axis=-1), L0_ffn_gate_w, L0_ffn_Wg, L0_ffn_Wu, L0_ffn_Wd, L0_ffn_Ws_g, L0_ffn_Ws_u, L0_ffn_Ws_d)
    x = x + _L1_xattn_ref(_layernorm(x, axis=-1), ctx_1024)
    x = x + _L1_ffn_ref(_layernorm(x, axis=-1), L1_ffn_Wg, L1_ffn_bg, L1_ffn_W1, L1_ffn_b1, L1_ffn_W2, L1_ffn_b2, L1_ffn_gamma, L1_ffn_beta)
    return x

_drawn_inputs = setup_inputs


def setup_inputs(seed=0):
    import zlib

    import numpy as np

    out = dict(_drawn_inputs(seed))
    spreads = {'L0_xattn_ln_scale': (1.0, 0.2), 'L1_ffn_gamma': (1.0, 0.6), 'L1_ffn_beta': (0.0, 0.8)}
    factors = {'L0_ffn_gate_w': 8.0,
     'L0_ffn_Wg': 8.0,
     'L0_ffn_Wu': 8.0,
     'L0_ffn_Wd': 8.0,
     'L0_ffn_Ws_g': 2.756,
     'L0_ffn_Ws_u': 2.715,
     'L0_ffn_Ws_d': 2.799,
     'L1_ffn_Wg': 8.0,
     'L1_ffn_bg': 8.0,
     'L1_ffn_W1': 8.0,
     'L1_ffn_b1': 8.0,
     'L1_ffn_W2': 8.0,
     'L1_ffn_b2': 8.0}
    for name, (base, spread) in spreads.items():
        noise = np.random.default_rng([zlib.crc32(name.encode()), seed]).standard_normal(out[name].shape)
        drawn = base * np.exp(spread * noise) if base else spread * noise
        out[name] = jnp.asarray(drawn.astype(out[name].dtype))
    for name, factor in factors.items():
        out[name] = (out[name] * factor).astype(out[name].dtype)
    return out
```

```python
import numpy as np
import concourse.bass as bass
from concourse import mybir
from contextlib import ExitStack

FP = mybir.dt.float32
BF = mybir.dt.bfloat16
U32 = mybir.dt.uint32
I32 = mybir.dt.int32
ALU = mybir.AluOpType
ACT = mybir.ActivationFunctionType
AX = mybir.AxisListType

B, S, D, NH = 16, 256, 256, 8
N = B * S
E0, F0, CAP = 16, 512, 32
E1, H1 = 8, 1024
NT = N // 128
TILES = 2 * N // 128 + E1 - 1
EPS = 1e-5
R32 = float(np.sqrt(32.0))


class Handle:
    __slots__ = ("eng", "seq", "sem", "val", "marked")

    def __init__(self, eng, sem=None, val=0):
        self.eng, self.sem, self.val, self.marked = eng, sem, val, False


def flat(x):
    if x is None:
        return
    if isinstance(x, Handle):
        yield x
    else:
        for y in x:
            yield from flat(y)


class Program:

    def __init__(self, nc, ctx):
        self.nc, self.ctx = nc, ctx
        self.q = {e: [] for e in ("tensor", "vector", "scalar", "gpsimd", "sync")}
        self.sems = {e: ctx.enter_context(nc.semaphore(f"s_{e}")) for e in self.q}
        self.lanes = {}

    def op(self, eng, fn, *after):
        h = Handle(eng)
        ws = list(flat(after))
        for w in ws:
            w.marked = True
        self.q[eng].append((fn, ws, h))
        return h

    def lane(self, name, n):
        if name not in self.lanes:
            self.lanes[name] = [[self.ctx.enter_context(self.nc.semaphore(f"d_{name}{i}")), 0, None]
                                for i in range(n)] + [0]
        return self.lanes[name]

    def dma(self, eng, name, n, fn, *after):
        l = self.lane(name, n)
        k = l[-1]
        l[-1] = (k + 1) % n
        sem, cnt, last = l[k]
        h = Handle(eng, sem, cnt + 16)
        l[k][1] += 16
        l[k][2] = h
        h.marked = True
        ws = list(flat(after)) + ([last] if last else [])
        for w in ws:
            w.marked = True
        self.q[eng].append((fn, ws, h))
        return h

    def barrier(self):
        hs = []
        for e in self.q:
            own = [h for _, _, h in self.q[e] if h is not None and h.sem is None]
            hs += own[-1:]
        for l in self.lanes.values():
            hs += [x[2] for x in l[:-1] if x[2]]
        for h in hs:
            h.marked = True
        for e in self.q:
            self.q[e].append((None, hs, None))

    def emit(self, block):
        for e in self.q:
            n = 0
            for fn, ws, h in self.q[e]:
                if h is not None and h.sem is None and h.marked:
                    n += 1
                    h.val = n
                    h.sem = self.sems[e]

        def replay(eng, e):
            seen = {}
            for fn, ws, h in self.q[e]:
                need = {}
                for w in ws:
                    need[w.sem] = max(need.get(w.sem, 0), w.val)
                for s, v in need.items():
                    if seen.get(s, 0) < v:
                        eng.wait_ge(s, v)
                        seen[s] = v
                if fn is None:
                    continue
                ins = fn(eng)
                if h.marked:
                    ins.then_inc(h.sem, 1 if h.sem is self.sems[e] else 16)

        for e in self.q:
            register = {"tensor": block.tensor, "vector": block.vector, "scalar": block.scalar,
                             "gpsimd": block.gpsimd, "sync": block.sync}[e]
            register(lambda eng, e=e: replay(eng, e))


class Slot:

    def __init__(self, t):
        self.t, self.free = t, []


class Ring:
    def __init__(self, slots):
        self.slots, self.i = slots, -1

    def next(self):
        self.i = (self.i + 1) % len(self.slots)
        return self.slots[self.i]


def build(nc, A, out, stop=99):
    ctx = ExitStack()
    with ctx:
        P = Program(nc, ctx)

        def sem(name):
            return ctx.enter_context(nc.semaphore(name))

        def dram(name, shape, dt=FP):
            return nc.dram_tensor(name, shape, dt, kind="Internal").ap()

        dH = dram("dH", [N, D])
        dACC = dram("dACC", [N, D])
        dX3 = dram("dX3", [N, D])
        dXS = dram("dXS", [TILES * 128, D])
        dYS = dram("dYS", [TILES * 128, D])

        banks = [Slot(ctx.enter_context(nc.psum_tensor(f"pb{i}", [128, 512], FP))) for i in range(8)]

        class Mem:
            made = 0

            def __init__(self):
                self.st = ExitStack()

            def sb(self, name, shape, dt=FP):
                Mem.made += 1
                return self.st.enter_context(nc.sbuf_tensor(f"{name}_{Mem.made}", shape, dt))

            def ring(self, name, n, shape, dt=FP):
                return Ring([Slot(self.sb(f"{name}{i}", shape, dt)) for i in range(n)])

        G = Mem()
        ctx.enter_context(G.st)

        pe = lambda fn, *a: P.op("tensor", fn, *a)
        dve = lambda fn, *a: P.op("vector", fn, *a)
        act = lambda fn, *a: P.op("scalar", fn, *a)
        pool = lambda fn, *a: P.op("gpsimd", fn, *a)

        def load(out_, in_, *a, n=8):
            return P.dma("sync", "ld", n, lambda e: e.dma_start(out_, in_), *a)

        def store(out_, in_, *a, n=4):
            return P.dma("sync", "st", n, lambda e: e.dma_start(out_, in_), *a)

        def mm(o, l, r, s, t, *a):
            return pe(lambda e: e.matmul(o, l, r, start=s, stop=t), *a)

        def tr(o, i, idn, *a):
            return pe(lambda e: e.transpose(o, i, idn), *a)

        ident = G.sb("ident", [128, 128])
        ones = G.sb("ones", [128, 256])
        hm8 = G.sb("hm8", [128, 8])
        hm4 = G.sb("hm4", [128, 4])
        tri = G.sb("tri", [128, 128])
        stri = G.sb("stri", [128, 128])
        idxJ = G.sb("idxJ", [128, 4, E0], U32)
        wJ = G.sb("wJ", [128, 4, E0])
        lg1 = G.sb("lg1", [128, NT, E1])

        c_id0 = pool(lambda e: e.memset(ident[:, :], 0.0))
        c_ones = pool(lambda e: e.memset(ones[:, :], 1.0))
        c_id = pool(lambda e: e.affine_select(out=ident[:, :], in_=ident[:, :], compare_op=ALU.not_equal, fill=1.0,
                                              base=0, pattern=[[-1, 128]], channel_multiplier=1), c_id0)
        c = None
        for j in range(4):
            c = dve(lambda e, j=j: e.tensor_copy(hm8[32 * j:32 * j + 32, :], ident[0:32, 0:8]), c_id)
        c_h8 = c
        c_a = pool(lambda e: e.affine_select(out=hm4[:, :], in_=ones[:, 0:4], compare_op=ALU.is_ge, fill=0.0,
                                             base=0, pattern=[[-32, 4]], channel_multiplier=1), c_ones)
        c_h4 = pool(lambda e: e.affine_select(out=hm4[:, :], in_=hm4[:, :], compare_op=ALU.is_ge, fill=0.0,
                                              base=31, pattern=[[32, 4]], channel_multiplier=-1), c_a)
        c_tri = pool(lambda e: e.affine_select(out=tri[:, :], in_=ones[:, 0:128], compare_op=ALU.is_ge, fill=0.0,
                                               base=0, pattern=[[1, 128]], channel_multiplier=-1), c_ones)
        c_stri = pool(lambda e: e.affine_select(out=stri[:, :], in_=ones[:, 0:128], compare_op=ALU.is_gt, fill=0.0,
                                                base=0, pattern=[[1, 128]], channel_multiplier=-1), c_ones)
        mhalf = G.sb("mhalf", [128, 1])
        c_mh = pool(lambda e: e.memset(mhalf[:, :], -0.5))
        identb = G.sb("identb", [128, 128], BF)
        maskb = G.sb("maskb", [128, 128], BF)
        c_mk = [dve(lambda e: e.tensor_copy(identb[:, :], ident[:, :]), c_id),
                dve(lambda e: e.tensor_scalar(maskb[:, :], tri[:, :], 1.0, 1e30, ALU.subtract, ALU.mult), c_tri)]
        consts = [c_id, c_ones, c_h8, c_h4, c_tri, c_stri]

        M1 = Mem()
        gw0 = M1.sb("gw0", [128, 2, 6, 32])
        gw = M1.sb("gw", [128, 2, 4, 32])
        gb = M1.sb("gb", [128, 2])
        lns = M1.sb("lns", [128, D])
        rw = M1.sb("rw", [128, 2, E0])
        wsg = M1.sb("wsg", [128, 2, F0])
        wsu = M1.sb("wsu", [128, 2, F0])
        wsd = M1.sb("wsd", [128, 4, D])
        z1 = pool(lambda e: e.memset(gw0[:, :, :, :], 0.0))
        z2 = pool(lambda e: e.memset(gb[:, :], 0.0))
        ld = []
        for t, w in enumerate((A["igate_w"], A["fgate_w"])):
            for k in range(6):
                ld.append(load(gw0[:, t, k, 0:8], w[k], z1))
        for t, w in enumerate((A["igate_b"], A["fgate_b"])):
            for j in range(4):
                ld.append(load(gb[32 * j:32 * j + 8, t:t + 1], w.rearrange("(p a) -> p a", a=1), z2))
        ld_ln = load(lns[:, :], A["ln_scale"].rearrange("(a n) -> a n", a=1).to_broadcast([128, D]))
        ld_rw = load(rw[:, :, :], A["gate_w"].rearrange("(k p) e -> p k e", p=128))
        ld_ws = [load(wsg[:, :, :], A["Ws_g"].rearrange("(k p) f -> p k f", p=128)),
                 load(wsu[:, :, :], A["Ws_u"].rearrange("(k p) f -> p k f", p=128)),
                 load(wsd[:, :, :], A["Ws_d"].rearrange("(k p) f -> p k f", p=128))]
        g1 = dve(lambda e: e.tensor_copy(gw[:, :, 0:2, :], gw0[:, :, 0:2, :]), ld)
        g2 = dve(lambda e: e.tensor_tensor(gw[:, :, 2:4, :], gw0[:, :, 2:4, :], gw0[:, :, 4:6, :], ALU.add), ld)
        ld_gw = [g1, g2]

        rX = M1.ring("xb", 4, [128, 2, D])
        rC = M1.ring("cb", 4, [128, 2, D])
        rCT = M1.ring("cT", 4, [128, 2, S])
        rQ = M1.ring("q", 2, [128, 2, D])
        rQT = M1.ring("qT", 4, [128, 2, S])
        small = M1.ring("sm", 4, [128, 2, 16])
        rHT = M1.ring("hT", 2, [128, 2, 512])
        rX1 = M1.ring("x1", 4, [128, 2, D])

        T, GB, SB0, SB1, BB0, BB1, O1, O2 = banks

        def layernorm(src, dst, after, dst_free, c):
            sm = small.next()
            s = sm.t
            h = dve(lambda e: e.bn_stats(s[:, c, 0:6], src), after, sm.free)
            h = dve(lambda e: e.bn_aggr(s[:, c, 6:8], s[:, c, 0:6]), h)
            h = dve(lambda e: e.tensor_scalar(s[:, c, 9:10], s[:, c, 7:8], EPS, None, ALU.add), h)
            h = pool(lambda e: e.tensor_tensor(s[:, c, 8:9], s[:, c, 9:10], mhalf[:, :], ALU.pow), h, c_mh)
            h = dve(lambda e: e.tensor_scalar(dst, src, s[:, c, 6:7], s[:, c, 8:9], ALU.subtract, ALU.mult),
                    h, dst_free)
            sm.free = [h]
            return h

        row = {n: M1.sb(n, [128, S]) for n in ("igr", "zr", "er", "lr", "csr", "ar", "Mr", "nMr", "tr", "eer")}
        wfr = M1.sb("wfr", [128, S])
        Mx = M1.sb("Mx", [128, 8, S])
        cols = M1.sb("cols", [128, 6, 128])
        colrel = []
        rowrel = []
        mxrel = []
        rqx = M1.ring("qx", 2, [128, 2, 4, 128])
        rD = M1.ring("Dm", 2, [128, 8, 128])
        rCm = M1.ring("Cm", 2, [128, 8, 128])
        rV = M1.ring("V1", 2, [128, 2, 8, 33])
        rW = M1.ring("wV", 2, [128, 8, 33])
        rKV = M1.ring("KV", 2, [128, 2, 4, 33])
        rO = M1.ring("Oo", 2, [128, 8, 33])
        rn = M1.ring("nn", 2, [128, 3, 8])
        rh = M1.ring("hh1", 2, [128, D])
        rH = M1.ring("Ht", 2, [128, D])
        lgt = M1.sb("lgt", [128, 2, 8, E0])
        lgrel = [[]]
        rg = M1.ring("gs", 2, [128, 512])
        rhh = M1.ring("hhs", 1, [128, 4, 512])
        rys = M1.ring("ys", 2, [128, D])

        for sl in rV.slots:
            sl.free = [pool(lambda e, t=sl.t: e.memset(t[:, :, :, 32:33], 1.0))]

        LG = []
        for g in range(4):
            info = []
            gates = []
            for j in range(4):
                b = 4 * g + j
                x, cb, cT = rX.next(), rC.next(), rCT.next()
                rows = slice(256 * b, 256 * b + 256)
                lx = load(x.t[:, :, :], A["x"][rows, :].rearrange("(c p) d -> p c d", p=128), x.free)
                lc = load(cb.t[:, :, :], A["ctx"][rows, :].rearrange("(c p) d -> p c d", p=128), cb.free)
                lct = load(cT.t[:, :, :], A["ctxT"][:, rows].rearrange("(k p) t -> p k t", p=128), cT.free)
                q, qT = rQ.next(), rQT.next()
                hq = [layernorm(x.t[:, c, :], q.t[:, c, :], lx, q.free, c) for c in range(2)]
                tv = T.t[:, :].rearrange("p (k t) -> p k t", k=2)
                for k in range(2):
                    for c in range(2):
                        h = tr(tv[:, k, 128 * c:128 * c + 128], q.t[:, c, 128 * k:128 * k + 128], ident[:, :],
                               hq, consts, T.free)
                q.free = [h]
                hqT = act(lambda e, o=qT.t, i=tv: e.copy(o[:, :, :], i), h, qT.free)
                T.free = [hqT]
                for t in range(2):
                    for k in range(4):
                        rhs = qT.t[:, k, :] if k < 2 else cT.t[:, k - 2, :]
                        h = mm(GB.t[32 * j:32 * j + 32, 256 * t:256 * t + 256], gw[:, t, k, :], rhs,
                               k == 0, k == 3, hqT, lct, ld_gw, GB.free)
                gates.append(h)
                info.append((b, x, cb, cT, qT, lc, lct, hqT))
            r = row
            gt = GB.t
            h1 = dve(lambda e: e.tensor_scalar(r["igr"][:, :], gt[:, 0:256], gb[:, 0:1], None, ALU.add), gates, ld, rowrel)
            h2 = dve(lambda e: e.tensor_scalar(r["zr"][:, :], gt[:, 256:512], gb[:, 1:2], None, ALU.add), gates, ld, rowrel)
            GB.free = [h1, h2]
            h3 = dve(lambda e: e.scalar_tensor_tensor(out=r["er"][:, :], in0=r["zr"][:, :], scalar=-1.0, in1=r["zr"][:, :],
                                                      op0=ALU.mult, op1=ALU.min), h2)
            h4 = act(lambda e: e.activation(r["lr"][:, :], r["er"][:, :], ACT.Exp), h3)
            h4 = act(lambda e: e.activation(r["lr"][:, :], r["lr"][:, :], ACT.Ln, bias=ones[:, 0:1]), h4, c_ones)
            h5 = dve(lambda e: e.scalar_tensor_tensor(out=r["zr"][:, :], in0=r["zr"][:, :], scalar=0.0, in1=r["lr"][:, :],
                                                      op0=ALU.min, op1=ALU.subtract), h4)
            h6 = dve(lambda e: e.tensor_tensor_scan(r["csr"][:, :], ones[:, 0:256], r["zr"][:, :], 0.0, ALU.mult, ALU.add), h5)
            h7 = dve(lambda e: e.tensor_tensor(r["ar"][:, :], r["igr"][:, :], r["csr"][:, :], ALU.subtract), h6, h1)
            h8 = dve(lambda e: e.tensor_tensor_scan(r["Mr"][:, :], r["ar"][:, :], r["ar"][:, :], -3.0e38, ALU.max, ALU.max), h7)
            h9 = dve(lambda e: e.tensor_scalar(r["nMr"][:, :], r["Mr"][:, :], -1.0, None, ALU.mult), h8)
            h10 = dve(lambda e: e.tensor_tensor(r["tr"][:, :], r["csr"][:, :], r["Mr"][:, :], ALU.add), h8)
            h11 = act(lambda e: e.activation(r["eer"][:, :], r["tr"][:, :], ACT.Exp, scale=-1.0), h10)
            h12 = act(lambda e: e.activation(wfr[:, 0:128], r["ar"][:, 0:128], ACT.Exp, bias=r["nMr"][:, 127:128]), h9, rowrel)
            h13 = act(lambda e: e.activation(wfr[:, 128:256], r["nMr"][:, 128:256], ACT.Exp, bias=r["Mr"][:, 127:128]), h9)
            hmx = dve(lambda e: e.tensor_tensor(Mx[:, :, :], r["nMr"][:, :].unsqueeze(1).to_broadcast([128, 8, S]),
                                                hm8[:, :].unsqueeze(2).to_broadcast([128, 8, S]), ALU.mult), h9, c_h8, mxrel)
            srcs = [r["ar"][:, 0:128], r["ar"][:, 128:256], r["eer"][:, 0:128], r["eer"][:, 128:256],
                    wfr[:, 0:128], wfr[:, 128:256]]
            newcol = []
            ht = []
            for i0 in (0, 3):
                for i in range(i0, i0 + 3):
                    h = tr(T.t[:, 128 * (i - i0):128 * (i - i0) + 128], srcs[i], ident[:, :], h7, h11, h12, h13, T.free)
                ht.append(h)
                h = act(lambda e, i0=i0: e.copy(cols[:, i0:i0 + 3, :], T.t[:, 0:384].rearrange("p (i t) -> p i t", i=3)),
                        h, colrel)
                T.free = [h]
                newcol.append(h)
            rowrel = [ht[-1], hmx]
            colrel, mxrel = [], []

            for j, (b, x, cb, cT, qT, lc, lct, hqT) in enumerate(info):
                jc = slice(32 * j, 32 * j + 8)
                V = rV.next()
                hV = act(lambda e, V=V, cb=cb: e.copy(V.t[:, :, :, 0:32], cb.t[:, :, :].rearrange("p c (h d) -> p c h d", h=8)), lc, V.free)
                wV = rW.next()
                hW = dve(lambda e, V=V, wV=wV, jc=jc: e.tensor_tensor(wV.t[:, :, :], V.t[:, 0, :, :],
                         cols[:, 4, jc].unsqueeze(2).to_broadcast([128, 8, 33]), ALU.mult), hV, newcol, wV.free)
                x1 = rX1.next()
                if b % 2 == 0:
                    hT = rHT.next()
                    hTw, x1w = [], []
                KV = rKV.next()
                for c in range(2):
                    cs_ = slice(128 * c, 128 * c + 128)
                    qx = rqx.next()
                    for k in range(2):
                        h = dve(lambda e, qx=qx, k=k, qT=qT, cs_=cs_: e.tensor_tensor(qx.t[:, k, :, :],
                                qT.t[:, k, cs_].unsqueeze(1).to_broadcast([128, 4, 128]),
                                hm4[:, :].unsqueeze(2).to_broadcast([128, 4, 128]), ALU.mult), hqT, c_h4, qx.free)
                    hqx = h
                    for k, bk in enumerate((SB0, SB1)):
                        hs = mm(bk.t[:, :], cT.t[:, k, cs_], qx.t[:, k, :, :], True, True, hqx, lct, bk.free)
                    qx.free = [hs]
                    hbs = []
                    for k, bk in enumerate((BB0, BB1)):
                        mm(bk.t[:, :], identb[:, :], maskb[:, :].unsqueeze(1).to_broadcast([128, 4, 128]), True, False,
                           c_mk, bk.free)
                        hb = mm(bk.t[:, :], ones[32 * j:32 * j + 32, 0:128], Mx[32 * j:32 * j + 32, 4 * k:4 * k + 4, cs_],
                                False, True, hmx)
                        hbs.append(hb)
                    mxrel.append(hb)
                    Dm = rD.next()
                    he = []
                    for hd in range(8):
                        bk = (BB0, BB1)[hd // 4]
                        h = act(lambda e, Dm=Dm, bk=bk, hd=hd, c=c, j=j: e.activation(Dm.t[:, hd, :],
                                bk.t[:, 128 * (hd % 4):128 * (hd % 4) + 128], ACT.Exp,
                                bias=cols[:, c, 32 * j + hd:32 * j + hd + 1]), hbs[hd // 4], newcol, Dm.free)
                        bk.free = [h]
                    hD = h
                    Cm = rCm.next()
                    for k, bk in enumerate((SB0, SB1)):
                        h = dve(lambda e, Cm=Cm, Dm=Dm, k=k, bk=bk: e.tensor_tensor(Cm.t[:, 4 * k:4 * k + 4, :],
                                bk.t[:, :].rearrange("p (h s) -> p h s", h=4), Dm.t[:, 4 * k:4 * k + 4, :], ALU.mult),
                                hD, hs, Cm.free)
                        bk.free = [h]
                    Dm.free = [h]
                    hC = h
                    for hd in range(8):
                        h = mm(O1.t[:, 33 * hd:33 * hd + 33], Cm.t[:, hd, :], V.t[:, c, hd, :], True, True, hC, hV, O1.free)
                    Cm.free = [h]
                    hO1 = h
                    O = rO.next()
                    if c == 0:
                        for k in range(2):
                            h = mm(O2.t[:, 132 * k:132 * k + 132], cb.t[:, 0, 128 * k:128 * k + 128],
                                   wV.t[:, 4 * k:4 * k + 4, :], True, True, hW, lc, O2.free)
                        wV.free = [h]
                        hKV = dve(lambda e, KV=KV: e.tensor_tensor(KV.t[:, :, :, :],
                                  O2.t[:, 0:264].rearrange("p (k h d) -> p k h d", k=2, h=4),
                                  hm4[:, :].unsqueeze(1).unsqueeze(3).to_broadcast([128, 2, 4, 33]), ALU.mult), h, KV.free)
                        O2.free = [hKV]
                        hO = dve(lambda e, O=O: e.tensor_copy(O.t[:, :, :], O1.t[:, 0:264].rearrange("p (h d) -> p h d", h=8)),
                                 hO1, O.free)
                        O1.free = [hO]
                    else:
                        for k in range(2):
                            h = mm(O2.t[:, 132 * k:132 * k + 132], qT.t[:, k, cs_], KV.t[:, k, :, :], True, True,
                                   hKV, O2.free)
                        KV.free = [h]
                        hO = dve(lambda e, O=O, jc=jc: e.tensor_tensor(O.t[:, :, :],
                                 O2.t[:, 0:264].rearrange("p (h d) -> p h d", h=8),
                                 cols[:, 5, jc].unsqueeze(2).to_broadcast([128, 8, 33]), ALU.mult), h, O.free, newcol)
                        O2.free = [hO]
                        hO = dve(lambda e, O=O: e.tensor_tensor(O.t[:, :, :], O.t[:, :, :],
                                 O1.t[:, 0:264].rearrange("p (h d) -> p h d", h=8), ALU.add), hO, hO1)
                        O1.free = [hO]
                        V.free = [hO1]
                    nn = rn.next()
                    h = dve(lambda e, nn=nn, c=c, jc=jc: e.tensor_scalar(nn.t[:, 0, :], cols[:, 2 + c, jc], R32, None, ALU.mult),
                            newcol, nn.free)
                    h = dve(lambda e, nn=nn, O=O: e.scalar_tensor_tensor(out=nn.t[:, 1, :], in0=O.t[:, :, 32], scalar=-1.0,
                            in1=O.t[:, :, 32], op0=ALU.mult, op1=ALU.max), hO, h)
                    h = dve(lambda e, nn=nn: e.tensor_tensor(nn.t[:, 1, :], nn.t[:, 1, :], nn.t[:, 0, :], ALU.max), h)
                    h = dve(lambda e, nn=nn: e.tensor_scalar(nn.t[:, 1, :], nn.t[:, 1, :], R32 * 1e-6, None, ALU.add), h)
                    h = dve(lambda e, nn=nn: e.reciprocal(nn.t[:, 2, :], nn.t[:, 1, :]), h)
                    hh = rh.next()
                    h = dve(lambda e, nn=nn, O=O, hh=hh: e.tensor_tensor(hh.t[:, :].rearrange("p (h d) -> p h d", h=8),
                            O.t[:, :, 0:32], nn.t[:, 2, :].unsqueeze(2).to_broadcast([128, 8, 32]), ALU.mult), h, hh.free)
                    nn.free, O.free = [h], [h]
                    h = layernorm(hh.t[:, :], hh.t[:, :], h, None, c)
                    h = dve(lambda e, hh=hh: e.tensor_tensor(hh.t[:, :], hh.t[:, :], lns[:, :], ALU.mult), h, ld_ln)
                    hx1 = dve(lambda e, hh=hh, x1=x1, x=x, c=c: e.tensor_tensor(x1.t[:, c, :], hh.t[:, :], x.t[:, c, :], ALU.add),
                              h, x1.free)
                    hh.free = [hx1]
                    Ht = rH.next()
                    hH = layernorm(x1.t[:, c, :], Ht.t[:, :], hx1, Ht.free, c)
                    sH = store(dH[256 * b + 128 * c:256 * b + 128 * c + 128, :], Ht.t[:, :], hH)
                    for k in range(2):
                        h = tr(T.t[:, 128 * k:128 * k + 128], Ht.t[:, 128 * k:128 * k + 128], ident[:, :], hH, T.free)
                    Ht.free = [h, sH]
                    t0 = 256 * (b % 2) + 128 * c
                    hhT = act(lambda e, hT=hT, t0=t0: e.copy(hT.t[:, :, t0:t0 + 128], T.t[:, 0:256].rearrange("p (k t) -> p k t", k=2)),
                              h, hT.free)
                    T.free = [hhT]
                    hTw.append(hhT)
                    x1w.append(hx1)
                    for k in range(2):
                        h = mm(T.t[:, 0:E0], hT.t[:, k, t0:t0 + 128], rw[:, k, :], k == 0, k == 1, hhT, ld_rw, T.free)
                    h = act(lambda e, b=b, c=c: e.copy(lgt[:, c, b % 8, :], T.t[:, 0:E0]), h, lgrel[0])
                    T.free = [h]
                    LG.append(h)
                    x1.own = (b, c)
                colrel.append(hx1)
                x.free, cb.free, cT.free, qT.free = [hx1], [hO1, hKV], [hs], [hs, hO]
                if b % 2 == 1:
                    hhs = rhh.next()
                    ws = []
                    for f in range(4):
                        fs = slice(128 * f, 128 * f + 128)
                        bg, bu = ((SB0, BB0), (SB1, BB1))[f % 2]
                        for k in range(2):
                            hg = mm(bg.t[:, :], wsg[:, k, fs], hT.t[:, k, :], k == 0, k == 1, hTw, ld_ws, bg.free)
                        for k in range(2):
                            hu = mm(bu.t[:, :], wsu[:, k, fs], hT.t[:, k, :], k == 0, k == 1, bu.free)
                        gs = rg.next()
                        h = act(lambda e, gs=gs, bg=bg: e.activation(gs.t[:, :], bg.t[:, :], ACT.Gelu), hg, gs.free)
                        bg.free = [h]
                        h = dve(lambda e, gs=gs, bu=bu, f=f, hhs=hhs: e.tensor_tensor(hhs.t[:, f, :], gs.t[:, :], bu.t[:, :], ALU.mult),
                                h, hu, hhs.free)
                        gs.free, bu.free = [h], [h]
                        ws.append(h)
                    hT.free = [hu]
                    for tt in range(4):
                        ybk = (O1, O2)[tt % 2]
                        for f in range(4):
                            h = mm(ybk.t[:, 0:256], hhs.t[:, f, 128 * tt:128 * tt + 128], wsd[:, f, :], f == 0, f == 3, ws, ybk.free)
                        hy = h
                        ys = rys.next()
                        xs = prev_x1 if tt < 2 else x1
                        h = dve(lambda e, ys=ys, ybk=ybk, xs=xs, tt=tt: e.tensor_tensor(ys.t[:, :], ybk.t[:, 0:256], xs.t[:, tt % 2, :], ALU.add),
                                hy, ys.free, x1w)
                        ybk.free = [h]
                        xs.free = [h]
                        r0 = 256 * (b - 1) + 128 * tt
                        ys.free = [store(dACC[r0:r0 + 128, :], ys.t[:, :], h)]
                    hhs.free = [hy]
                prev_x1 = x1
            if g % 2 == 1:
                G8 = g // 2
                if g == 1:
                    sm1 = M1.sb("sm1", [128, 16])
                    sc = M1.sb("sc", [128, S])
                    sc2 = M1.sb("sc2", [128, S])
                    vals = M1.sb("vals", [128, CAP])
                    ix = M1.sb("ix", [128, CAP], U32)
                    ixf = M1.sb("ixf", [128, CAP])
                    bof = M1.sb("bof", [128, 1])
                    bofi = M1.sb("bofi", [128, 1], I32)
                    rt = []
                l3 = lgt[:, :, :, :].rearrange("p c b e -> p (c b) e")
                h = dve(lambda e: e.tensor_reduce(sm1[:, :], l3, AX.X, ALU.max), LG, rt)
                h = dve(lambda e: e.tensor_tensor(l3, l3, sm1[:, :].unsqueeze(2).to_broadcast([128, 16, E0]), ALU.subtract), h)
                h = act(lambda e: e.activation(l3, l3, ACT.Exp), h)
                h = dve(lambda e: e.tensor_reduce(sm1[:, :], l3, AX.X, ALU.add), h)
                h = dve(lambda e: e.reciprocal(sm1[:, :], sm1[:, :]), h)
                h = dve(lambda e: e.tensor_tensor(l3, l3, sm1[:, :].unsqueeze(2).to_broadcast([128, 16, E0]), ALU.mult), h)
                for c in range(2):
                    ht_ = tr(T.t[:, 128 * c:128 * c + 128], lgt[:, c, :, :], ident[:, :], h, T.free)
                lgrel[0] = [ht_]
                LG = []
                h = act(lambda e: e.copy(sc[:, :], T.t[:, 0:256]), ht_, rt)
                T.free = [h]
                for rd in range(4):
                    v8, i8 = vals[:, 8 * rd:8 * rd + 8], ix[:, 8 * rd:8 * rd + 8]
                    a, bb = (sc, sc2) if rd % 2 == 0 else (sc2, sc)
                    h = dve(lambda e, v8=v8, a=a: e.max(v8, a[:, :]), h, rt)
                    h = dve(lambda e, v8=v8, a=a, i8=i8: e.max_index(i8, v8, a[:, :]), h)
                    if rd < 3:
                        h = dve(lambda e, v8=v8, a=a, bb=bb: e.match_replace(bb[:, :], v8, a[:, :], -1.0), h)
                hb = pool(lambda e, G8=G8: e.iota(bofi[:, :], [[0, 1]], base=0, channel_multiplier=1), rt)
                hb = dve(lambda e: e.tensor_scalar(bofi[:, :], bofi[:, :], 4, 8, ALU.arith_shift_right, ALU.arith_shift_left), hb)
                hb = dve(lambda e, G8=G8: e.tensor_scalar(bof[:, :], bofi[:, :], float(2048 * G8), None, ALU.add), hb)
                h = dve(lambda e: e.tensor_scalar(ixf[:, :], ix[:, :], bof[:, 0:1], None, ALU.add), h, hb)
                h1 = tr(T.t[0:32, 0:128], ixf[:, :], ident[:, :], h, T.free)
                h1 = tr(T.t[0:32, 128:256], vals[:, :], ident[:, :], h)
                rt = [h1]
                hh_ = []
                for bl in range(8):
                    jj, bg = bl % 4, 2 * G8 + bl // 4
                    ps = slice(32 * jj, 32 * jj + 32)
                    h = dve(lambda e, ps=ps, bg=bg, bl=bl: e.tensor_copy(idxJ[ps, bg, :], T.t[0:32, 16 * bl:16 * bl + 16]), h1)
                    h = dve(lambda e, ps=ps, bg=bg, bl=bl: e.tensor_copy(wJ[ps, bg, :], T.t[0:32, 128 + 16 * bl:128 + 16 * bl + 16]), h1)
                T.free = [h]
        P.barrier()
        M1.st.close()
        for s in banks:
            s.free = []

        if stop >= 2:
            M2 = Mem()
            rwg = M2.ring("wg", 2, [128, 2, F0])
            rwu = M2.ring("wu", 2, [128, 2, F0])
            rwd = M2.ring("wd", 2, [128, 4, D])
            rxe = M2.ring("xe", 2, [128, 4, D])
            rxT = M2.ring("xeT", 2, [128, 2, 512])
            rg = M2.ring("g2", 2, [128, 512])
            rhh = M2.ring("h2", 2, [128, 4, 512])
            rye = M2.ring("ye", 2, [128, 4, D])
            GBK = Ring(banks[0:2])
            UBK = Ring(banks[2:4])
            TBK = Ring(banks[4:6])
            YBK = Ring(banks[6:8])
            scat = []
            for x in range(E0):
                wg, wu, wd, xe, xT, hhs, ye = (r.next() for r in (rwg, rwu, rwd, rxe, rxT, rhh, rye))
                lw = [load(wg.t[:, :, :], A["Wg"][x].rearrange("(k p) f -> p k f", p=128), wg.free),
                      load(wu.t[:, :, :], A["Wu"][x].rearrange("(k p) f -> p k f", p=128), wu.free)]
                lwd = load(wd.t[:, :, :], A["Wd"][x].rearrange("(k p) f -> p k f", p=128), wd.free)
                xw = []
                for bg in range(4):
                    ga = P.dma("gpsimd", "ga", 4, lambda e, xe=xe, bg=bg, x=x: e.indirect_dma_start(
                        out=xe.t[:, bg, :], out_offset=None, in_=dH[:, :],
                        in_offset=bass.IndirectOffsetOnAxis(ap=idxJ[:, bg, x:x + 1], axis=0)), xe.free)
                    tb = TBK.next()
                    for k in range(2):
                        h = tr(tb.t[:, 128 * k:128 * k + 128], xe.t[:, bg, 128 * k:128 * k + 128], ident[:, :], ga, tb.free)
                    hx = h
                    h = act(lambda e, xT=xT, tb=tb, bg=bg: e.copy(xT.t[:, :, 128 * bg:128 * bg + 128],
                            tb.t[:, 0:256].rearrange("p (k t) -> p k t", k=2)), h, xT.free)
                    tb.free = [h]
                    xw.append(h)
                xe.free = [hx]
                ws = []
                for f in range(4):
                    fs = slice(128 * f, 128 * f + 128)
                    bgk, bu = GBK.next(), UBK.next()
                    for k in range(2):
                        hg = mm(bgk.t[:, :], wg.t[:, k, fs], xT.t[:, k, :], k == 0, k == 1, xw, lw, bgk.free)
                    for k in range(2):
                        hu = mm(bu.t[:, :], wu.t[:, k, fs], xT.t[:, k, :], k == 0, k == 1, bu.free)
                    gs = rg.next()
                    h = act(lambda e, gs=gs, bgk=bgk: e.activation(gs.t[:, :], bgk.t[:, :], ACT.Gelu), hg, gs.free)
                    bgk.free = [h]
                    h = dve(lambda e, gs=gs, bu=bu, f=f, hhs=hhs: e.tensor_tensor(hhs.t[:, f, :], gs.t[:, :], bu.t[:, :], ALU.mult),
                            h, hu, hhs.free)
                    gs.free, bu.free = [h], [h]
                    ws.append(h)
                xT.free, wg.free, wu.free = [hu], [hu], [hu]
                prev = scat
                scat = []
                for tt in range(4):
                    yb = YBK.next()
                    for f in range(4):
                        hy = mm(yb.t[:, 0:256], hhs.t[:, f, 128 * tt:128 * tt + 128], wd.t[:, f, :], f == 0, f == 3, ws, lwd, yb.free)
                    h = act(lambda e, ye=ye, yb=yb, tt=tt, x=x: e.activation(ye.t[:, tt, :], yb.t[:, 0:256], ACT.Copy,
                            scale=wJ[:, tt, x:x + 1]), hy, ye.free)
                    yb.free = [h]
                    sc_ = P.dma("gpsimd", "sc", 8, lambda e, ye=ye, tt=tt, x=x: e.indirect_dma_start(
                        out=dACC[:, :], out_offset=bass.IndirectOffsetOnAxis(ap=idxJ[:, tt, x:x + 1], axis=0),
                        in_=ye.t[:, tt, :], in_offset=None, compute_op=ALU.add), h, prev[tt] if prev else None)
                    scat.append(sc_)
                hhs.free, wd.free, ye.free = [hy], [hy], list(scat)
            P.barrier()
            M2.st.close()
            for s in banks:
                s.free = []

        if stop >= 3:
            M3 = Mem()
            W1 = M3.sb("W1", [128, E1, 2, H1])
            W2 = M3.sb("W2", [128, E1, 8, D])
            lw1 = [load(W1[:, x, :, :], A["W1"][x].rearrange("(k p) f -> p k f", p=128)) for x in range(E1)]
            lw2 = [load(W2[:, x, :, :], A["W2"][x].rearrange("(k p) f -> p k f", p=128)) for x in range(E1)]
            oh = M3.sb("oh", [128, 2, NT, E1])
            wts = M3.sb("wts", [128, 2, NT])
            posi = M3.sb("posi", [128, 2, NT], U32)
            te = M3.sb("te", [128, TILES], I32)
            b2sb = M3.sb("b2sb", [E1, D])
            gam = M3.sb("gam", [128, D])
            bet = M3.sb("bet", [128, D])
            ld_b2 = load(b2sb[:, :], A["b2"])
            ld_ga = load(gam[:, :], A["gamma"].rearrange("(a n) -> a n", a=1).to_broadcast([128, D]))
            ld_be = load(bet[:, :], A["beta"].rearrange("(a n) -> a n", a=1).to_broadcast([128, D]))
            dZ = dram("dZ", [N, D])
            M4 = Mem()
            small = M4.ring("sma", 4, [128, 2, 16])
            w1r = M4.sb("w1r", [128, 2, E1])
            bgr = M4.sb("bgr", [128, E1])
            ld_wr = load(w1r[:, :, :], A["L1g"].rearrange("(k p) e -> p k e", p=128))
            ld_bg = load(bgr[:, :], A["bg"].rearrange("(a n) -> a n", a=1).to_broadcast([128, E1]))
            zer = M4.sb("zer", [128, D])
            hz = pool(lambda e: e.memset(zer[:, :], 0.0))
            zs = [store(dXS[128 * i:128 * i + 128, :], zer[:, :], hz) for i in range(TILES)]
            rx = M4.ring("x2", 2, [128, 2, D])
            rct = M4.ring("c3T", 2, [128, 2, S])
            rq = M4.ring("Q3", 2, [128, 2, D])
            rs = M4.ring("S3", 2, [128, 3, 128])
            rz = M4.ring("z3", 2, [128, 2, D])
            rzT = M4.ring("zT", 2, [128, 2, S])
            SBK, QBK, TBK, LBK = (Ring(banks[2 * i:2 * i + 2]) for i in range(4))
            lgw = []
            for b in range(B):
                rows = slice(256 * b, 256 * b + 256)
                x, ct, q, s3, z, zT = (r.next() for r in (rx, rct, rq, rs, rz, rzT))
                lx = load(x.t[:, :, :], dACC[rows, :].rearrange("(c p) d -> p c d", p=128), x.free)
                lct = load(ct.t[:, :, :], A["ctxT"][:, rows].rearrange("(k p) t -> p k t", p=128), ct.free)
                sb_ = SBK.next()
                for k in range(2):
                    h = mm(sb_.t[:, 0:256], ct.t[:, k, 0:128], ct.t[:, k, :], k == 0, k == 1, lct, sb_.free)
                for k in range(2):
                    h = mm(sb_.t[:, 256:384], ct.t[:, k, 128:256], ct.t[:, k, 128:256], k == 0, k == 1)
                ct.free = [h]
                h1 = dve(lambda e, s3=s3, sb_=sb_: e.tensor_tensor(s3.t[:, 0, :], sb_.t[:, 0:128], tri[:, :], ALU.mult), h, s3.free)
                h2 = dve(lambda e, s3=s3, sb_=sb_: e.tensor_tensor(s3.t[:, 2, :], sb_.t[:, 256:384], tri[:, :], ALU.mult), h)
                h3 = dve(lambda e, s3=s3, sb_=sb_: e.tensor_copy(s3.t[:, 1, :], sb_.t[:, 128:256]), h)
                sb_.free = [h3]
                hq = [layernorm(x.t[:, c, :], q.t[:, c, :], lx, q.free, c) for c in range(2)]
                qb = QBK.next()
                mm(qb.t[:, 0:256], s3.t[:, 0, :], q.t[:, 0, :], True, True, hq, h3, qb.free)
                mm(qb.t[:, 256:512], s3.t[:, 1, :], q.t[:, 0, :], True, False)
                h = mm(qb.t[:, 256:512], s3.t[:, 2, :], q.t[:, 1, :], False, True)
                s3.free = [h]
                h4 = dve(lambda e, q=q, x=x: e.tensor_tensor(x.t[:, :, :], x.t[:, :, :], q.t[:, :, :], ALU.add), hq)
                h4 = dve(lambda e, x=x, qb=qb: e.tensor_tensor(x.t[:, :, :], x.t[:, :, :],
                         qb.t[:, :].rearrange("p (c d) -> p c d", c=2), ALU.add), h4, h)
                q.free, qb.free = [h4], [h4]
                s1 = store(dX3[rows, :].rearrange("(c p) d -> p c d", p=128), x.t[:, :, :], h4)
                hz_ = [layernorm(x.t[:, c, :], z.t[:, c, :], h4, z.free, c) for c in range(2)]
                x.free = [s1, hz_]
                s2 = store(dZ[rows, :].rearrange("(c p) d -> p c d", p=128), z.t[:, :, :], hz_)
                tb = TBK.next()
                tv = tb.t[:, :].rearrange("p (k t) -> p k t", k=2)
                for k in range(2):
                    for c in range(2):
                        h = tr(tv[:, k, 128 * c:128 * c + 128], z.t[:, c, 128 * k:128 * k + 128], ident[:, :], hz_, tb.free)
                z.free = [h, s2]
                h = act(lambda e, zT=zT, tv=tv: e.copy(zT.t[:, :, :], tv), h, zT.free)
                tb.free = [h]
                lb = LBK.next()
                for c in range(2):
                    for k in range(2):
                        hl = mm(lb.t[:, 8 * c:8 * c + 8], zT.t[:, k, 128 * c:128 * c + 128], w1r[:, k, :], k == 0, k == 1,
                                h, ld_wr, lb.free)
                zT.free = [hl]
                h = dve(lambda e, lb=lb, b=b: e.tensor_tensor(lg1[:, 2 * b:2 * b + 2, :],
                        lb.t[:, 0:16].rearrange("p (c x) -> p c x", c=2), bgr[:, :].unsqueeze(1).to_broadcast([128, 2, 8]), ALU.add),
                        hl, ld_bg)
                lb.free = [h]
                lgw.append(h)
            P.barrier()
            M4.st.close()
            for s in banks:
                s.free = []

            M5 = Mem()
            v8 = M5.sb("v8", [128, NT, 8])
            i8 = M5.sb("i8", [128, NT, 8], U32)
            i8f = M5.sb("i8f", [128, NT, 8])
            iox = M5.sb("iox", [128, 8], I32)
            ioxf = M5.sb("ioxf", [128, 8])
            msk = M5.sb("msk", [128, NT, 8])
            pfx = M5.sb("pfx", [128, NT, 8])
            tot = M5.sb("tot", [128, NT, 8])
            inc = M5.sb("inc", [128, NT, 8])
            cn = M5.sb("cn", [128, 6, 8])
            cni = M5.sb("cni", [128, 8], I32)
            sel = M5.sb("sel", [128, NT, 8])
            ti = M5.sb("ti", [128, TILES], I32)
            tf = M5.sb("tf", [128, TILES])
            cmpt = M5.sb("cmpt", [128, TILES, 8])
            d1 = M5.sb("d1", [128, NT])
            posf = M5.sb("posf", [128, 2, NT])
            hi_ = pool(lambda e: e.iota(iox[:, :], [[1, 8]], base=0, channel_multiplier=0))
            hi_ = dve(lambda e: e.tensor_copy(ioxf[:, :], iox[:, :]), hi_)
            for t in range(NT):
                h = dve(lambda e, t=t: e.max(v8[:, t, :], lg1[:, t, :]))
            for t in range(NT):
                h = dve(lambda e, t=t: e.max_index(i8[:, t, :], v8[:, t, :], lg1[:, t, :]), h)
            h = dve(lambda e: e.tensor_copy(i8f[:, :, :], i8[:, :, :]), h)
            for k in range(2):
                hoh = dve(lambda e, k=k: e.tensor_tensor(oh[:, k, :, :], i8f[:, :, k].unsqueeze(2).to_broadcast([128, NT, 8]),
                          ioxf[:, :].unsqueeze(1).to_broadcast([128, NT, 8]), ALU.is_equal), h, hi_)
            hm = dve(lambda e: e.tensor_tensor(msk[:, :, :], oh[:, 0, :, :], oh[:, 1, :, :], ALU.add), hoh)
            h = dve(lambda e: e.tensor_tensor(d1[:, :], v8[:, :, 1], v8[:, :, 0], ALU.subtract), h)
            h = act(lambda e: e.activation(d1[:, :], d1[:, :], ACT.Exp), h)
            h = dve(lambda e: e.tensor_scalar(wts[:, 0, :], d1[:, :], 1.0, None, ALU.add), h)
            h = dve(lambda e: e.reciprocal(wts[:, 0, :], wts[:, 0, :]), h)
            hwt = dve(lambda e: e.tensor_tensor(wts[:, 1, :], d1[:, :], wts[:, 0, :], ALU.mult), h)
            b0, b1_ = banks[0], banks[1]
            h0 = mm(b0.t[:, 0:256], stri[:, :], msk[:, :, :], True, True, hm)
            h1 = mm(b1_.t[:, 0:256], ones[:, 0:128], msk[:, :, :], True, True)
            hp = dve(lambda e: e.tensor_copy(pfx[:, :, :], b0.t[:, 0:256].rearrange("p (t x) -> p t x", x=8)), h0)
            ht = dve(lambda e: e.tensor_copy(tot[:, :, :], b1_.t[:, 0:256].rearrange("p (t x) -> p t x", x=8)), h1)
            for x in range(8):
                h = dve(lambda e, x=x: e.tensor_tensor_scan(inc[:, :, x], ones[:, 0:NT], tot[:, :, x], 0.0, ALU.mult, ALU.add), ht)
            h2 = dve(lambda e: e.tensor_scalar(cni[:, :], inc[:, NT - 1, :], 127.0, None, ALU.add), h)
            h2 = dve(lambda e: e.tensor_scalar(cni[:, :], cni[:, :], 7, 7, ALU.arith_shift_right, ALU.arith_shift_left), h2)
            h2 = dve(lambda e: e.tensor_copy(cn[:, 0, :], cni[:, :]), h2)
            h2 = dve(lambda e: e.tensor_tensor_scan(cn[:, 1, :], ones[:, 0:8], cn[:, 0, :], 0.0, ALU.mult, ALU.add), h2)
            h3 = dve(lambda e: e.tensor_tensor(cn[:, 2, :], cn[:, 1, :], cn[:, 0, :], ALU.subtract), h2)
            h = dve(lambda e: e.tensor_tensor(inc[:, :, :], inc[:, :, :], tot[:, :, :], ALU.subtract), h2)
            h = dve(lambda e: e.tensor_tensor(inc[:, :, :], inc[:, :, :], pfx[:, :, :], ALU.add), h, hp)
            h = dve(lambda e: e.tensor_tensor(inc[:, :, :], inc[:, :, :], cn[:, 2, :].unsqueeze(1).to_broadcast([128, NT, 8]), ALU.add), h, h3)
            hpos = h
            for k in range(2):
                h = dve(lambda e, k=k: e.tensor_tensor(sel[:, :, :], inc[:, :, :], oh[:, k, :, :], ALU.mult), h)
                h = dve(lambda e, k=k: e.tensor_reduce(posf[:, k, :], sel[:, :, :], AX.X, ALU.add), h)
            h = dve(lambda e: e.tensor_copy(posi[:, :, :], posf[:, :, :]), h)
            hposi = h
            hi_ = pool(lambda e: e.iota(ti[:, :], [[128, TILES]], base=0, channel_multiplier=0))
            h = dve(lambda e: e.tensor_copy(tf[:, :], ti[:, :]), hi_)
            h = dve(lambda e: e.tensor_tensor(cmpt[:, :, :], tf[:, :].unsqueeze(2).to_broadcast([128, TILES, 8]),
                    cn[:, 1, :].unsqueeze(1).to_broadcast([128, TILES, 8]), ALU.is_ge), h, h2)
            h = dve(lambda e: e.tensor_reduce(tf[:, :], cmpt[:, :, :], AX.X, ALU.add), h)
            h = dve(lambda e: e.tensor_scalar(te[:, :], tf[:, :], 7.0, None, ALU.min), h)
            hte = h
            P.barrier()
            M5.st.close()
            for s in banks:
                s.free = []

        if stop >= 4:
            M6 = Mem()
            rz = M6.ring("zl", 4, [128, D])
            sc_all = []
            for t in range(NT):
                z = rz.next()
                lz = load(z.t[:, :], dZ[128 * t:128 * t + 128, :], z.free)
                ss = [P.dma("gpsimd", "sx", 8, lambda e, z=z, k=k, t=t: e.indirect_dma_start(
                    out=dXS[:, :], out_offset=bass.IndirectOffsetOnAxis(ap=posi[:, k, t:t + 1], axis=0),
                    in_=z.t[:, :], in_offset=None), lz) for k in range(2)]
                z.free = ss
                sc_all += ss
            P.barrier()
            M6.st.close()

            M7 = Mem()
            rxs = M7.ring("xs", 3, [128, D])
            rxT = M7.ring("xsT", 2, [128, 2, 128])
            rhp = M7.ring("hp", 2, [128, H1])
            rhT = M7.ring("hT1", 2, [128, 8, 128])
            rb1 = M7.ring("b1c", 3, [128, 8])
            ry = M7.ring("y1", 2, [128, D])
            w1f = W1[:, :, :, :].rearrange("p x k f -> p (x k f)")
            w2f = W2[:, :, :, :].rearrange("p x k f -> p (x k f)")
            b1f = A["b1"].rearrange("x p c -> p (x c)") if False else A["b1"]
            Tb = Ring(banks[0:1])
            Hb = banks[1:3]
            HTb = banks[3:5]
            Yb = Ring(banks[5:7])
            for i in range(TILES):
                xs, xT, hp, hT, b1c, y = (r.next() for r in (rxs, rxT, rhp, rhT, rb1, ry))
                lx = load(xs.t[:, :], dXS[128 * i:128 * i + 128, :], xs.free)

                def ldb1(e, i=i, b1c=b1c):
                    r = e.value_load(te[0:1, i:i + 1], min_val=0, max_val=E1 - 1)
                    return e.dma_start(b1c.t[:, :], b1f[bass.ds(r, 1), :, :].rearrange("a p c -> (a p) c"))
                lb = P.dma("sync", "lb", 4, ldb1, b1c.free)
                tb = Tb.next()
                for k in range(2):
                    h = tr(tb.t[:, 128 * k:128 * k + 128], xs.t[:, 128 * k:128 * k + 128], ident[:, :], lx, tb.free)
                xs.free = [h]
                h = act(lambda e, xT=xT, tb=tb: e.copy(xT.t[:, :, :], tb.t[:, 0:256].rearrange("p (k t) -> p k t", k=2)), h, xT.free)
                tb.free = [h]
                reg = {}
                for half in range(2):
                    for k in range(2):
                        def f(e, half=half, k=k, i=i, xT=xT, reg=reg):
                            if not reg:
                                reg["r"] = e.value_load(te[0:1, i:i + 1], min_val=0, max_val=E1 - 1)
                            return e.matmul(Hb[half].t[:, :], xT.t[:, k, :],
                                            w1f[:, bass.ds(reg["r"] * 2048 + (1024 * k + 512 * half), 512)],
                                            start=(k == 0), stop=(k == 1))
                        hh = pe(f, h, lw1, Hb[half].free)
                    if half == 0:
                        h0 = act(lambda e, hp=hp: e.copy(hp.t[:, 0:512], Hb[0].t[:, :]), hh, hp.free)
                        Hb[0].free = [h0]
                    else:
                        h1 = dve(lambda e, hp=hp: e.tensor_copy(hp.t[:, 512:1024], Hb[1].t[:, :]), hh, hp.free)
                        Hb[1].free = [h1]
                xT.free = [hh]
                hg = []
                for half in range(2):
                    for c in range(4):
                        cc = 4 * half + c
                        h = tr(HTb[half].t[:, 128 * c:128 * c + 128], hp.t[:, 128 * cc:128 * cc + 128], ident[:, :],
                               (h0, h1)[half], HTb[half].free)
                    for c in range(4):
                        cc = 4 * half + c
                        ha = act(lambda e, hT=hT, half=half, c=c, cc=cc, b1c=b1c: e.activation(hT.t[:, cc, :],
                                 HTb[half].t[:, 128 * c:128 * c + 128], ACT.Gelu, bias=b1c.t[:, cc:cc + 1]), h, lb, hT.free)
                    HTb[half].free = [ha]
                hp.free, b1c.free = [h], [ha]
                yb = Yb.next()
                for c in range(8):
                    def f2(e, c=c, i=i, hT=hT, yb=yb, reg=reg):
                        return e.matmul(yb.t[:, 0:256], hT.t[:, c, :], w2f[:, bass.ds(reg["r"] * 2048 + 256 * c, 256)],
                                        start=(c == 0), stop=(c == 7))
                    h = pe(f2, ha, lw2, yb.free)
                hT.free = [h]
                h = dve(lambda e, y=y, yb=yb: e.tensor_copy(y.t[:, :], yb.t[:, 0:256]), h, y.free)
                yb.free = [h]
                y.free = [store(dYS[128 * i:128 * i + 128, :], y.t[:, :], h)]
            P.barrier()
            M7.st.close()
            for s in banks:
                s.free = []

            M8 = Mem()
            small = M8.ring("smc", 4, [128, 2, 16])
            ry = M8.ring("yg", 3, [128, 2, D])
            rz = M8.ring("zc", 3, [128, 2, D])
            rcb = M8.ring("cbn", 2, [128, 16])
            rct = M8.ring("cbT", 2, [8, 128])
            Tb = Ring(banks[0:2])
            Bb = Ring(banks[2:4])
            fin = []
            for t in range(NT):
                yg, z, cb, ct = (r.next() for r in (ry, rz, rcb, rct))
                gy = [P.dma("gpsimd", "gy", 8, lambda e, yg=yg, k=k, t=t: e.indirect_dma_start(
                    out=yg.t[:, k, :], out_offset=None, in_=dYS[:, :],
                    in_offset=bass.IndirectOffsetOnAxis(ap=posi[:, k, t:t + 1], axis=0)), yg.free) for k in range(2)]
                lz = [load(z.t[:, 0, :], dZ[128 * t:128 * t + 128, :], z.free),
                      load(z.t[:, 1, :], dX3[128 * t:128 * t + 128, :], z.free)]
                h = dve(lambda e, cb=cb, t=t: e.tensor_scalar(cb.t[:, 0:8], oh[:, 0, t, :], wts[:, 0, t:t + 1], None, ALU.mult), cb.free)
                h = dve(lambda e, cb=cb, t=t: e.scalar_tensor_tensor(out=cb.t[:, 8:16], in0=oh[:, 1, t, :], scalar=wts[:, 1, t:t + 1],
                        in1=cb.t[:, 0:8], op0=ALU.mult, op1=ALU.add), h)
                tb, bb = Tb.next(), Bb.next()
                h = tr(tb.t[0:8, 0:128], cb.t[:, 8:16], ident[:, :], h, tb.free)
                cb.free = [h]
                h = act(lambda e, ct=ct, tb=tb: e.copy(ct.t[:, :], tb.t[0:8, 0:128]), h, ct.free)
                tb.free = [h]
                hb = mm(bb.t[:, 0:256], ct.t[:, :], b2sb[:, :], True, True, h, ld_b2, bb.free)
                ct.free = [hb]
                h = dve(lambda e, yg=yg, t=t: e.tensor_scalar(yg.t[:, 0, :], yg.t[:, 0, :], wts[:, 0, t:t + 1], None, ALU.mult), gy)
                h = dve(lambda e, yg=yg, t=t: e.scalar_tensor_tensor(out=yg.t[:, 0, :], in0=yg.t[:, 1, :], scalar=wts[:, 1, t:t + 1],
                        in1=yg.t[:, 0, :], op0=ALU.mult, op1=ALU.add), h)
                h = dve(lambda e, yg=yg, bb=bb: e.tensor_tensor(yg.t[:, 0, :], yg.t[:, 0, :], bb.t[:, 0:256], ALU.add), h, hb)
                bb.free = [h]
                h = dve(lambda e, yg=yg, z=z: e.tensor_tensor(yg.t[:, 0, :], yg.t[:, 0, :], z.t[:, 0, :], ALU.add), h, lz)
                h = layernorm(yg.t[:, 0, :], z.t[:, 0, :], h, None, 0)
                yg.free = [h]
                h = dve(lambda e, z=z: e.tensor_tensor(z.t[:, 0, :], z.t[:, 0, :], gam[:, :], ALU.mult), h, ld_ga)
                h = dve(lambda e, z=z: e.tensor_tensor(z.t[:, 0, :], z.t[:, 0, :], bet[:, :], ALU.add), h, ld_be)
                h = dve(lambda e, z=z: e.tensor_tensor(z.t[:, 0, :], z.t[:, 0, :], z.t[:, 1, :], ALU.add), h)
                so = P.dma("sync", "out", 4, lambda e, z=z, t=t: e.dma_start(out[128 * t:128 * t + 128, :], z.t[:, 0, :]), h)
                z.free = [so]
            M8.st.close()
            M3.st.close()
        elif stop >= 3:
            M3.st.close()
        P.barrier()
        block = ctx.enter_context(nc.Block())
        P.emit(block)


STOP = 99


def kernel(**inputs):
    import concourse.bacc as _bacc
    from concourse.bass_utils import run_bass_kernel_spmd as _run

    i = {k: np.asarray(v) for k, v in inputs.items()}
    t = lambda a: np.ascontiguousarray(np.swapaxes(a, -1, -2))
    arrays = {
        "x": i["x"].reshape(N, D),
        "ctx": i["ctx_1024"].reshape(N, D),
        "ctxT": t(i["ctx_1024"].reshape(N, D)),
        "igate_w": t(i["L0_xattn_igate_w"]).reshape(6, 128, 8),
        "fgate_w": t(i["L0_xattn_fgate_w"]).reshape(6, 128, 8),
        "igate_b": i["L0_xattn_igate_b"],
        "fgate_b": i["L0_xattn_fgate_b"],
        "ln_scale": i["L0_xattn_ln_scale"],
        "gate_w": t(i["L0_ffn_gate_w"]),
        "Wg": t(i["L0_ffn_Wg"]), "Wu": t(i["L0_ffn_Wu"]), "Wd": t(i["L0_ffn_Wd"]),
        "Ws_g": t(i["L0_ffn_Ws_g"]), "Ws_u": t(i["L0_ffn_Ws_u"]), "Ws_d": t(i["L0_ffn_Ws_d"]),
        "L1g": i["L1_ffn_Wg"], "bg": i["L1_ffn_bg"],
        "W1": i["L1_ffn_W1"], "b1": t(i["L1_ffn_b1"].reshape(E1, 8, 128)),
        "W2": i["L1_ffn_W2"], "b2": i["L1_ffn_b2"],
        "gamma": i["L1_ffn_gamma"], "beta": i["L1_ffn_beta"],
    }
    nc = _bacc.Bacc("TRN2", target_bir_lowering=False, num_devices=1)
    maps, aps = {}, {}
    for name, a in arrays.items():
        a = np.ascontiguousarray(a)
        maps["in_" + name] = a
        aps[name] = nc.dram_tensor("in_" + name, a.shape, mybir.dt.from_np(a.dtype), kind="ExternalInput").ap()
    out = nc.dram_tensor("out_0", [N, D], FP, kind="ExternalOutput").ap()
    build(nc, aps, out, STOP)
    r = _run(nc, [maps], core_ids=[0])
    return r.results[0]["out_0"].reshape(B, S, D)
```

```python
import numpy as np
import concourse.bass as bass
from concourse import mybir
from contextlib import ExitStack

FP = mybir.dt.float32
BF = mybir.dt.bfloat16
U32 = mybir.dt.uint32
I32 = mybir.dt.int32
FR = mybir.dt.float32r
ALU = mybir.AluOpType
ACT = mybir.ActivationFunctionType
AX = mybir.AxisListType

B, S, D, NH = 16, 256, 256, 8
N = B * S
E0, F0, CAP = 16, 512, 32
E1, H1 = 8, 1024
NT = N // 128
TS = 256
TILES = (2 * N + E1 * (TS - 1)) // TS
EPS = 1e-5
ROW = D + 2
REG = N + TS
R32 = float(np.sqrt(32.0))


class Handle:
    __slots__ = ("eng", "seq", "sem", "val", "marked")

    def __init__(self, eng, sem=None, val=0):
        self.eng, self.sem, self.val, self.marked = eng, sem, val, False


def flat(x):
    if x is None:
        return
    if isinstance(x, Handle):
        yield x
    else:
        for y in x:
            yield from flat(y)


class Program:

    def __init__(self, nc, ctx):
        self.nc, self.ctx = nc, ctx
        self.q = {e: [] for e in ("tensor", "vector", "scalar", "gpsimd", "sync")}
        self.sems = {e: ctx.enter_context(nc.semaphore(f"s_{e}")) for e in self.q}
        self.lanes = {}

    def op(self, eng, fn, *after):
        h = Handle(eng)
        ws = list(flat(after))
        for w in ws:
            w.marked = True
        self.q[eng].append((fn, ws, h))
        return h

    def lane(self, name, n):
        if name not in self.lanes:
            self.lanes[name] = [[self.ctx.enter_context(self.nc.semaphore(f"d_{name}{i}")), 0, None]
                                for i in range(n)] + [0]
        return self.lanes[name]

    def dma(self, eng, name, n, fn, *after):
        l = self.lane(name, n)
        k = l[-1]
        l[-1] = (k + 1) % n
        sem, cnt, last = l[k]
        h = Handle(eng, sem, cnt + 16)
        l[k][1] += 16
        l[k][2] = h
        h.marked = True
        ws = list(flat(after)) + ([last] if last else [])
        for w in ws:
            w.marked = True
        self.q[eng].append((fn, ws, h))
        return h

    def barrier(self):
        hs = []
        for e in self.q:
            own = [h for _, _, h in self.q[e] if h is not None and h.sem is None]
            hs += own[-1:]
        for l in self.lanes.values():
            hs += [x[2] for x in l[:-1] if x[2]]
        for h in hs:
            h.marked = True
        for e in self.q:
            self.q[e].append((None, hs, None))

    def emit(self, block):
        for e in self.q:
            n = 0
            for fn, ws, h in self.q[e]:
                if h is not None and h.sem is None and h.marked:
                    n += 1
                    h.val = n
                    h.sem = self.sems[e]

        def replay(eng, e):
            seen = {}
            for fn, ws, h in self.q[e]:
                need = {}
                for w in ws:
                    need[w.sem] = max(need.get(w.sem, 0), w.val)
                for s, v in need.items():
                    if seen.get(s, 0) < v:
                        eng.wait_ge(s, v)
                        seen[s] = v
                if fn is None:
                    continue
                ins = fn(eng)
                if h.marked:
                    ins.then_inc(h.sem, 1 if h.sem is self.sems[e] else 16)

        for e in self.q:
            register = {"tensor": block.tensor, "vector": block.vector, "scalar": block.scalar,
                             "gpsimd": block.gpsimd, "sync": block.sync}[e]
            register(lambda eng, e=e: replay(eng, e))


class Slot:

    def __init__(self, t):
        self.t, self._free, self.busy = t, [], False

    @property
    def free(self):
        return self._free

    @free.setter
    def free(self, x):
        self._free, self.busy = x, False

    def take(self):
        assert not self.busy, "the buffer's last users aren't queued yet"
        self.busy = True
        return self


class Ring:
    def __init__(self, slots):
        self.slots, self.i = slots, -1

    def next(self):
        self.i = (self.i + 1) % len(self.slots)
        return self.slots[self.i].take()


def pipeline(makers):
    run = []
    for make in list(makers) + [None] * 99:
        if make:
            run.append(make())
        run = [g for g in run if next(g, run) is not run]


def zip_(*gens):
    live = list(gens)
    while live:
        live = [g for g in live if next(g, live) is not live]
        if live:
            yield


def build(nc, A, out, stop=99):
    ctx = ExitStack()
    with ctx:
        P = Program(nc, ctx)

        def sem(name):
            return ctx.enter_context(nc.semaphore(name))

        def dram(name, shape, dt=FP):
            return nc.dram_tensor(name, shape, dt, kind="Internal").ap()

        dH = dram("dH", [N, D])
        dACC = dram("dACC", [N, D])
        dX3 = dram("dX3", [N, D])
        dXS = dram("dXS", [E1 * REG + TS, ROW])
        dOUT = dram("dOUT", [N + TS, D])

        banks = [Slot(ctx.enter_context(nc.psum_tensor(f"pb{i}", [128, 512], FP))) for i in range(8)]

        class Mem:
            made = 0

            def __init__(self):
                self.st = ExitStack()

            def sb(self, name, shape, dt=FP):
                Mem.made += 1
                return self.st.enter_context(nc.sbuf_tensor(f"{name}_{Mem.made}", shape, dt))

            def ring(self, name, n, shape, dt=FP):
                return Ring([Slot(self.sb(f"{name}{i}", shape, dt)) for i in range(n)])

        G = Mem()
        ctx.enter_context(G.st)

        pe = lambda fn, *a: P.op("tensor", fn, *a)
        dve = lambda fn, *a: P.op("vector", fn, *a)
        act = lambda fn, *a: P.op("scalar", fn, *a)
        pool = lambda fn, *a: P.op("gpsimd", fn, *a)

        def load(out_, in_, *a, n=8):
            return P.dma("sync", "ld", n, lambda e: e.dma_start(out_, in_), *a)

        def store(out_, in_, *a, n=4):
            return P.dma("sync", "st", n, lambda e: e.dma_start(out_, in_), *a)

        def mm(o, l, r, s, t, *a):
            return pe(lambda e: e.matmul(o, l, r, start=s, stop=t), *a)

        def tr(o, i, idn, *a):
            return pe(lambda e: e.transpose(o, i, idn), *a)

        ident = G.sb("ident", [128, 128])
        ones = G.sb("ones", [128, 256])
        hm8 = G.sb("hm8", [128, 8])
        hm4 = G.sb("hm4", [128, 4])
        tri = G.sb("tri", [128, 128])
        stri = G.sb("stri", [128, 128])
        idxJ = G.sb("idxJ", [128, 4, E0], U32)
        wJ = G.sb("wJ", [128, 4, E0])

        c_id0 = pool(lambda e: e.memset(ident[:, :], 0.0))
        c_ones = pool(lambda e: e.memset(ones[:, :], 1.0))
        c_id = pool(lambda e: e.affine_select(out=ident[:, :], in_=ident[:, :], compare_op=ALU.not_equal, fill=1.0,
                                              base=0, pattern=[[-1, 128]], channel_multiplier=1), c_id0)
        c = None
        for j in range(4):
            c = dve(lambda e, j=j: e.tensor_copy(hm8[32 * j:32 * j + 32, :], ident[0:32, 0:8]), c_id)
        c_h8 = c
        c_a = pool(lambda e: e.affine_select(out=hm4[:, :], in_=ones[:, 0:4], compare_op=ALU.is_ge, fill=0.0,
                                             base=0, pattern=[[-32, 4]], channel_multiplier=1), c_ones)
        c_h4 = pool(lambda e: e.affine_select(out=hm4[:, :], in_=hm4[:, :], compare_op=ALU.is_ge, fill=0.0,
                                              base=31, pattern=[[32, 4]], channel_multiplier=-1), c_a)
        c_tri = pool(lambda e: e.affine_select(out=tri[:, :], in_=ones[:, 0:128], compare_op=ALU.is_ge, fill=0.0,
                                               base=0, pattern=[[1, 128]], channel_multiplier=-1), c_ones)
        c_stri = pool(lambda e: e.affine_select(out=stri[:, :], in_=ones[:, 0:128], compare_op=ALU.is_gt, fill=0.0,
                                                base=0, pattern=[[1, 128]], channel_multiplier=-1), c_ones)
        mhalf = G.sb("mhalf", [128, 1])
        c_mh = pool(lambda e: e.memset(mhalf[:, :], -0.5))
        identb = G.sb("identb", [128, 128], BF)
        maskb = G.sb("maskb", [128, 128], BF)
        c_mk = [dve(lambda e: e.tensor_copy(identb[:, :], ident[:, :]), c_id),
                dve(lambda e: e.tensor_scalar(maskb[:, :], tri[:, :], 1.0, 1e30, ALU.subtract, ALU.mult), c_tri)]
        consts = [c_id, c_ones, c_h8, c_h4, c_tri, c_stri]

        M1 = Mem()
        gw0 = M1.sb("gw0", [128, 2, 6, 32])
        gw = M1.sb("gw", [128, 2, 4, 32])
        gb = M1.sb("gb", [128, 2])
        lns = M1.sb("lns", [128, D])
        rw = M1.sb("rw", [128, 2, E0])
        wsg = M1.sb("wsg", [128, 2, F0])
        wsu = M1.sb("wsu", [128, 2, F0])
        wsd = M1.sb("wsd", [128, 4, D])
        z1 = pool(lambda e: e.memset(gw0[:, :, :, :], 0.0))
        z2 = pool(lambda e: e.memset(gb[:, :], 0.0))
        ld = []
        for t, w in enumerate((A["igate_w"], A["fgate_w"])):
            for k in range(6):
                ld.append(load(gw0[:, t, k, 0:8], w[k], z1))
        for t, w in enumerate((A["igate_b"], A["fgate_b"])):
            for j in range(4):
                ld.append(load(gb[32 * j:32 * j + 8, t:t + 1], w.rearrange("(p a) -> p a", a=1), z2))
        ld_ln = load(lns[:, :], A["ln_scale"].rearrange("(a n) -> a n", a=1).to_broadcast([128, D]))
        ld_rw = load(rw[:, :, :], A["gate_w"].rearrange("(k p) e -> p k e", p=128))
        ld_ws = [load(wsg[:, :, :], A["Ws_g"].rearrange("(k p) f -> p k f", p=128)),
                 load(wsu[:, :, :], A["Ws_u"].rearrange("(k p) f -> p k f", p=128)),
                 load(wsd[:, :, :], A["Ws_d"].rearrange("(k p) f -> p k f", p=128))]
        g1 = dve(lambda e: e.tensor_copy(gw[:, :, 0:2, :], gw0[:, :, 0:2, :]), ld)
        g2 = dve(lambda e: e.tensor_tensor(gw[:, :, 2:4, :], gw0[:, :, 2:4, :], gw0[:, :, 4:6, :], ALU.add), ld)
        ld_gw = [g1, g2]

        rX = M1.ring("xb", 4, [128, 2, D])
        rC = M1.ring("cb", 4, [128, 2, D])
        rCT = M1.ring("cT", 4, [128, 2, S])
        rQ = M1.ring("q", 2, [128, 2, D])
        rQT = M1.ring("qT", 4, [128, 2, S])
        small = M1.ring("sm", 4, [128, 2, 16])
        rHT = M1.ring("hT", 2, [128, 2, 512])
        rX1 = M1.ring("x1", 4, [128, 2, D])

        def layernorm2(src, dst, w, after, dst_free):
            sm = small.next()
            s = sm.t
            h = [dve(lambda e, c=c: e.bn_stats(s[:, c, 0:6], src[:, c, 0:w]), after, sm.free) for c in range(2)]
            h = [dve(lambda e, c=c: e.bn_aggr(s[:, c, 6:8], s[:, c, 0:6]), h) for c in range(2)]
            h = dve(lambda e: e.tensor_scalar(s[:, :, 9:10], s[:, :, 7:8], EPS, None, ALU.add), h)
            h = pool(lambda e: e.tensor_tensor(s[:, :, 8:9], s[:, :, 9:10],
                     mhalf[:, :].unsqueeze(1).to_broadcast([128, 2, 1]), ALU.pow), h, c_mh)
            yield
            h = [dve(lambda e, c=c: e.tensor_scalar(dst[:, c, 0:w], src[:, c, 0:w], s[:, c, 6:7], s[:, c, 8:9],
                     ALU.subtract, ALU.mult), h, dst_free) for c in range(2)]
            sm.free = [h]
            return h

        T, GB, SB0, SB1, BB0, BB1, O1, O2 = banks

        def layernorm(src, dst, after, dst_free, c):
            sm = small.next()
            s = sm.t
            h = dve(lambda e: e.bn_stats(s[:, c, 0:6], src), after, sm.free)
            h = dve(lambda e: e.bn_aggr(s[:, c, 6:8], s[:, c, 0:6]), h)
            h = dve(lambda e: e.tensor_scalar(s[:, c, 9:10], s[:, c, 7:8], EPS, None, ALU.add), h)
            h = pool(lambda e: e.tensor_tensor(s[:, c, 8:9], s[:, c, 9:10], mhalf[:, :], ALU.pow), h, c_mh)
            h = dve(lambda e: e.tensor_scalar(dst, src, s[:, c, 6:7], s[:, c, 8:9], ALU.subtract, ALU.mult),
                    h, dst_free)
            sm.free = [h]
            return h

        row = {n: M1.sb(n, [128, S]) for n in ("igr", "zr", "er", "lr", "csr", "ar", "Mr", "nMr", "tr", "eer")}
        wfr = M1.sb("wfr", [128, S])
        Mx = M1.sb("Mx", [128, 8, S])
        cols = M1.sb("cols", [128, 6, 128])
        colrel = []
        rowrel = []
        mxrel = []
        rqx = M1.ring("qx", 2, [128, 2, 4, 128])
        rD = M1.ring("Dm", 2, [128, 8, 128])
        rCm = M1.ring("Cm", 2, [128, 8, 128])
        rV = M1.ring("V1", 2, [128, 2, 8, 33])
        rW = M1.ring("wV", 2, [128, 8, 33])
        rKV = M1.ring("KV", 2, [128, 2, 4, 33])
        rO = M1.ring("Oo", 2, [128, 8, 33])
        rn = M1.ring("nn", 2, [128, 3, 8])
        rh = M1.ring("hh1", 2, [128, D])
        rH = M1.ring("Ht", 2, [128, D])
        lgt = M1.sb("lgt", [128, 2, 8, E0])
        lgrel = [[]]
        rg = M1.ring("gs", 2, [128, 512])
        rhh = M1.ring("hhs", 1, [128, 4, 512])
        rys = M1.ring("ys", 2, [128, D])

        for sl in rV.slots:
            sl.free = [pool(lambda e, t=sl.t: e.memset(t[:, :, :, 32:33], 1.0))]

        LG = []
        for g in range(4):
            info = []
            gates = []
            for j in range(4):
                b = 4 * g + j
                x, cb, cT = rX.next(), rC.next(), rCT.next()
                rows = slice(256 * b, 256 * b + 256)
                lx = load(x.t[:, :, :], A["x"][rows, :].rearrange("(c p) d -> p c d", p=128), x.free)
                lc = load(cb.t[:, :, :], A["ctx"][rows, :].rearrange("(c p) d -> p c d", p=128), cb.free)
                lct = load(cT.t[:, :, :], A["ctxT"][:, rows].rearrange("(k p) t -> p k t", p=128), cT.free)
                q, qT = rQ.next(), rQT.next()
                hq = [layernorm(x.t[:, c, :], q.t[:, c, :], lx, q.free, c) for c in range(2)]
                tv = T.t[:, :].rearrange("p (k t) -> p k t", k=2)
                for k in range(2):
                    for c in range(2):
                        h = tr(tv[:, k, 128 * c:128 * c + 128], q.t[:, c, 128 * k:128 * k + 128], ident[:, :],
                               hq, consts, T.free)
                q.free = [h]
                hqT = act(lambda e, o=qT.t, i=tv: e.copy(o[:, :, :], i), h, qT.free)
                T.free = [hqT]
                for t in range(2):
                    for k in range(4):
                        rhs = qT.t[:, k, :] if k < 2 else cT.t[:, k - 2, :]
                        h = mm(GB.t[32 * j:32 * j + 32, 256 * t:256 * t + 256], gw[:, t, k, :], rhs,
                               k == 0, k == 3, hqT, lct, ld_gw, GB.free)
                gates.append(h)
                info.append((b, x, cb, cT, qT, lc, lct, hqT))
            r = row
            gt = GB.t
            h1 = dve(lambda e: e.tensor_scalar(r["igr"][:, :], gt[:, 0:256], gb[:, 0:1], None, ALU.add), gates, ld, rowrel)
            h2 = dve(lambda e: e.tensor_scalar(r["zr"][:, :], gt[:, 256:512], gb[:, 1:2], None, ALU.add), gates, ld, rowrel)
            GB.free = [h1, h2]
            h3 = dve(lambda e: e.scalar_tensor_tensor(out=r["er"][:, :], in0=r["zr"][:, :], scalar=-1.0, in1=r["zr"][:, :],
                                                      op0=ALU.mult, op1=ALU.min), h2)
            h4 = act(lambda e: e.activation(r["lr"][:, :], r["er"][:, :], ACT.Exp), h3)
            h4 = act(lambda e: e.activation(r["lr"][:, :], r["lr"][:, :], ACT.Ln, bias=ones[:, 0:1]), h4, c_ones)
            h5 = dve(lambda e: e.scalar_tensor_tensor(out=r["zr"][:, :], in0=r["zr"][:, :], scalar=0.0, in1=r["lr"][:, :],
                                                      op0=ALU.min, op1=ALU.subtract), h4)
            h6 = dve(lambda e: e.tensor_tensor_scan(r["csr"][:, :], ones[:, 0:256], r["zr"][:, :], 0.0, ALU.mult, ALU.add), h5)
            h7 = dve(lambda e: e.tensor_tensor(r["ar"][:, :], r["igr"][:, :], r["csr"][:, :], ALU.subtract), h6, h1)
            h8 = dve(lambda e: e.tensor_tensor_scan(r["Mr"][:, :], r["ar"][:, :], r["ar"][:, :], -3.0e38, ALU.max, ALU.max), h7)
            h9 = dve(lambda e: e.tensor_scalar(r["nMr"][:, :], r["Mr"][:, :], -1.0, None, ALU.mult), h8)
            h10 = dve(lambda e: e.tensor_tensor(r["tr"][:, :], r["csr"][:, :], r["Mr"][:, :], ALU.add), h8)
            h11 = act(lambda e: e.activation(r["eer"][:, :], r["tr"][:, :], ACT.Exp, scale=-1.0), h10)
            h12 = act(lambda e: e.activation(wfr[:, 0:128], r["ar"][:, 0:128], ACT.Exp, bias=r["nMr"][:, 127:128]), h9, rowrel)
            h13 = act(lambda e: e.activation(wfr[:, 128:256], r["nMr"][:, 128:256], ACT.Exp, bias=r["Mr"][:, 127:128]), h9)
            hmx = dve(lambda e: e.tensor_tensor(Mx[:, :, :], r["nMr"][:, :].unsqueeze(1).to_broadcast([128, 8, S]),
                                                hm8[:, :].unsqueeze(2).to_broadcast([128, 8, S]), ALU.mult), h9, c_h8, mxrel)
            srcs = [r["ar"][:, 0:128], r["ar"][:, 128:256], r["eer"][:, 0:128], r["eer"][:, 128:256],
                    wfr[:, 0:128], wfr[:, 128:256]]
            newcol = []
            ht = []
            for i0 in (0, 3):
                for i in range(i0, i0 + 3):
                    h = tr(T.t[:, 128 * (i - i0):128 * (i - i0) + 128], srcs[i], ident[:, :], h7, h11, h12, h13, T.free)
                ht.append(h)
                h = act(lambda e, i0=i0: e.copy(cols[:, i0:i0 + 3, :], T.t[:, 0:384].rearrange("p (i t) -> p i t", i=3)),
                        h, colrel)
                T.free = [h]
                newcol.append(h)
            rowrel = [ht[-1], hmx]
            colrel, mxrel = [], []

            for j, (b, x, cb, cT, qT, lc, lct, hqT) in enumerate(info):
                jc = slice(32 * j, 32 * j + 8)
                V = rV.next()
                hV = act(lambda e, V=V, cb=cb: e.copy(V.t[:, :, :, 0:32], cb.t[:, :, :].rearrange("p c (h d) -> p c h d", h=8)), lc, V.free)
                wV = rW.next()
                hW = dve(lambda e, V=V, wV=wV, jc=jc: e.tensor_tensor(wV.t[:, :, :], V.t[:, 0, :, :],
                         cols[:, 4, jc].unsqueeze(2).to_broadcast([128, 8, 33]), ALU.mult), hV, newcol, wV.free)
                x1 = rX1.next()
                if b % 2 == 0:
                    hT = rHT.next()
                    hTw, x1w = [], []
                KV = rKV.next()
                for c in range(2):
                    cs_ = slice(128 * c, 128 * c + 128)
                    qx = rqx.next()
                    for k in range(2):
                        h = dve(lambda e, qx=qx, k=k, qT=qT, cs_=cs_: e.tensor_tensor(qx.t[:, k, :, :],
                                qT.t[:, k, cs_].unsqueeze(1).to_broadcast([128, 4, 128]),
                                hm4[:, :].unsqueeze(2).to_broadcast([128, 4, 128]), ALU.mult), hqT, c_h4, qx.free)
                    hqx = h
                    for k, bk in enumerate((SB0, SB1)):
                        hs = mm(bk.t[:, :], cT.t[:, k, cs_], qx.t[:, k, :, :], True, True, hqx, lct, bk.free)
                    qx.free = [hs]
                    hbs = []
                    for k, bk in enumerate((BB0, BB1)):
                        mm(bk.t[:, :], identb[:, :], maskb[:, :].unsqueeze(1).to_broadcast([128, 4, 128]), True, False,
                           c_mk, bk.free)
                        hb = mm(bk.t[:, :], ones[32 * j:32 * j + 32, 0:128], Mx[32 * j:32 * j + 32, 4 * k:4 * k + 4, cs_],
                                False, True, hmx)
                        hbs.append(hb)
                    mxrel.append(hb)
                    Dm = rD.next()
                    he = []
                    for hd in range(8):
                        bk = (BB0, BB1)[hd // 4]
                        h = act(lambda e, Dm=Dm, bk=bk, hd=hd, c=c, j=j: e.activation(Dm.t[:, hd, :],
                                bk.t[:, 128 * (hd % 4):128 * (hd % 4) + 128], ACT.Exp,
                                bias=cols[:, c, 32 * j + hd:32 * j + hd + 1]), hbs[hd // 4], newcol, Dm.free)
                        bk.free = [h]
                    hD = h
                    Cm = rCm.next()
                    for k, bk in enumerate((SB0, SB1)):
                        h = dve(lambda e, Cm=Cm, Dm=Dm, k=k, bk=bk: e.tensor_tensor(Cm.t[:, 4 * k:4 * k + 4, :],
                                bk.t[:, :].rearrange("p (h s) -> p h s", h=4), Dm.t[:, 4 * k:4 * k + 4, :], ALU.mult),
                                hD, hs, Cm.free)
                        bk.free = [h]
                    Dm.free = [h]
                    hC = h
                    for hd in range(8):
                        h = mm(O1.t[:, 33 * hd:33 * hd + 33], Cm.t[:, hd, :], V.t[:, c, hd, :], True, True, hC, hV, O1.free)
                    Cm.free = [h]
                    hO1 = h
                    O = rO.next()
                    if c == 0:
                        for k in range(2):
                            h = mm(O2.t[:, 132 * k:132 * k + 132], cb.t[:, 0, 128 * k:128 * k + 128],
                                   wV.t[:, 4 * k:4 * k + 4, :], True, True, hW, lc, O2.free)
                        wV.free = [h]
                        hKV = dve(lambda e, KV=KV: e.tensor_tensor(KV.t[:, :, :, :],
                                  O2.t[:, 0:264].rearrange("p (k h d) -> p k h d", k=2, h=4),
                                  hm4[:, :].unsqueeze(1).unsqueeze(3).to_broadcast([128, 2, 4, 33]), ALU.mult), h, KV.free)
                        O2.free = [hKV]
                        hO = dve(lambda e, O=O: e.tensor_copy(O.t[:, :, :], O1.t[:, 0:264].rearrange("p (h d) -> p h d", h=8)),
                                 hO1, O.free)
                        O1.free = [hO]
                    else:
                        for k in range(2):
                            h = mm(O2.t[:, 132 * k:132 * k + 132], qT.t[:, k, cs_], KV.t[:, k, :, :], True, True,
                                   hKV, O2.free)
                        KV.free = [h]
                        hO = dve(lambda e, O=O, jc=jc: e.tensor_tensor(O.t[:, :, :],
                                 O2.t[:, 0:264].rearrange("p (h d) -> p h d", h=8),
                                 cols[:, 5, jc].unsqueeze(2).to_broadcast([128, 8, 33]), ALU.mult), h, O.free, newcol)
                        O2.free = [hO]
                        hO = dve(lambda e, O=O: e.tensor_tensor(O.t[:, :, :], O.t[:, :, :],
                                 O1.t[:, 0:264].rearrange("p (h d) -> p h d", h=8), ALU.add), hO, hO1)
                        O1.free = [hO]
                        V.free = [hO1]
                    nn = rn.next()
                    h = dve(lambda e, nn=nn, c=c, jc=jc: e.tensor_scalar(nn.t[:, 0, :], cols[:, 2 + c, jc], R32, None, ALU.mult),
                            newcol, nn.free)
                    h = dve(lambda e, nn=nn, O=O: e.scalar_tensor_tensor(out=nn.t[:, 1, :], in0=O.t[:, :, 32], scalar=-1.0,
                            in1=O.t[:, :, 32], op0=ALU.mult, op1=ALU.max), hO, h)
                    h = dve(lambda e, nn=nn: e.tensor_tensor(nn.t[:, 1, :], nn.t[:, 1, :], nn.t[:, 0, :], ALU.max), h)
                    h = dve(lambda e, nn=nn: e.tensor_scalar(nn.t[:, 1, :], nn.t[:, 1, :], R32 * 1e-6, None, ALU.add), h)
                    h = dve(lambda e, nn=nn: e.reciprocal(nn.t[:, 2, :], nn.t[:, 1, :]), h)
                    hh = rh.next()
                    h = dve(lambda e, nn=nn, O=O, hh=hh: e.tensor_tensor(hh.t[:, :].rearrange("p (h d) -> p h d", h=8),
                            O.t[:, :, 0:32], nn.t[:, 2, :].unsqueeze(2).to_broadcast([128, 8, 32]), ALU.mult), h, hh.free)
                    nn.free, O.free = [h], [h]
                    h = layernorm(hh.t[:, :], hh.t[:, :], h, None, c)
                    h = dve(lambda e, hh=hh: e.tensor_tensor(hh.t[:, :], hh.t[:, :], lns[:, :], ALU.mult), h, ld_ln)
                    hx1 = dve(lambda e, hh=hh, x1=x1, x=x, c=c: e.tensor_tensor(x1.t[:, c, :], hh.t[:, :], x.t[:, c, :], ALU.add),
                              h, x1.free)
                    hh.free = [hx1]
                    Ht = rH.next()
                    hH = layernorm(x1.t[:, c, :], Ht.t[:, :], hx1, Ht.free, c)
                    sH = store(dH[256 * b + 128 * c:256 * b + 128 * c + 128, :], Ht.t[:, :], hH)
                    for k in range(2):
                        h = tr(T.t[:, 128 * k:128 * k + 128], Ht.t[:, 128 * k:128 * k + 128], ident[:, :], hH, T.free)
                    Ht.free = [h, sH]
                    t0 = 256 * (b % 2) + 128 * c
                    hhT = act(lambda e, hT=hT, t0=t0: e.copy(hT.t[:, :, t0:t0 + 128], T.t[:, 0:256].rearrange("p (k t) -> p k t", k=2)),
                              h, hT.free)
                    T.free = [hhT]
                    hTw.append(hhT)
                    x1w.append(hx1)
                    for k in range(2):
                        h = mm(T.t[:, 0:E0], hT.t[:, k, t0:t0 + 128], rw[:, k, :], k == 0, k == 1, hhT, ld_rw, T.free)
                    h = act(lambda e, b=b, c=c: e.copy(lgt[:, c, b % 8, :], T.t[:, 0:E0]), h, lgrel[0])
                    T.free = [h]
                    LG.append(h)
                    x1.own = (b, c)
                colrel.append(hx1)
                x.free, cb.free, cT.free, qT.free = [hx1], [hO1, hKV], [hs], [hs, hO]
                if b % 2 == 1:
                    hhs = rhh.next()
                    ws = []
                    for f in range(4):
                        fs = slice(128 * f, 128 * f + 128)
                        bg, bu = ((SB0, BB0), (SB1, BB1))[f % 2]
                        for k in range(2):
                            hg = mm(bg.t[:, :], wsg[:, k, fs], hT.t[:, k, :], k == 0, k == 1, hTw, ld_ws, bg.free)
                        for k in range(2):
                            hu = mm(bu.t[:, :], wsu[:, k, fs], hT.t[:, k, :], k == 0, k == 1, bu.free)
                        gs = rg.next()
                        h = act(lambda e, gs=gs, bg=bg: e.activation(gs.t[:, :], bg.t[:, :], ACT.Gelu), hg, gs.free)
                        bg.free = [h]
                        h = dve(lambda e, gs=gs, bu=bu, f=f, hhs=hhs: e.tensor_tensor(hhs.t[:, f, :], gs.t[:, :], bu.t[:, :], ALU.mult),
                                h, hu, hhs.free)
                        gs.free, bu.free = [h], [h]
                        ws.append(h)
                    hT.free = [hu]
                    for tt in range(4):
                        ybk = (O1, O2)[tt % 2]
                        for f in range(4):
                            h = mm(ybk.t[:, 0:256], hhs.t[:, f, 128 * tt:128 * tt + 128], wsd[:, f, :], f == 0, f == 3, ws, ybk.free)
                        hy = h
                        ys = rys.next()
                        xs = prev_x1 if tt < 2 else x1
                        h = dve(lambda e, ys=ys, ybk=ybk, xs=xs, tt=tt: e.tensor_tensor(ys.t[:, :], ybk.t[:, 0:256], xs.t[:, tt % 2, :], ALU.add),
                                hy, ys.free, x1w)
                        ybk.free = [h]
                        xs.free = [h]
                        r0 = 256 * (b - 1) + 128 * tt
                        ys.free = [store(dACC[r0:r0 + 128, :], ys.t[:, :], h)]
                    hhs.free = [hy]
                prev_x1 = x1
            if g % 2 == 1:
                G8 = g // 2
                if g == 1:
                    sm1 = M1.sb("sm1", [128, 16])
                    sc = M1.sb("sc", [128, S])
                    sc2 = M1.sb("sc2", [128, S])
                    vals = M1.sb("vals", [128, CAP])
                    ix = M1.sb("ix", [128, CAP], U32)
                    ixf = M1.sb("ixf", [128, CAP])
                    bof = M1.sb("bof", [128, 1])
                    bofi = M1.sb("bofi", [128, 1], I32)
                    rt = []
                l3 = lgt[:, :, :, :].rearrange("p c b e -> p (c b) e")
                h = dve(lambda e: e.tensor_reduce(sm1[:, :], l3, AX.X, ALU.max), LG, rt)
                h = dve(lambda e: e.tensor_tensor(l3, l3, sm1[:, :].unsqueeze(2).to_broadcast([128, 16, E0]), ALU.subtract), h)
                h = act(lambda e: e.activation(l3, l3, ACT.Exp), h)
                h = dve(lambda e: e.tensor_reduce(sm1[:, :], l3, AX.X, ALU.add), h)
                h = dve(lambda e: e.reciprocal(sm1[:, :], sm1[:, :]), h)
                h = dve(lambda e: e.tensor_tensor(l3, l3, sm1[:, :].unsqueeze(2).to_broadcast([128, 16, E0]), ALU.mult), h)
                for c in range(2):
                    ht_ = tr(T.t[:, 128 * c:128 * c + 128], lgt[:, c, :, :], ident[:, :], h, T.free)
                lgrel[0] = [ht_]
                LG = []
                h = act(lambda e: e.copy(sc[:, :], T.t[:, 0:256]), ht_, rt)
                T.free = [h]
                for rd in range(4):
                    v8, i8 = vals[:, 8 * rd:8 * rd + 8], ix[:, 8 * rd:8 * rd + 8]
                    a, bb = (sc, sc2) if rd % 2 == 0 else (sc2, sc)
                    h = dve(lambda e, v8=v8, a=a: e.max(v8, a[:, :]), h, rt)
                    h = dve(lambda e, v8=v8, a=a, i8=i8: e.max_index(i8, v8, a[:, :]), h)
                    if rd < 3:
                        h = dve(lambda e, v8=v8, a=a, bb=bb: e.match_replace(bb[:, :], v8, a[:, :], -1.0), h)
                hb = pool(lambda e, G8=G8: e.iota(bofi[:, :], [[0, 1]], base=0, channel_multiplier=1), rt)
                hb = dve(lambda e: e.tensor_scalar(bofi[:, :], bofi[:, :], 4, 8, ALU.arith_shift_right, ALU.arith_shift_left), hb)
                hb = dve(lambda e, G8=G8: e.tensor_scalar(bof[:, :], bofi[:, :], float(2048 * G8), None, ALU.add), hb)
                h = dve(lambda e: e.tensor_scalar(ixf[:, :], ix[:, :], bof[:, 0:1], None, ALU.add), h, hb)
                h1 = tr(T.t[0:32, 0:128], ixf[:, :], ident[:, :], h, T.free)
                h1 = tr(T.t[0:32, 128:256], vals[:, :], ident[:, :], h)
                rt = [h1]
                hh_ = []
                for bl in range(8):
                    jj, bg = bl % 4, 2 * G8 + bl // 4
                    ps = slice(32 * jj, 32 * jj + 32)
                    h = dve(lambda e, ps=ps, bg=bg, bl=bl: e.tensor_copy(idxJ[ps, bg, :], T.t[0:32, 16 * bl:16 * bl + 16]), h1)
                    h = dve(lambda e, ps=ps, bg=bg, bl=bl: e.tensor_copy(wJ[ps, bg, :], T.t[0:32, 128 + 16 * bl:128 + 16 * bl + 16]), h1)
                T.free = [h]
        P.barrier()
        M1.st.close()
        for s in banks:
            s.free = []

        M2 = Mem()
        rraw = M2.ring("wraw", 2, [128, 3, 1024])
        rwh = M2.ring("wh", 2, [128, 3, 1024], FR)
        rwl = M2.ring("wl", 2, [128, 3, 1024], FR)
        rxe = M2.ring("xe", 2, [128, 4, D])
        rxh = M2.ring("xeh", 2, [128, 2, 512], FR)
        rxl = M2.ring("xel", 2, [128, 2, 512], FR)
        rg = M2.ring("g2", 2, [128, 512])
        rgf = M2.ring("gf", 2, [128, 512])
        rhh = M2.ring("h2h", 2, [128, 4, 512], FR)
        rhl = M2.ring("h2l", 2, [128, 4, 512], FR)
        rye = M2.ring("ye", 3, [128, 4, D])
        GBK = Ring(banks[0:2])
        UBK = Ring(banks[2:4])
        TBK = Ring(banks[4:6])
        YBK = Ring(banks[6:8])
        scat = [None] * 4

        def e_weights(x):
            raw, wh, wl = rraw.next(), rwh.next(), rwl.next()
            lw = []
            for m, name in enumerate(("Wg", "Wu", "Wd")):
                lw.append(load(raw.t[:, m, :].rearrange("p (k f) -> p k f", k=4 if m == 2 else 2),
                               A[name][x].rearrange("(k p) f -> p k f", p=128), raw.free))
            out_ = []
            for m in range(3):
                h = act(lambda e, m=m: e.copy(wh.t[:, m, :], raw.t[:, m, :]), lw[m], wh.free)
                h2 = dve(lambda e, m=m: e.tensor_tensor(wl.t[:, m, :], raw.t[:, m, :], wh.t[:, m, :], ALU.subtract), h, wl.free)
                out_.append([h, h2])
            raw.free = [h, h2]
            return wh, wl, out_

        def e_gather(x):
            xe = rxe.next()
            return xe, [P.dma("gpsimd", "ga", 8, lambda e, bg=bg: e.indirect_dma_start(
                out=xe.t[:, bg, :], out_offset=None, in_=dH[:, :],
                in_offset=bass.IndirectOffsetOnAxis(ap=idxJ[:, bg, x:x + 1], axis=0)), xe.free) for bg in range(4)]

        def e_xprep(st):
            xe, ga = st
            xh, xl = rxh.next(), rxl.next()
            out_ = []
            for bp in range(4):
                tb = TBK.next()
                for k in range(2):
                    h = tr(tb.t[:, 128 * k:128 * k + 128], xe.t[:, bp, 128 * k:128 * k + 128], ident[:, :], ga[bp], tb.free)
                ts_ = slice(128 * bp, 128 * bp + 128)
                tv = tb.t[:, 0:256].rearrange("p (k t) -> p k t", k=2)
                h1 = act(lambda e, ts_=ts_, tv=tv: e.copy(xh.t[:, :, ts_], tv), h, xh.free)
                h2 = dve(lambda e, ts_=ts_, tv=tv: e.tensor_tensor(xl.t[:, :, ts_], tv, xh.t[:, :, ts_], ALU.subtract), h1, xl.free)
                tb.free = [h2]
                out_ += [h1, h2]
            xe.free = [h]
            return xh, xl, out_

        def e_down(x, tt, hh, hl, hw_, w, ye):
            wh, wl, hw = w
            yb = YBK.next()
            n = 0
            for f in range(4):
                for a_, b_ in ((hh, wh), (hh, wl), (hl, wh)):
                    hy = mm(yb.t[:, 0:256], a_.t[:, f, 128 * tt:128 * tt + 128], b_.t[:, 2, 256 * f:256 * f + 256],
                            n == 0, n == 11, hw_, hw[2], yb.free)
                    n += 1
            h = act(lambda e: e.activation(ye.t[:, tt, :], yb.t[:, 0:256], ACT.Copy, scale=wJ[:, tt, x:x + 1]), hy, ye.free)
            yb.free = [h]
            scat[tt] = P.dma("gpsimd", "sc", 8, lambda e: e.indirect_dma_start(
                out=dACC[:, :], out_offset=bass.IndirectOffsetOnAxis(ap=idxJ[:, tt, x:x + 1], axis=0),
                in_=ye.t[:, tt, :], in_offset=None, compute_op=ALU.add), h, scat[tt])
            return hy, scat[tt]

        gath = [e_gather(0), e_gather(1)]
        w = e_weights(0)
        xp = e_xprep(gath.pop(0))
        prev = None
        for x in range(E0 + 1):
            if x < E0:
                xh, xl, hx = xp
                wh, wl, hw = w
                hh, hl = rhh.next(), rhl.next()
                hws = []
            if prev:
                ye = rye.next()
                dn = []
            for f in range(4):
                if x < E0:
                    fs = lambda k: slice(512 * k + 128 * f, 512 * k + 128 * f + 128)
                    hb = []
                    bks = (GBK.next(), UBK.next())
                    for m, bk in enumerate(bks):
                        n = 0
                        for a_, b_ in ((wh, xh), (wl, xh), (wh, xl)):
                            for k in range(2):
                                h = mm(bk.t[:, :], a_.t[:, m, fs(k)], b_.t[:, k, :], n == 0, n == 5, hx, hw[m], bk.free)
                                n += 1
                        hb.append(h)
                    gs, gf = rg.next(), rgf.next()
                    bgk, bu = bks
                    h = act(lambda e, gs=gs, bgk=bgk: e.activation(gs.t[:, :], bgk.t[:, :], ACT.Gelu), hb[0], gs.free)
                    bgk.free = [h]
                    h = dve(lambda e, gs=gs, bu=bu, gf=gf: e.tensor_tensor(gf.t[:, :], gs.t[:, :], bu.t[:, :], ALU.mult),
                            h, hb[1], gf.free)
                    gs.free, bu.free = [h], [h]
                    h1 = act(lambda e, gf=gf, f=f, hh=hh: e.copy(hh.t[:, f, :], gf.t[:, :]), h, hh.free)
                    h2 = dve(lambda e, gf=gf, f=f, hh=hh, hl=hl: e.tensor_tensor(hl.t[:, f, :], gf.t[:, :], hh.t[:, f, :], ALU.subtract),
                             h1, hl.free)
                    gf.free = [h2]
                    hws += [h1, h2]
                if prev:
                    dn.append(e_down(x - 1, f, *prev, ye))
                if f == 1 and x + 1 < E0:
                    xp = e_xprep(gath.pop(0))
                    if x + 2 < E0:
                        gath.append(e_gather(x + 2))
            if prev:
                prev[0].free, prev[1].free = [dn[-1][0]], [dn[-1][0]]
                prev[3][0].free, prev[3][1].free = [dn[-1][0]], [dn[-1][0]]
                ye.free = [d[1] for d in dn]
            if x < E0:
                xh.free, xl.free = [hb[1]], [hb[1]]
                prev = (hh, hl, hws, w)
                if x + 1 < E0:
                    w = e_weights(x + 1)
        P.barrier()
        M2.st.close()
        for s in banks:
            s.free = []

        M3 = Mem()
        W1 = M3.sb("W1", [128, E1, 2, H1])
        W2 = M3.sb("W2", [128, E1, 8, D])
        lw1 = [load(W1[:, x, :, :], A["W1"][x].rearrange("(k p) f -> p k f", p=128)) for x in range(0)]
        te = M3.sb("te", [128, 2, TILES], I32)
        M4 = Mem()
        small = M4.ring("sma", 8, [128, 2, 16])
        w1r = M4.sb("w1r", [128, 2, E1])
        bgr = M4.sb("bgr", [128, E1])
        b2sb = M4.sb("b2sb", [E1, D])
        ld_wr = load(w1r[:, :, :], A["L1g"].rearrange("(k p) e -> p k e", p=128))
        ld_bg = load(bgr[:, :], A["bg"].rearrange("(a n) -> a n", a=1).to_broadcast([128, E1]))
        ld_b2 = load(b2sb[:, :], A["b2"])
        zer = M4.sb("zer", [128, 2, ROW])
        zeri = zer[:, :, :].bitcast(I32)
        io8 = M4.sb("io8", [128, 8], I32)
        io8f = M4.sb("io8f", [128, 8])
        tok = M4.sb("tok", [128, NT], I32)
        run = M4.sb("run", [128, 2, 8])
        rx = M4.ring("x2", 5, [128, 2, D])
        rct = M4.ring("c3T", 3, [128, 2, S])
        rq = M4.ring("Q3", 3, [128, 2, D])
        rs = M4.ring("S3", 2, [128, 3, 128])
        rz = M4.ring("z3", 6, [128, 2, ROW])
        rz2 = M4.ring("z32", 2, [128, 2, ROW])
        rzb = M4.ring("zb", 2, [128, 2, D])
        rzT = M4.ring("zT", 3, [128, 2, S])
        rlg = M4.ring("lg", 3, [128, 2, 8])
        rv8 = M4.ring("v8", 3, [128, 2, 8])
        ri8 = M4.ring("i8", 3, [128, 2, 8], U32)
        rrt = M4.ring("rt", 4, [128, 6, 2, 8])
        rpo = M4.ring("po", 4, [128, 2, 2], U32)
        rcb = M4.ring("cbT", 2, [8, 256])
        SBK, QBK = banks[0], banks[1]
        TBK, LBK = banks[2], banks[3]
        RBK, CBK, BBK = banks[4], banks[5], banks[6]

        h0 = pool(lambda e: e.memset(zer[:, :, :], 0.0))
        hzi = pool(lambda e: e.iota(zeri[:, :, D + 1:D + 2], [[128, 2], [0, 1]], base=N, channel_multiplier=1), h0)
        h1 = pool(lambda e: e.iota(io8[:, :], [[1, 8]], base=0, channel_multiplier=0))
        hio = dve(lambda e: e.tensor_copy(io8f[:, :], io8[:, :]), h1)
        htok = pool(lambda e: e.iota(tok[:, :], [[128, NT]], base=0, channel_multiplier=1))
        runs = [[dve(lambda e: e.memset(run[:, 0, :], 0.0))]]
        ztr = store(dOUT[N:N + 256, :].rearrange("(c p) d -> p c d", p=128), zer[:, :, 0:D], h0)
        xsd = []

        def layer1(b):
            rows = slice(256 * b, 256 * b + 256)
            x, ct = rx.next(), rct.next()
            lx = load(x.t[:, :, :], dACC[rows, :].rearrange("(c p) d -> p c d", p=128), x.free)
            lct = load(ct.t[:, :, :], A["ctxT"][:, rows].rearrange("(k p) t -> p k t", p=128), ct.free)
            yield
            q, sb_ = rq.next(), SBK.take()
            for k in range(2):
                h = mm(sb_.t[:, 0:256], ct.t[:, k, 0:128], ct.t[:, k, :], k == 0, k == 1, lct, sb_.free)
            for k in range(2):
                h = mm(sb_.t[:, 256:384], ct.t[:, k, 128:256], ct.t[:, k, 128:256], k == 0, k == 1)
            ct.free = [h]
            s3 = rs.next()
            dve(lambda e: e.tensor_tensor(s3.t[:, 0, :], sb_.t[:, 0:128], tri[:, :], ALU.mult), h, s3.free)
            dve(lambda e: e.tensor_tensor(s3.t[:, 2, :], sb_.t[:, 256:384], tri[:, :], ALU.mult), h)
            h3 = dve(lambda e: e.tensor_copy(s3.t[:, 1, :], sb_.t[:, 128:256]), h)
            sb_.free = [h3]
            hq = yield from layernorm2(x.t, q.t, D, lx, q.free)
            qb = QBK.take()
            mm(qb.t[:, 0:256], s3.t[:, 0, :], q.t[:, 0, :], True, True, hq, h3, qb.free)
            mm(qb.t[:, 256:512], s3.t[:, 1, :], q.t[:, 0, :], True, False)
            h = mm(qb.t[:, 256:512], s3.t[:, 2, :], q.t[:, 1, :], False, True)
            s3.free = [h]
            h4 = dve(lambda e: e.tensor_tensor(x.t[:, :, :], x.t[:, :, :], q.t[:, :, :], ALU.add), hq)
            yield
            h4 = dve(lambda e: e.tensor_tensor(x.t[:, :, :], x.t[:, :, :],
                     qb.t[:, :].rearrange("p (c d) -> p c d", c=2), ALU.add), h4, h)
            q.free, qb.free = [h4], [h4]
            s1 = store(dX3[rows, :].rearrange("(c p) d -> p c d", p=128), x.t[:, :, :], h4)
            z = rz.next()
            hz = yield from layernorm2(x.t, z.t, D, h4, z.free)
            x.free = [s1, hz]
            tb, zT = TBK.take(), rzT.next()
            tv = tb.t[:, :].rearrange("p (k t) -> p k t", k=2)
            for k in range(2):
                for c in range(2):
                    h = tr(tv[:, k, 128 * c:128 * c + 128], z.t[:, c, 128 * k:128 * k + 128], ident[:, :], hz, tb.free)
            hzt = act(lambda e: e.copy(zT.t[:, :, :], tv), h, zT.free)
            tb.free = [hzt]
            yield
            lb = LBK.take()
            for c in range(2):
                for k in range(2):
                    hl = mm(lb.t[:, 8 * c:8 * c + 8], zT.t[:, k, 128 * c:128 * c + 128], w1r[:, k, :], k == 0, k == 1,
                            hzt, ld_wr, lb.free)
            zT.free = [hl]
            yield
            lg, v8, i8, rt, po = (r.next() for r in (rlg, rv8, ri8, rrt, rpo))
            i8f, oh, prd, pos, cmb = (rt.t[:, m, :, :] for m in (0, slice(1, 3), 3, 4, 5))
            h = dve(lambda e: e.tensor_tensor(lg.t[:, :, :], lb.t[:, 0:16].rearrange("p (c x) -> p c x", c=2),
                    bgr[:, :].unsqueeze(1).to_broadcast([128, 2, 8]), ALU.add), hl, ld_bg, lg.free)
            lb.free = [h]
            hm = [dve(lambda e, c=c: e.max(v8.t[:, c, :], lg.t[:, c, :]), h, v8.free) for c in range(2)]
            hi = [dve(lambda e, c=c: e.max_index(i8.t[:, c, :], v8.t[:, c, :], lg.t[:, c, :]), hm, i8.free) for c in range(2)]
            hd = dve(lambda e: e.tensor_tensor(i8f[:, :, 2:3], v8.t[:, :, 1:2], v8.t[:, :, 0:1], ALU.subtract), hm, rt.free)
            lg.free = hi
            h = dve(lambda e: e.tensor_copy(i8f[:, :, 0:2], i8.t[:, :, 0:2]), hi, hd)
            v8.free, i8.free = [hd, hi], [h]
            he = act(lambda e: e.activation(i8f[:, :, 3:4], i8f[:, :, 2:3], ACT.Exp), h)
            for k in range(2):
                h = dve(lambda e, k=k: e.tensor_tensor(oh[:, k, :, :], i8f[:, :, k:k + 1].to_broadcast([128, 2, 8]),
                        io8f[:, :].unsqueeze(1).to_broadcast([128, 2, 8]), ALU.is_equal), h, hio)
            hk = dve(lambda e: e.tensor_tensor(prd[:, :, :], oh[:, 0, :, :], oh[:, 1, :, :], ALU.add), h)
            h = dve(lambda e: e.tensor_scalar(i8f[:, :, 4:5], i8f[:, :, 3:4], 1.0, None, ALU.add), he)
            h = dve(lambda e: e.reciprocal(i8f[:, :, 4:5], i8f[:, :, 4:5]), h)
            hw = dve(lambda e: e.tensor_tensor(i8f[:, :, 5:6], i8f[:, :, 3:4], i8f[:, :, 4:5], ALU.mult), h)
            rb = RBK.take()
            h1 = mm(rb.t[:, 0:16], stri[:, :], prd[:, :, :], True, True, hk, rb.free)
            hr = mm(rb.t[:, 16:32], ones[:, 0:128], prd[:, :, :], True, True)
            h = dve(lambda e: e.tensor_tensor(cmb[:, :, :], oh[:, 0, :, :], i8f[:, :, 4:5].to_broadcast([128, 2, 8]), ALU.mult), hw)
            h = dve(lambda e: e.tensor_tensor(pos[:, :, :], oh[:, 1, :, :], i8f[:, :, 5:6].to_broadcast([128, 2, 8]), ALU.mult), h)
            h = dve(lambda e: e.tensor_tensor(cmb[:, :, :], cmb[:, :, :], pos[:, :, :], ALU.add), h)
            cbk = CBK.take()
            for c in range(2):
                hct = tr(cbk.t[0:8, 128 * c:128 * c + 128], cmb[:, c, :], ident[:, :], h, cbk.free)
            yield
            cb = rcb.next()
            hcb = act(lambda e: e.copy(cb.t[:, :], cbk.t[0:8, 0:256]), hct, cb.free)
            cbk.free = [hcb]
            a, nx = b % 2, 1 - b % 2
            h = dve(lambda e: e.tensor_tensor(pos[:, 0, :], rb.t[:, 0:8], run[:, a, :], ALU.add), hr, runs[-1], h)
            h = dve(lambda e: e.tensor_tensor(run[:, nx, :], rb.t[:, 16:24], run[:, a, :], ALU.add), h)
            h = dve(lambda e: e.tensor_tensor(pos[:, 1, :], rb.t[:, 8:16], run[:, nx, :], ALU.add), h)
            h = dve(lambda e: e.tensor_tensor(run[:, nx, :], rb.t[:, 24:32], run[:, nx, :], ALU.add), h)
            rb.free = [h]
            runs.append([h])
            h = dve(lambda e: e.scalar_tensor_tensor(out=pos[:, :, :], in0=io8f[:, :].unsqueeze(1).to_broadcast([128, 2, 8]),
                    scalar=float(REG), in1=pos[:, :, :], op0=ALU.mult, op1=ALU.add), h)
            for k in range(2):
                h = dve(lambda e, k=k: e.tensor_tensor(prd[:, :, :], pos[:, :, :], oh[:, k, :, :], ALU.mult), h, hr)
                h = dve(lambda e, k=k: e.tensor_reduce(i8f[:, :, 6 + k], prd[:, :, :], AX.X, ALU.add), h)
            hp = dve(lambda e: e.tensor_copy(po.t[:, :, :], i8f[:, :, 6:8]), h, po.free)
            ht = dve(lambda e: e.tensor_copy(z.t[:, :, D + 1:D + 2].bitcast(I32), tok[:, 2 * b:2 * b + 2].unsqueeze(2)), htok, hz)
            bb = BBK.take()
            for c in range(2):
                hb = mm(bb.t[:, 256 * c:256 * c + 256], cb.t[:, 128 * c:128 * c + 128], b2sb[:, :], True, True, hcb, ld_b2, bb.free)
            cb.free = [hb]
            prev = None
            ends = []
            z2 = rz2.next()
            hz2 = pool(lambda e: e.tensor_copy(z2.t[:, :, 0:D], z.t[:, :, 0:D]), hz, z2.free)
            hz2 = [hz2, dve(lambda e: e.tensor_copy(z2.t[:, :, D + 1:D + 2].bitcast(I32), tok[:, 2 * b:2 * b + 2].unsqueeze(2)), htok, z2.free)]
            for k, zz in enumerate((z, z2)):
                h = dve(lambda e, k=k, zz=zz: e.tensor_copy(zz.t[:, :, D:D + 1], i8f[:, :, 4 + k:5 + k]), hw, hz2)
                sc = [P.dma("gpsimd", "sx", 8, lambda e, c=c, k=k, zz=zz: e.indirect_dma_start(
                      out=dXS[:, :], out_offset=bass.IndirectOffsetOnAxis(ap=po.t[:, c, k:k + 1], axis=0),
                      in_=zz.t[:, c, :], in_offset=None), h, hp, ht) for c in range(2)]
                ends += sc
                xsd.extend(sc)
                if k:
                    z2.free = sc
            rt.free = [h]
            yield
            zb = rzb.next()
            h = dve(lambda e: e.tensor_tensor(zb.t[:, :, :], z.t[:, :, 0:D], bb.t[:, :].rearrange("p (c d) -> p c d", c=2), ALU.add),
                    hb, zb.free)
            bb.free = [h]
            z.free = ends[0:2] + [h]
            po.free = ends
            zb.free = [store(dOUT[rows, :].rearrange("(c p) d -> p c d", p=128), zb.t[:, :, :], h)]

        def wload(x):
            lw1.append(load(W1[:, x, :, :], A["W1"][x].rearrange("(k p) f -> p k f", p=128), n=8))
            lw1.append(load(W2[:, x, :, :], A["W2"][x].rearrange("(k p) f -> p k f", p=128), n=8))
            yield

        def both(b):
            g = layer1(b)
            if b >= 2 and b - 2 < E1:
                yield from zip_(g, wload(b - 2))
            else:
                yield from g

        pipeline([(lambda b=b: both(b)) for b in range(B)])
        M5 = Mem()
        cn = M5.sb("cn", [128, 6, 8])
        cni = M5.sb("cni", [128, 8], I32)
        zp = M5.sb("zp", [128, 2, 8])
        pi = M5.sb("pi", [128, 1], I32)
        zpi = M5.sb("zpi", [128, 2, 8], U32)
        ti = M5.sb("ti", [128, TILES], I32)
        tf = M5.sb("tf", [128, 5, TILES])
        cmpt = M5.sb("cmpt", [128, TILES, 8])
        cnt = run[:, 0, :]
        hpi = pool(lambda e: e.iota(pi[:, :], [[0, 1]], base=0, channel_multiplier=1))
        hti = pool(lambda e: e.iota(ti[:, :], [[1, TILES]], base=0, channel_multiplier=0))
        h = dve(lambda e: e.tensor_copy(cn[:, 5, 0:1], pi[:, :]), hpi)
        h = dve(lambda e: e.scalar_tensor_tensor(out=cn[:, 4, :], in0=io8f[:, :], scalar=float(REG), in1=cnt, op0=ALU.mult, op1=ALU.add),
                runs[-1], h)
        for c in range(2):
            h = dve(lambda e, c=c: e.tensor_scalar(zp[:, c, :], cn[:, 4, :], cn[:, 5, 0:1], float(128 * c), ALU.add, ALU.add), h)
        h = dve(lambda e: e.tensor_copy(zpi[:, :, :], zp[:, :, :]), h)
        for x in range(E1):
            for c in range(2):
                xsd.append(P.dma("gpsimd", "sx", 8, lambda e, c=c, x=x: e.indirect_dma_start(
                    out=dXS[:, :], out_offset=bass.IndirectOffsetOnAxis(ap=zpi[:, c, x:x + 1], axis=0),
                    in_=zer[:, c, :], in_offset=None), h, hzi))
        h2 = dve(lambda e: e.tensor_scalar(cni[:, :], cnt, float(TS - 1), None, ALU.add), h)
        h2 = dve(lambda e: e.tensor_scalar(cni[:, :], cni[:, :], 8, None, ALU.arith_shift_right), h2)
        h2 = dve(lambda e: e.tensor_copy(cn[:, 0, :], cni[:, :]), h2)
        h2 = dve(lambda e: e.tensor_tensor_scan(cn[:, 1, :], ones[:, 0:8], cn[:, 0, :], 0.0, ALU.mult, ALU.add), h2)
        h = dve(lambda e: e.tensor_copy(tf[:, 0, :], ti[:, :]), hti)
        h = dve(lambda e: e.tensor_tensor(cmpt[:, :, :], tf[:, 0, :].unsqueeze(2).to_broadcast([128, TILES, 8]),
                cn[:, 1, :].unsqueeze(1).to_broadcast([128, TILES, 8]), ALU.is_ge), h, h2)
        h = dve(lambda e: e.tensor_reduce(tf[:, 1, :], cmpt[:, :, :], AX.X, ALU.add), h)
        h = dve(lambda e: e.tensor_tensor(cmpt[:, :, :], cmpt[:, :, :], cn[:, 0, :].unsqueeze(1).to_broadcast([128, TILES, 8]), ALU.mult), h)
        h = dve(lambda e: e.tensor_reduce(tf[:, 2, :], cmpt[:, :, :], AX.X, ALU.add), h)
        h = dve(lambda e: e.tensor_tensor(tf[:, 2, :], tf[:, 0, :], tf[:, 2, :], ALU.subtract), h)
        h = dve(lambda e: e.tensor_scalar(tf[:, 3, :], tf[:, 1, :], float(REG // TS), None, ALU.mult), h)
        h = dve(lambda e: e.tensor_tensor(tf[:, 2, :], tf[:, 2, :], tf[:, 3, :], ALU.add), h)
        h = dve(lambda e: e.tensor_scalar(tf[:, 4, :], tf[:, 1, :], 8.0, None, ALU.is_lt), h)
        h = dve(lambda e: e.tensor_tensor(te[:, 0, :], tf[:, 1, :], tf[:, 4, :], ALU.mult), h)
        h = dve(lambda e: e.tensor_scalar(tf[:, 3, :], tf[:, 4, :], -float(E1 * REG // TS), float(E1 * REG // TS), ALU.mult, ALU.add), h)
        h = dve(lambda e: e.tensor_tensor(tf[:, 2, :], tf[:, 2, :], tf[:, 4, :], ALU.mult), h)
        h = dve(lambda e: e.tensor_tensor(te[:, 1, :], tf[:, 2, :], tf[:, 3, :], ALU.add), h)
        hzt = store(dXS[E1 * REG:E1 * REG + TS, :].rearrange("(c p) d -> p c d", p=128), zer[:, :, :], hzi)
        P.barrier()
        M5.st.close()
        M4.st.close()
        for s in banks:
            s.free = []

        M7 = Mem()
        rxs = M7.ring("xs", 3, [128, 2, ROW])
        rxh = M7.ring("xh", 1, [128, 2, TS], FR)
        rxl = M7.ring("xl", 1, [128, 2, TS], FR)
        rgl = M7.ring("gl", 3, [128, 2, TS])
        rhh = M7.ring("hh", 3, [128, 4, TS], FR)
        rhl = M7.ring("hl", 3, [128, 4, TS], FR)
        rwh = M7.ring("wh", 3, [128, 1024], FR)
        rwl = M7.ring("wl", 3, [128, 1024], FR)
        rb1 = M7.ring("b1c", 3, [128, 8])
        ry = M7.ring("y1", 2, [128, 2, D])
        w1f = W1[:, :, :, :].rearrange("p x k f -> p (x k) f")
        w2f = W2[:, :, :, :].rearrange("p x k f -> p (x k f)")
        Tb = banks[0]
        Ab = Ring(banks[1:4])
        Yb = banks[4:8]
        regs = {}

        def expert(e, name, i):
            if regs.get(name, (None, None))[0] != i:
                regs[name] = (i, e.value_load(te[0:1, 0, i:i + 1], min_val=0, max_val=E1 - 1))
            return regs[name][1]

        def part(i, kind, half):
            wh, wl = rwh.next(), rwl.next()
            if kind == 1:
                def src(r):
                    return w1f[:, bass.ds(r * 2, 2), 512 * half:512 * half + 512]
                vh, vl = (w.t[:, :].rearrange("p (k f) -> p k f", k=2) for w in (wh, wl))
            else:
                def src(r):
                    return w2f[:, bass.ds(r * 2048 + 1024 * half, 1024)]
                vh, vl = wh.t[:, :], wl.t[:, :]
            who, name = HI[(kind, half)]
            h = who(lambda e: (e.copy if name == "a" else e.tensor_copy)(vh, src(expert(e, name, i))), wh.free)
            h2 = dve(lambda e: e.tensor_tensor(vl, src(expert(e, "v", i)), vh, ALU.subtract), h, wl.free)
            return wh, wl, vh, vl, [h, h2]

        HI = {(1, 0): (act, "a"), (1, 1): (pool, "p"), (2, 0): (act, "a"), (2, 1): (dve, "v")}

        def x_load(i):
            xs, b1c = rxs.next(), rb1.next()

            def ldx(e):
                r = e.value_load(te[0:1, 1, i:i + 1], min_val=0, max_val=E1 * REG // TS)
                return e.dma_start(xs.t[:, :, :], dXS.rearrange("(n c p) d -> n p c d", p=128, c=2)[bass.ds(r, 1), :, :, :]
                                   .rearrange("a p c d -> (a p) c d"))

            def ldb1(e):
                r = e.value_load(te[0:1, 0, i:i + 1], min_val=0, max_val=E1 - 1)
                return e.dma_start(b1c.t[:, :], A["b1"][bass.ds(r, 1), :, :].rearrange("a p c -> (a p) c"))
            return xs, b1c, P.dma("sync", "lx", 4, ldx, xs.free), P.dma("sync", "lb", 4, ldb1, b1c.free)

        def x_prep(st):
            xs, b1c, lx, lb = st
            Tb.take()
            tv = Tb.t[:, :].rearrange("p (k t) -> p k t", k=2)
            for k in range(2):
                for c in range(2):
                    h = tr(tv[:, k, 128 * c:128 * c + 128], xs.t[:, c, 128 * k:128 * k + 128], ident[:, :], lx, Tb.free)
            xh, xl = rxh.next(), rxl.next()
            h1 = act(lambda e: e.copy(xh.t[:, :, :], tv), h, xh.free)
            h2 = dve(lambda e: e.tensor_tensor(xl.t[:, :, :], tv, xh.t[:, :, :], ALU.subtract), h1, xl.free)
            Tb.free = [h2]
            return xh, xl, b1c, lb, [h1, h2], xs, h

        def up(i, x, half, w):
            xh, xl, b1c, lb, hx, xs, hxs = x
            wh, wl, vh, vl, hw = w
            hh, hl = rhh.next(), rhl.next()
            out_ = []
            for q in range(2):
                ab = Ab.next()
                for c in range(2):
                    fs = slice(128 * (2 * q + c), 128 * (2 * q + c) + 128)
                    o = ab.t[:, TS * c:TS * c + TS]
                    n = 0
                    for ww, xx in ((vh, xh), (vh, xl), (vl, xh)):
                        for k in range(2):
                            h = mm(o, ww[:, k, fs], xx.t[:, k, :], n == 0, n == 5, hx, hw, ab.free)
                            n += 1
                gl = rgl.next()
                for c in range(2):
                    cc = 4 * half + 2 * q + c
                    ha = act(lambda e, c=c, cc=cc, gl=gl, ab=ab: e.activation(gl.t[:, c, :], ab.t[:, TS * c:TS * c + TS],
                             ACT.Gelu, bias=b1c.t[:, cc:cc + 1]), h, lb, gl.free)
                ab.free = [ha]
                qs = slice(2 * q, 2 * q + 2)
                h1 = act(lambda e, qs=qs, gl=gl: e.copy(hh.t[:, qs, :], gl.t[:, :, :]), ha, hh.free)
                h2 = dve(lambda e, qs=qs, gl=gl: e.tensor_tensor(hl.t[:, qs, :], gl.t[:, :, :], hh.t[:, qs, :], ALU.subtract),
                         h1, hl.free)
                gl.free = [h2]
                out_ += [h1, h2]
            wh.free, wl.free = [h], [h]
            if half == 1:
                xh.free, xl.free, b1c.free = [h], [h], [ha]
            return hh, hl, out_, xs, hxs

        last = [None]

        def down(i, half, hp, w):
            hh, hl, hw_, xs, hxs = hp
            wh, wl, vh, vl, hw = w
            for tt in range(2):
                yb = Yb[2 * (i % 2) + tt]
                if half == 0:
                    yb.take()
                n = 0
                for c in range(4):
                    for a_, b_ in ((hh, vh), (hh, vl), (hl, vh)):
                        h = mm(yb.t[:, 0:256], a_.t[:, c, 128 * tt:128 * tt + 128], b_[:, 256 * c:256 * c + 256],
                               half == 0 and n == 0, half == 1 and n == 11, hw_, hw, yb.free)
                        n += 1
            hh.free, hl.free, wh.free, wl.free = [h], [h], [h], [h]
            if half == 1:
                y = ry.next()
                sc = []
                for tt in range(2):
                    yb = Yb[2 * (i % 2) + tt]
                    h2 = dve(lambda e, tt=tt, yb=yb: e.tensor_scalar(y.t[:, tt, :], yb.t[:, 0:256], xs.t[:, tt, D:D + 1], None,
                             ALU.mult), h, y.free)
                    yb.free = [h2]
                    last[0] = P.dma("gpsimd", "sy", 4, lambda e, tt=tt: e.indirect_dma_start(
                        out=dOUT[:, :], out_offset=bass.IndirectOffsetOnAxis(ap=xs.t[:, tt, D + 1:D + 2].bitcast(U32), axis=0),
                        in_=y.t[:, tt, :], in_offset=None, compute_op=ALU.add), h2, last[0])
                    sc.append(last[0])
                y.free = sc
                xs.free = sc + [hxs]

        units = []
        for i in range(TILES):
            units.append((i, 1, 0))
            if i:
                units.append((i - 1, 2, 1))
            units += [(i, 1, 1), (i, 2, 0)]
        units.append((TILES - 1, 2, 1))
        wq_ = [part(*units[n]) for n in range(2)]
        xl_ = x_load(0)
        x = x_prep(xl_)
        xl_ = x_load(1)
        hp = {}
        for n, (i, kind, half) in enumerate(units):
            if n + 2 < len(units):
                wq_.append(part(*units[n + 2]))
            if kind == 1:
                hp[(i, half)] = up(i, x, half, wq_[n])
                if half == 1 and i + 1 < TILES:
                    x = x_prep(xl_)
            else:
                down(i, half, hp.pop((i, half)), wq_[n])
                if half == 1 and i + 3 <= TILES:
                    xl_ = x_load(i + 2)
            if n == 2:
                pass
            wq_[n] = None
        P.barrier()
        M7.st.close()
        M3.st.close()
        for s in banks:
            s.free = []

        M8 = Mem()
        small = M8.ring("smc", 8, [128, 2, 16])
        gam = M8.sb("gam", [128, D])
        bet = M8.sb("bet", [128, D])
        ld_ga = load(gam[:, :], A["gamma"].rearrange("(a n) -> a n", a=1).to_broadcast([128, D]))
        ld_be = load(bet[:, :], A["beta"].rearrange("(a n) -> a n", a=1).to_broadcast([128, D]))
        rz = M8.ring("zc", 6, [128, 2, D])
        rx = M8.ring("xc", 6, [128, 2, D])
        ry = M8.ring("yc", 3, [128, 2, D])

        def last_norm(b):
            rows = slice(256 * b, 256 * b + 256)
            z, x = rz.next(), rx.next()
            lz = load(z.t[:, :, :], dOUT[rows, :].rearrange("(c p) d -> p c d", p=128), z.free)
            lx = load(x.t[:, :, :], dX3[rows, :].rearrange("(c p) d -> p c d", p=128), x.free)
            yield
            yield
            sm = small.next()
            s = sm.t
            hb = pool(lambda e: e.tensor_tensor(x.t[:, :, :], x.t[:, :, :], bet[:, :].unsqueeze(1).to_broadcast([128, 2, D]), ALU.add),
                      lx, ld_be)
            h = [dve(lambda e, c=c: e.bn_stats(s[:, c, 0:6], z.t[:, c, :]), lz, sm.free) for c in range(2)]
            h = [dve(lambda e, c=c: e.bn_aggr(s[:, c, 6:8], s[:, c, 0:6]), h) for c in range(2)]
            h = dve(lambda e: e.tensor_scalar(s[:, :, 9:10], s[:, :, 7:8], EPS, None, ALU.add), h)
            h = pool(lambda e: e.tensor_tensor(s[:, :, 8:9], s[:, :, 9:10], mhalf[:, :].unsqueeze(1).to_broadcast([128, 2, 1]), ALU.pow), h, c_mh)
            yield
            y = ry.next()
            for c in range(2):
                h1 = dve(lambda e, c=c: e.scalar_tensor_tensor(out=z.t[:, c, :], in0=z.t[:, c, :], scalar=s[:, c, 6:7], in1=gam[:, :],
                         op0=ALU.subtract, op1=ALU.mult), h, ld_ga)
                h2 = dve(lambda e, c=c: e.scalar_tensor_tensor(out=y.t[:, c, :], in0=z.t[:, c, :], scalar=s[:, c, 8:9], in1=x.t[:, c, :],
                         op0=ALU.mult, op1=ALU.add), h1, hb, y.free)
            sm.free, z.free, x.free = [h2], [h2], [h2]
            y.free = [P.dma("sync", "out", 4, lambda e: e.dma_start(out[rows, :].rearrange("(c p) d -> p c d", p=128), y.t[:, :, :]), h2)]

        pipeline([(lambda b=b: last_norm(b)) for b in range(B)])
        M8.st.close()
        P.barrier()
        block = ctx.enter_context(nc.Block())
        P.emit(block)


STOP = 99


def kernel(**inputs):
    import concourse.bacc as _bacc
    from concourse.bass_utils import run_bass_kernel_spmd as _run

    i = {k: np.asarray(v) for k, v in inputs.items()}
    t = lambda a: np.ascontiguousarray(np.swapaxes(a, -1, -2))
    arrays = {
        "x": i["x"].reshape(N, D),
        "ctx": i["ctx_1024"].reshape(N, D),
        "ctxT": t(i["ctx_1024"].reshape(N, D)),
        "igate_w": t(i["L0_xattn_igate_w"]).reshape(6, 128, 8),
        "fgate_w": t(i["L0_xattn_fgate_w"]).reshape(6, 128, 8),
        "igate_b": i["L0_xattn_igate_b"],
        "fgate_b": i["L0_xattn_fgate_b"],
        "ln_scale": i["L0_xattn_ln_scale"],
        "gate_w": t(i["L0_ffn_gate_w"]),
        "Wg": t(i["L0_ffn_Wg"]), "Wu": t(i["L0_ffn_Wu"]), "Wd": t(i["L0_ffn_Wd"]),
        "Ws_g": t(i["L0_ffn_Ws_g"]), "Ws_u": t(i["L0_ffn_Ws_u"]), "Ws_d": t(i["L0_ffn_Ws_d"]),
        "L1g": i["L1_ffn_Wg"], "bg": i["L1_ffn_bg"],
        "W1": i["L1_ffn_W1"], "b1": t(i["L1_ffn_b1"].reshape(E1, 8, 128)),
        "W2": i["L1_ffn_W2"], "b2": i["L1_ffn_b2"],
        "gamma": i["L1_ffn_gamma"], "beta": i["L1_ffn_beta"],
    }
    nc = _bacc.Bacc("TRN2", target_bir_lowering=False, num_devices=1)
    maps, aps = {}, {}
    for name, a in arrays.items():
        a = np.ascontiguousarray(a)
        maps["in_" + name] = a
        aps[name] = nc.dram_tensor("in_" + name, a.shape, mybir.dt.from_np(a.dtype), kind="ExternalInput").ap()
    out = nc.dram_tensor("out_0", [N, D], FP, kind="ExternalOutput").ap()
    build(nc, aps, out, STOP)
    r = _run(nc, [maps], core_ids=[0])
    return r.results[0]["out_0"].reshape(B, S, D)
```

```python
import numpy as np
import concourse.bass as bass
from concourse import mybir
from contextlib import ExitStack

FP = mybir.dt.float32
BF = mybir.dt.bfloat16
U32 = mybir.dt.uint32
I32 = mybir.dt.int32
FR = mybir.dt.float32r
ALU = mybir.AluOpType
ACT = mybir.ActivationFunctionType
AX = mybir.AxisListType

B, S, D, NH = 16, 256, 256, 8
N = B * S
E0, F0, CAP = 16, 512, 32
E1, H1 = 8, 1024
NT = N // 128
TS = 256
TILES = (2 * N + E1 * (TS - 1)) // TS
EPS = 1e-5
REG = N + TS
R32 = float(np.sqrt(32.0))


class Handle:
    __slots__ = ("eng", "sem", "val", "marked", "t")

    def __init__(self, eng, sem=None, val=0):
        self.eng, self.sem, self.val, self.marked, self.t = eng, sem, val, False, 0.0


def flat(x):
    if x is None:
        return
    if isinstance(x, Handle):
        yield x
    else:
        for y in x:
            yield from flat(y)


class Program:

    def __init__(self, nc, ctx):
        self.nc, self.ctx = nc, ctx
        self.q = {e: [] for e in ("tensor", "vector", "scalar", "gpsimd", "sync")}
        self.sems = {e: ctx.enter_context(nc.semaphore(f"s_{e}")) for e in self.q}
        self.lanes = {}
        self.time = {e: 0.0 for e in self.q}

    def op(self, eng, fn, *after, cost=100):
        h = Handle(eng)
        ws = list(flat(after))
        self.time[eng] = h.t = max([self.time[eng]] + [w.t + (110 if w.eng == eng else 180) for w in ws]) + cost
        for w in ws:
            w.marked = True
        self.q[eng].append((fn, ws, h))
        return h

    def lane(self, name, n):
        if name not in self.lanes:
            self.lanes[name] = [[self.ctx.enter_context(self.nc.semaphore(f"d_{name}{i}")), 0, None]
                                for i in range(n)] + [0]
        return self.lanes[name]

    def dma(self, eng, name, n, fn, *after):
        l = self.lane(name, n)
        k = l[-1]
        l[-1] = (k + 1) % n
        sem, cnt, last = l[k]
        h = Handle(eng, sem, cnt + 16)
        self.time[eng] = max([self.time[eng]] + [w.t for w in flat(after)]) + (1040 if eng == "gpsimd" else 50)
        h.t = self.time[eng] + 2500
        l[k][1] += 16
        l[k][2] = h
        h.marked = True
        ws = list(flat(after)) + ([last] if last else [])
        for w in ws:
            w.marked = True
        self.q[eng].append((fn, ws, h))
        return h

    def barrier(self):
        hs = []
        for e in self.q:
            own = [h for _, _, h in self.q[e] if h is not None and h.sem is None]
            hs += own[-1:]
        for l in self.lanes.values():
            hs += [x[2] for x in l[:-1] if x[2]]
        for h in hs:
            h.marked = True
        now = max([h.t for h in hs] + list(self.time.values()))
        for e in self.q:
            self.time[e] = now
            self.q[e].append((None, hs, None))

    def emit(self, block):
        for e in self.q:
            n = 0
            for fn, ws, h in self.q[e]:
                if h is not None and h.sem is None and h.marked:
                    n += 1
                    h.val = n
                    h.sem = self.sems[e]

        def replay(eng, e):
            seen = {}
            for fn, ws, h in self.q[e]:
                need = {}
                for w in ws:
                    need[w.sem] = max(need.get(w.sem, 0), w.val)
                for s, v in need.items():
                    if seen.get(s, 0) < v:
                        eng.wait_ge(s, v)
                        seen[s] = v
                if fn is None:
                    continue
                ins = fn(eng)
                if h.marked:
                    ins.then_inc(h.sem, 1 if h.sem is self.sems[e] else 16)

        for e in self.q:
            register = {"tensor": block.tensor, "vector": block.vector, "scalar": block.scalar,
                             "gpsimd": block.gpsimd, "sync": block.sync}[e]
            register(lambda eng, e=e: replay(eng, e))


class Slot:

    def __init__(self, t):
        self.t, self._free, self.busy = t, [], False

    @property
    def free(self):
        return self._free

    @free.setter
    def free(self, x):
        self._free, self.busy = list(flat(x)), False

    def take(self):
        assert not self.busy, "the buffer's last users aren't queued yet"
        self.busy = True
        return self


class Ring:
    def __init__(self, slots):
        self.slots, self.i = slots, -1

    def next(self):
        self.i = (self.i + 1) % len(self.slots)
        return self.slots[self.i].take()

    def get(self):
        me = Blocked()
        while True:
            free = [x for x in self.slots if not x.busy]
            if free:
                return min(free, key=lambda x: max([h.t for h in x.free], default=0)).take()
            yield me


class Blocked:
    __slots__ = ()


def until(cond):
    me = Blocked()
    while not cond():
        yield me


def interleave(gens):
    ready = [(0.0, n, g) for n, g in enumerate(gens)]
    blocked = []
    now = 0.0
    while ready or blocked:
        assert ready, "all generators are blocked"
        ready.sort(key=lambda x: x[:2])
        t, n, g = ready.pop(0)
        now = max(now, t)
        todo = [(n, g, None)]
        moved = False
        while todo:
            n, g, last = todo.pop(0)
            try:
                got = next(g)
            except StopIteration:
                moved = True
            else:
                if isinstance(got, Blocked):
                    moved = moved or got is not last
                    blocked.append((n, g, got))
                else:
                    ready.append((got if isinstance(got, float) else max([h.t for h in flat(got)], default=now), n, g))
                    moved = True
            if moved and not todo and blocked:
                todo, blocked, moved = sorted(blocked, key=lambda x: x[0]), [], False


def pipeline(makers):
    run = []
    for make in list(makers) + [None] * 99:
        if make:
            run.append(make())
        run = [g for g in run if next(g, run) is not run]


def zip_(*gens):
    live = list(gens)
    while live:
        live = [g for g in live if next(g, live) is not live]
        if live:
            yield


class Tables:

    def __init__(self):
        self.queue, self.kind, self.n = [], None, 0

    def get(self, kind):
        me = Blocked()
        self.queue.append(me)
        while self.queue[0] is not me or (self.n and self.kind != kind):
            yield me
        self.queue.pop(0)
        self.kind = kind
        self.n += 1

    def put(self):
        self.n -= 1


def build(nc, A, out, stop=99):
    ctx = ExitStack()
    with ctx:
        P = Program(nc, ctx)

        def sem(name):
            return ctx.enter_context(nc.semaphore(name))

        def dram(name, shape, dt=FP):
            return nc.dram_tensor(name, shape, dt, kind="Internal").ap()

        dH = dram("dH", [N, D])
        dACC = dram("dACC", [N, D])
        dX3 = dram("dX3", [N, D])
        dZ = dram("dZ", [N + TS, D])
        dSL = dram("dSL", [E1 * REG + TS, 2])
        dOUT = dram("dOUT", [N + TS, D])

        banks = [Slot(ctx.enter_context(nc.psum_tensor(f"pb{i}", [128, 512], FP))) for i in range(8)]

        class Mem:
            made = 0

            def __init__(self):
                self.st = ExitStack()

            def sb(self, name, shape, dt=FP):
                Mem.made += 1
                return self.st.enter_context(nc.sbuf_tensor(f"{name}_{Mem.made}", shape, dt))

            def ring(self, name, n, shape, dt=FP):
                return Ring([Slot(self.sb(f"{name}{i}", shape, dt)) for i in range(n)])

        G = Mem()
        ctx.enter_context(G.st)

        pe = lambda fn, *a, cost=100: P.op("tensor", fn, *a, cost=cost)
        dve = lambda fn, *a, n=8: P.op("vector", fn, *a, cost=60 + 1.04 * n)
        act = lambda fn, *a, n=128: P.op("scalar", fn, *a, cost=190 + 0.83 * n)
        pool = lambda fn, *a, n=150: P.op("gpsimd", fn, *a, cost=100 + 3.4 * n)

        def load(out_, in_, *a, n=8):
            return P.dma("sync", "ld", n, lambda e: e.dma_start(out_, in_), *a)

        def store(out_, in_, *a, n=4):
            return P.dma("sync", "st", n, lambda e: e.dma_start(out_, in_), *a)

        def load2(out_, in_, *a, n=8):
            return P.dma("scalar", "ld2", n, lambda e: e.dma_start(out_, in_), *a)

        def store2(out_, in_, *a, n=4):
            return P.dma("scalar", "st2", n, lambda e: e.dma_start(out_, in_), *a)

        def mm(o, l, r, s, t, *a):
            return pe(lambda e: e.matmul(o, l, r, start=s, stop=t), *a,
                      cost=max(64, r.free_size()) * (4 if r.dtype == FP else 1) / 2.4)

        def tr(o, i, idn, *a):
            return pe(lambda e: e.transpose(o, i, idn), *a, cost=210)

        ident = G.sb("ident", [128, 128])
        ones = G.sb("ones", [128, 256])
        hm8 = G.sb("hm8", [128, 8])
        hm4 = G.sb("hm4", [128, 4])
        tri = G.sb("tri", [128, 128])
        stri = G.sb("stri", [128, 128])
        idxJ = G.sb("idxJ", [128, 4, E0], U32)
        wJ = G.sb("wJ", [128, 4, E0])

        c_id0 = pool(lambda e: e.memset(ident[:, :], 0.0))
        c_ones = pool(lambda e: e.memset(ones[:, :], 1.0))
        c_id = pool(lambda e: e.affine_select(out=ident[:, :], in_=ident[:, :], compare_op=ALU.not_equal, fill=1.0,
                                              base=0, pattern=[[-1, 128]], channel_multiplier=1), c_id0)
        c = None
        for j in range(4):
            c = dve(lambda e, j=j: e.tensor_copy(hm8[32 * j:32 * j + 32, :], ident[0:32, 0:8]), c_id)
        c_h8 = c
        c_a = pool(lambda e: e.affine_select(out=hm4[:, :], in_=ones[:, 0:4], compare_op=ALU.is_ge, fill=0.0,
                                             base=0, pattern=[[-32, 4]], channel_multiplier=1), c_ones)
        c_h4 = pool(lambda e: e.affine_select(out=hm4[:, :], in_=hm4[:, :], compare_op=ALU.is_ge, fill=0.0,
                                              base=31, pattern=[[32, 4]], channel_multiplier=-1), c_a)
        c_tri = pool(lambda e: e.affine_select(out=tri[:, :], in_=ones[:, 0:128], compare_op=ALU.is_ge, fill=0.0,
                                               base=0, pattern=[[1, 128]], channel_multiplier=-1), c_ones)
        c_stri = pool(lambda e: e.affine_select(out=stri[:, :], in_=ones[:, 0:128], compare_op=ALU.is_gt, fill=0.0,
                                                base=0, pattern=[[1, 128]], channel_multiplier=-1), c_ones)
        mhalf = G.sb("mhalf", [128, 1])
        c_mh = pool(lambda e: e.memset(mhalf[:, :], -0.5))
        identb = G.sb("identb", [128, 128], BF)
        maskb = G.sb("maskb", [128, 128], BF)
        c_mk = [dve(lambda e: e.tensor_copy(identb[:, :], ident[:, :]), c_id),
                dve(lambda e: e.tensor_scalar(maskb[:, :], tri[:, :], 1.0, 1e30, ALU.subtract, ALU.mult), c_tri)]
        consts = [c_id, c_ones, c_h8, c_h4, c_tri, c_stri]

        M1 = Mem()
        gw0 = M1.sb("gw0", [128, 2, 6, 8])
        gw = M1.sb("gw", [128, 4, 2, 4, 8])
        gbr = M1.sb("gbr", [128, 2, 8])
        gb = M1.sb("gb", [128, 2, 4, 8])
        lns = M1.sb("lns", [128, D])
        rw = M1.sb("rw", [128, 2, E0])
        rth = M1.sb("rth", [128, 2, E0], FR)
        rtl = M1.sb("rtl", [128, 2, E0], FR)
        wsh = M1.sb("wsh", [128, 3, 1024], FR)
        wsl = M1.sb("wsl", [128, 3, 1024], FR)
        onesb = M1.sb("onesb", [128, 128], BF)
        pint = M1.sb("pint", [128, 3], I32)
        pflt = M1.sb("pflt", [128, 3])
        i8r = M1.sb("i8r", [128, 8], I32)
        i8q = M1.sb("i8q", [128, 8])
        sel3 = M1.sb("sel3", [128, 3])
        hmb = M1.sb("hmb", [128, 8], BF)
        z1 = pool(lambda e: e.memset(gw[:, :, :, :, :], 0.0))
        z2 = pool(lambda e: e.memset(gb[:, :, :, :], 0.0))
        ld = []
        for t, w in enumerate((A["igate_w"], A["fgate_w"])):
            ld.append(load(gw0[:, t, :, :], w.rearrange("k p h -> p k h")))
        for t, w in enumerate((A["igate_b"], A["fgate_b"])):
            ld.append(load(gbr[:, t, :], w.rearrange("(a n) -> a n", a=1).to_broadcast([128, 8])))

        ld_gw = []
        for r in range(3):
            ld_gw.append(dve(lambda e, r=r: e.tensor_copy(gw[:, 0:2, :, r, :], gw0[:, :, 0:2, :].rearrange("p t k h -> p k t h")), ld, z1))
            ld_gw.append(dve(lambda e, r=r: e.tensor_tensor(gw[:, 2:4, :, r, :], gw0[:, :, 2:4, :].rearrange("p t k h -> p k t h"),
                         gw0[:, :, 4:6, :].rearrange("p t k h -> p k t h"), ALU.add), ld, z1))
            ld_gw.append(dve(lambda e, r=r: e.tensor_copy(gb[:, :, r, :], gbr[:, :, :]), ld, z2))
        c_ob = dve(lambda e: e.tensor_copy(onesb[:, :], ones[:, 0:128]), c_ones)
        h = pool(lambda e: e.iota(pint[:, 0:1], [[0, 1]], base=0, channel_multiplier=1))
        h2 = pool(lambda e: e.iota(i8r[:, :], [[1, 8]], base=0, channel_multiplier=0))
        h = dve(lambda e: e.tensor_scalar(pint[:, 1:2], pint[:, 0:1], 7, None, ALU.bitwise_and), h)
        h = dve(lambda e: e.tensor_scalar(pint[:, 2:3], pint[:, 0:1], 3, 3, ALU.logical_shift_right, ALU.bitwise_and), h)
        h = dve(lambda e: e.tensor_copy(pflt[:, :], pint[:, :]), h)
        h2 = dve(lambda e: e.tensor_copy(i8q[:, :], i8r[:, :]), h2)
        c_hm = dve(lambda e: e.tensor_scalar(hmb[:, :], i8q[:, :], pflt[:, 1:2], None, ALU.is_equal), h, h2)
        c_sel = [dve(lambda e, r=r: e.tensor_scalar(sel3[:, r:r + 1], pflt[:, 2:3], float(r), None, ALU.is_equal), h) for r in range(3)]

        def later_loads():
            qx = rqx.slots[1].take()
            ws = []
            wsr = qx.t[:, 0, :, :].rearrange("p a f -> p (a f)")
            free = None
            for m, (w, k) in enumerate((("Ws_g", 2), ("Ws_u", 2), ("Ws_d", 4))):
                w = load(wsr.rearrange("p (k f) -> p k f", k=k), A[w].rearrange("(k p) f -> p k f", p=128), free)
                yield w
                h = act(lambda e, m=m: e.copy(wsh[:, m, :], wsr), w, n=1024)
                yield h
                h2 = dve(lambda e, m=m: e.tensor_tensor(wsl[:, m, :], wsr, wsh[:, m, :], ALU.subtract), h, n=1024)
                free = h2
                ws.extend([h, h2])
                yield h2
            qx.free = [ws]
            ws_w.extend(ws)

        ws_w = []
        ld_ln = load(lns[:, :], A["ln_scale"].rearrange("(a n) -> a n", a=1).to_broadcast([128, D]))
        h = load(rw[:, :, :], A["gate_w"].rearrange("(k p) e -> p k e", p=128))
        h = dve(lambda e: e.tensor_copy(rth[:, :, :], rw[:, :, :]), h)
        rw_w = [h, dve(lambda e: e.tensor_tensor(rtl[:, :, :], rw[:, :, :], rth[:, :, :], ALU.subtract), h)]

        rXp = M1.ring("xp", 2, [128, 2, D])
        rX = M1.ring("xb", 3, [128, 2, D])
        rC = M1.ring("cb", 3, [128, 2, D])
        rCT = M1.ring("cT", 7, [128, 2, S])
        rQ = M1.ring("q", 2, [128, 2, D])
        rQT = M1.ring("qT", 7, [128, 2, S])
        rqx = M1.ring("qx", 2, [128, 2, 4, S])
        small = M1.ring("sm", 8, [128, 2, 16])
        rHh = M1.ring("hTh", 2, [128, 2, 512], FR)
        rHl = M1.ring("hTl", 2, [128, 2, 512], FR)
        rX1 = M1.ring("x1", 5, [128, 2, D])
        rD = M1.ring("Dm", 5, [128, 4, 128])
        rCm = M1.ring("Cm", 3, [128, 4, 128])
        rV = M1.ring("V1", 2, [128, 2, 8, 33])
        rW = M1.ring("wV", 1, [128, 8, 33])
        rKV = M1.ring("KV", 1, [128, 2, 4, 33])
        rO = M1.ring("Oo", 2, [128, 8, 33])
        rn = M1.ring("nn", 2, [128, 3, 8])
        rh = M1.ring("hh1", 2, [128, D])
        rH = M1.ring("Ht", 2, [128, D])
        rgc = M1.ring("gc", 1, [128, 2, 2, 4, 32])
        rcols = M1.ring("cols", 2, [128, 6, 128])
        rMx = M1.ring("Mx", 2, [128, 8, S], BF)
        row = {n: M1.sb(n, [128, S]) for n in ("igr", "zr", "er", "lr", "csr", "ar", "Mr", "eer", "wfr")}
        row.update(r1=row["igr"], r2=row["zr"], tr=row["er"], nMr=row["lr"])
        rowb = {n: M1.sb(n, [128, S], BF) for n in ("m1", "m2", "mr")}
        lgt = M1.sb("lgt", [128, 2, 8, E0])
        rg = M1.ring("gs", 2, [128, 512])
        rgf = M1.ring("gf", 1, [128, 512])
        rhh = M1.ring("hhs", 1, [128, 4, 512], FR)
        rhl = M1.ring("hls", 1, [128, 4, 512], FR)
        rys = M1.ring("ys", 2, [128, D])
        sm1 = M1.sb("sm1", [128, 16])
        sc = M1.sb("sc", [128, S])
        sc2 = M1.sb("sc2", [128, S])
        vals = M1.sb("vals", [128, CAP])
        ix = M1.sb("ix", [128, CAP], U32)
        ixf = M1.sb("ixf", [128, CAP])
        bof = M1.sb("bof", [128, 1])

        TB = SBk = BBk = FB = Ring(banks[0:5])
        OB1, OB2 = Ring(banks[5:7]), Ring(banks[7:8])
        tables = Tables()
        for sl in rV.slots:
            sl.free = [pool(lambda e, t=sl.t: e.memset(t[:, :, :, 32:33], 1.0))]

        def norm(src, dst, nc_, after, dst_free):
            sm = yield from small.get()
            s = sm.t
            h = [dve(lambda e, c=c: e.bn_stats(s[:, c, 0:6], src(c)), after, sm.free, n=D) for c in range(nc_)]
            yield h
            h = [dve(lambda e, c=c: e.bn_aggr(s[:, c, 6:8], s[:, c, 0:6]), h) for c in range(nc_)]
            yield h
            h = dve(lambda e: e.tensor_scalar(s[:, 0:nc_, 9:10], s[:, 0:nc_, 7:8], EPS, None, ALU.add), h)
            yield h
            h = pool(lambda e: e.tensor_tensor(s[:, 0:nc_, 8:9], s[:, 0:nc_, 9:10],
                     mhalf[:, :].unsqueeze(1).to_broadcast([128, nc_, 1]), ALU.pow), h, c_mh)
            yield h
            if dst is None:
                return sm, h
            h = [dve(lambda e, c=c: e.tensor_scalar(dst(c), src(c), s[:, c, 6:7], s[:, c, 8:9],
                     ALU.subtract, ALU.mult), h, dst_free, n=D // 2) for c in range(nc_)]
            sm.free = [h]
            return h

        BT = {}
        GR = {}
        PR = {}

        def prep(b):
            g, j = b // 4, b % 4
            rows = slice(256 * b, 256 * b + 256)
            x = yield from rXp.get()
            cT = yield from rCT.get()
            lx = load(x.t[:, :, :], A["x"][rows, :].rearrange("(c p) d -> p c d", p=128), x.free)
            lct = load(cT.t[:, :, :], A["ctxT"][:, rows].rearrange("(k p) t -> p k t", p=128), cT.free)
            yield lx
            q = yield from rQ.get()
            hq = yield from norm(lambda c: x.t[:, c, :], lambda c: q.t[:, c, :], 2, lx, q.free)
            x.free = [hq]
            yield hq
            tb = yield from TB.get()
            tv = tb.t[:, :].rearrange("p (k t) -> p k t", k=2)
            for k in range(2):
                for c in range(2):
                    h = tr(tv[:, k, 128 * c:128 * c + 128], q.t[:, c, 128 * k:128 * k + 128], ident[:, :],
                           hq, consts, tb.free)
            q.free = [h]
            qT = yield from rQT.get()
            hqT = act(lambda e: e.copy(qT.t[:, :, :], tv), h, qT.free, n=512)
            tb.free = [hqT]
            yield hqT
            yield from until(lambda: j == 0 or "gc" in GR.get(g, {}))
            if j == 0:
                gc = yield from rgc.get()
                GR[g] = {"gc": gc, "gates": []}
            gc = GR[g]["gc"]
            tb = yield from TB.get()
            for c in range(2):
                for k in range(4):
                    src = qT.t if k < 2 else cT.t
                    h = mm(tb.t[:, 64 * c:64 * c + 64], src[:, k % 2, 128 * c:128 * c + 128],
                           gw[:, k, :, :, :].rearrange("p t r h -> p (t r h)"), k == 0, k == 3, hqT, lct, ld_gw, tb.free)
            h = dve(lambda e: e.tensor_tensor(gc.t[:, :, :, j, :].rearrange("p t c r -> p c t r"),
                    tb.t[:, 0:128].rearrange("p (c t r) -> p c t r", c=2, t=2),
                    gb[:, :, :, :].rearrange("p t r h -> p t (r h)").unsqueeze(1).to_broadcast([128, 2, 2, 32]), ALU.add),
                    h, ld_gw, gc.free, n=128)
            tb.free = [h]
            GR[g]["gates"].append(h)
            BT[b] = dict(cT=cT, qT=qT, lct=lct, hqT=hqT)

        def rows_(b):
            rows = slice(256 * b, 256 * b + 256)
            cb = yield from rC.get()
            x = yield from rX.get()
            lc = load(cb.t[:, :, :], A["ctx"][rows, :].rearrange("(c p) d -> p c d", p=128), cb.free)
            lx = load(x.t[:, :, :], A["x"][rows, :].rearrange("(c p) d -> p c d", p=128), x.free)
            yield from until(lambda: b in BT)
            BT[b].update(x=x, cb=cb, lc=lc, lx=lx)

        def group(g):
            yield from until(lambda: len(GR.get(g, {}).get("gates", [])) == 4)
            gc, gates = GR[g]["gc"], GR[g]["gates"]
            yield gates
            tb = yield from TB.get()
            for t in range(2):
                for c in range(2):
                    h = tr(tb.t[:, 256 * t + 128 * c:256 * t + 128 * c + 128],
                           gc.t[:, t, c, :, :].rearrange("p j r -> p (j r)"), ident[:, :], gates, tb.free)
            gc.free = [h]
            yield h
            r = row
            rr = GR.get(g - 1, {}).get("rowrel", [])
            h1 = dve(lambda e, tb=tb: e.tensor_copy(r["igr"][:, :], tb.t[:, 0:256]), h, rr, n=256)
            h2 = dve(lambda e, tb=tb: e.tensor_copy(r["zr"][:, :], tb.t[:, 256:512]), h, rr, n=256)
            tb.free = [h1, h2]
            h3 = dve(lambda e: e.scalar_tensor_tensor(out=r["er"][:, :], in0=r["zr"][:, :], scalar=-1.0, in1=r["zr"][:, :],
                                                      op0=ALU.mult, op1=ALU.min), h2, n=256)
            yield from tables.get("exp")
            h4 = act(lambda e: e.activation(r["lr"][:, :], r["er"][:, :], ACT.Exp), h3, n=256)
            h4 = act(lambda e: e.activation(r["lr"][:, :], r["lr"][:, :], ACT.Ln, bias=ones[:, 0:1]), h4, c_ones, n=256)
            yield h4
            h5 = dve(lambda e: e.scalar_tensor_tensor(out=r["zr"][:, :], in0=r["zr"][:, :], scalar=0.0, in1=r["lr"][:, :],
                                                      op0=ALU.min, op1=ALU.subtract), h4, n=256)
            yield h5
            h6 = dve(lambda e: e.tensor_tensor_scan(r["csr"][:, :], ones[:, 0:256], r["zr"][:, :], 0.0, ALU.mult, ALU.add), h5, n=512)
            yield h6
            h7 = dve(lambda e: e.tensor_tensor(r["ar"][:, :], r["igr"][:, :], r["csr"][:, :], ALU.subtract), h6, h1, n=256)
            yield h7
            h8 = dve(lambda e: e.tensor_tensor_scan(r["Mr"][:, :], r["ar"][:, :], r["ar"][:, :], -3.0e38, ALU.max, ALU.max), h7, n=512)
            yield h8
            h9 = dve(lambda e: e.tensor_scalar(r["nMr"][:, :], r["Mr"][:, :], -1.0, None, ALU.mult), h8, n=128)
            h10 = dve(lambda e: e.tensor_tensor(r["tr"][:, :], r["csr"][:, :], r["Mr"][:, :], ALU.add), h8, n=256)
            h11 = act(lambda e: e.activation(r["eer"][:, :], r["tr"][:, :], ACT.Exp, scale=-1.0), h10, n=256)
            wf = r["wfr"]
            h12 = act(lambda e: e.activation(wf[:, 0:128], r["ar"][:, 0:128], ACT.Exp, bias=r["nMr"][:, 127:128]), h9)
            h13 = act(lambda e: e.activation(wf[:, 128:256], r["nMr"][:, 128:256], ACT.Exp, bias=r["Mr"][:, 127:128]), h9)
            tables.put()
            yield h9
            m = rowb
            h = dve(lambda e: e.tensor_copy(m["m1"][:, :], r["nMr"][:, :]), h9, n=128)
            yield h
            h = dve(lambda e: e.tensor_tensor(r["r1"][:, :], r["nMr"][:, :], m["m1"][:, :], ALU.subtract), h, n=256)
            yield h
            h = dve(lambda e: e.tensor_copy(m["m2"][:, :], r["r1"][:, :]), h, n=128)
            yield h
            h = dve(lambda e: e.tensor_tensor(r["r2"][:, :], r["r1"][:, :], m["m2"][:, :], ALU.subtract), h, n=256)
            yield h
            hs = dve(lambda e: e.tensor_scalar(m["mr"][:, :], m["m1"][:, :], sel3[:, 0:1], None, ALU.mult), h, c_sel, n=128)
            yield hs
            hs = dve(lambda e: e.scalar_tensor_tensor(out=m["mr"][:, :], in0=m["m2"][:, :], scalar=sel3[:, 1:2], in1=m["mr"][:, :],
                     op0=ALU.mult, op1=ALU.add), hs, n=256)
            yield hs
            hs = dve(lambda e: e.scalar_tensor_tensor(out=m["mr"][:, :], in0=r["r2"][:, :], scalar=sel3[:, 2:3], in1=m["mr"][:, :],
                     op0=ALU.mult, op1=ALU.add), hs, n=256)
            yield hs
            Mx = yield from rMx.get()
            hmx = dve(lambda e: e.tensor_tensor(Mx.t[:, :, :], m["mr"][:, :].unsqueeze(1).to_broadcast([128, 8, S]),
                      hmb[:, :].unsqueeze(2).to_broadcast([128, 8, S]), ALU.mult), hs, c_hm, Mx.free, n=2048)
            srcs = [r["ar"][:, 0:128], r["ar"][:, 128:256], r["eer"][:, 0:128], r["eer"][:, 128:256],
                    wf[:, 0:128], wf[:, 128:256]]
            newcol = []
            cols = yield from rcols.get()
            for i0 in (0, 3):
                tb = yield from TB.get()
                for i in range(i0, i0 + 3):
                    h = tr(tb.t[:, 128 * (i - i0):128 * (i - i0) + 128], srcs[i], ident[:, :], h7, h11, h12, h13, tb.free)
                ht = h
                h = act(lambda e, i0=i0, tb=tb: e.copy(cols.t[:, i0:i0 + 3, :], tb.t[:, 0:384].rearrange("p (i t) -> p i t", i=3)),
                        h, cols.free, n=384)
                tb.free = [h]
                newcol.append(h)
                yield h
            GR[g].update(rowrel=[ht, hmx], cols=cols, newcol=newcol, Mx=Mx, hmx=hmx, users=0, ends=[])

        def expand(b):
            yield from until(lambda: b in BT)
            qx = yield from rqx.get()
            t = BT[b]
            h = []
            for hd in range(4):
                h.append(act(lambda e, hd=hd: e.activation(qx.t[:, :, hd, :], t["qT"].t[:, :, :], ACT.Copy, scale=hm4[:, hd:hd + 1]),
                         t["hqT"], c_h4, qx.free, n=512))
                yield h
            t["qx"], t["hqx"] = qx, h

        def tail(b, c, hO, O, src):
            g, j = b // 4, b % 4
            G_, T_ = GR[g], BT[b]
            cols, newcol, x, x1 = G_["cols"].t, G_["newcol"], T_["x"], T_["x1"]
            jc = slice(32 * j, 32 * j + 8)
            nn = yield from rn.get()
            h0 = dve(lambda e: e.tensor_scalar(nn.t[:, 0, :], cols[:, 2 + c, jc], R32, None, ALU.mult), newcol, nn.free)
            h = dve(lambda e: e.tensor_copy(nn.t[:, 2, :], src[:, :, 32]), hO, nn.free)
            yield h
            h = dve(lambda e: e.scalar_tensor_tensor(out=nn.t[:, 1, :], in0=nn.t[:, 2, :], scalar=-1.0,
                    in1=nn.t[:, 2, :], op0=ALU.mult, op1=ALU.max), h, h0)
            yield h
            h = dve(lambda e: e.tensor_tensor(nn.t[:, 1, :], nn.t[:, 1, :], nn.t[:, 0, :], ALU.max), h)
            yield h
            h = dve(lambda e: e.tensor_scalar(nn.t[:, 1, :], nn.t[:, 1, :], R32 * 1e-6, None, ALU.add), h)
            yield h
            h = dve(lambda e: e.reciprocal(nn.t[:, 2, :], nn.t[:, 1, :]), h)
            yield h
            hh = yield from rh.get()
            h = dve(lambda e: e.tensor_tensor(hh.t[:, :].rearrange("p (h d) -> p h d", h=8), src[:, :, 0:32],
                    nn.t[:, 2, :].unsqueeze(2).to_broadcast([128, 8, 32]), ALU.mult), h, hh.free, n=256)
            nn.free, O.free = [h], [h]
            yield h
            sm, h = yield from norm(lambda c_: hh.t[:, :], None, 1, h, None)
            s = sm.t
            h = dve(lambda e: e.scalar_tensor_tensor(out=hh.t[:, :], in0=hh.t[:, :], scalar=s[:, 0, 6:7], in1=lns[:, :],
                    op0=ALU.subtract, op1=ALU.mult), h, ld_ln, n=256)
            yield h
            hx1 = dve(lambda e: e.scalar_tensor_tensor(out=x1.t[:, c, :], in0=hh.t[:, :], scalar=s[:, 0, 8:9], in1=x.t[:, c, :],
                      op0=ALU.mult, op1=ALU.add), h, T_["lx"], x1.free, n=256)
            sm.free, hh.free = [hx1], [hx1]
            yield hx1
            Ht = yield from rH.get()
            hH = yield from norm(lambda c_: x1.t[:, c, :], lambda c_: Ht.t[:, :], 1, hx1, Ht.free)
            yield hH
            sH = store(dH[256 * b + 128 * c:256 * b + 128 * c + 128, :], Ht.t[:, :], hH)
            tb = yield from TB.get()
            for k in range(2):
                h = tr(tb.t[:, 128 * k:128 * k + 128], Ht.t[:, 128 * k:128 * k + 128], ident[:, :], hH, tb.free)
            Ht.free = [h, sH]
            t0 = 256 * (b % 2) + 128 * c
            Hh, Hl = PR[b // 2]["Hh"], PR[b // 2]["Hl"]
            tv = tb.t[:, 0:256].rearrange("p (k t) -> p k t", k=2)
            yield h
            h1 = act(lambda e: e.copy(Hh.t[:, :, t0:t0 + 128], tv), h, Hh.free, n=256)
            yield h1
            h2 = dve(lambda e: e.tensor_tensor(Hl.t[:, :, t0:t0 + 128], tv, Hh.t[:, :, t0:t0 + 128], ALU.subtract), h1, Hl.free, n=256)
            tb.free = [h2]
            yield h2
            tb = yield from TB.get()
            n = 0
            for a_, b_ in ((Hh, rth), (Hl, rth), (Hh, rtl)):
                for k in range(2):
                    h = mm(tb.t[:, 0:E0], a_.t[:, k, t0:t0 + 128], b_[:, k, :], n == 0, n == 5, h1, h2, rw_w, tb.free)
                    n += 1
            lh = h
            yield from until(lambda: b < 8 or "lgfree" in RT)
            h = act(lambda e: e.copy(lgt[:, c, b % 8, :], tb.t[:, 0:E0]), h, RT.get("lgfree") if b >= 8 else None, n=16)
            tb.free = [h]
            RT.setdefault(b // 8, []).append(h)
            PR[b // 2]["w"] += [h1, h2]
            PR[b // 2]["lh"].append(lh)
            PR[b // 2]["x1w"].append(hx1)
            T_["xend"].append(hx1)
            if len(T_["xend"]) == 2:
                x.free = T_["xend"]
                G_["users"] += 1
                G_["ends"] += T_["xend"]
                if G_["users"] == 4:
                    G_["cols"].free = G_["ends"]

        RT = {}

        def spawn_tail(b, c, hO, O, src):
            T_ = BT[b]
            T_["tail"].append(tail(b, c, hO, O, src))

        def tails(b, c):
            yield from until(lambda: b in BT and len(BT[b].get("tail", [])) > c)
            yield from BT[b]["tail"][c]

        def attend(b):
            g, j = b // 4, b % 4
            yield from until(lambda: "hqx" in BT.get(b, {}) and "cb" in BT[b] and "cols" in GR.get(g, {}))
            T_, G_ = BT[b], GR[g]
            cols, newcol, Mx, hmx = G_["cols"].t, G_["newcol"], G_["Mx"].t, G_["hmx"]
            cb, cT, qT, qx = T_["cb"], T_["cT"], T_["qT"], T_["qx"]
            jc = slice(32 * j, 32 * j + 8)
            T_["xend"], T_["tail"] = [], []
            T_["x1"] = yield from rX1.get()
            if b % 2 == 0:
                Hh = yield from rHh.get()
                Hl = yield from rHl.get()
                PR[b // 2] = dict(Hh=Hh, Hl=Hl, w=[], lh=[], x1w=[])
            V = yield from rV.get()
            hV = act(lambda e: e.copy(V.t[:, :, :, 0:32], cb.t[:, :, :].rearrange("p c (h d) -> p c h d", h=8)), T_["lc"], V.free, n=512)
            wV = yield from rW.get()
            hW = dve(lambda e: e.tensor_tensor(wV.t[:, :, :], V.t[:, 0, :, :],
                     cols[:, 4, jc].unsqueeze(2).to_broadcast([128, 8, 33]), ALU.mult), hV, newcol, wV.free, n=264)
            o1 = {}

            def half(c, k):
                cs_ = slice(128 * c, 128 * c + 128)
                bb = yield from BBk.get()
                mm(bb.t[:, :], identb[:, :], maskb[:, :].unsqueeze(1).to_broadcast([128, 4, 128]), True, False, c_mk, bb.free)
                hb = mm(bb.t[:, :], onesb[32 * j:32 * j + 32, :], Mx[32 * j:32 * j + 32, 4 * k:4 * k + 4, cs_], False, True, hmx, c_ob)
                yield from tables.get("exp")
                Dm = yield from rD.get()
                for hd in range(4):
                    he = act(lambda e, hd=hd: e.activation(Dm.t[:, hd, :], bb.t[:, 128 * hd:128 * hd + 128], ACT.Exp,
                             bias=cols[:, c, 32 * j + 4 * k + hd:32 * j + 4 * k + hd + 1]), hb, newcol, Dm.free)
                tables.put()
                bb.free = [he]
                D_.append((c, k, Dm, he, hb))
                yield hb

            def rest(c, k):
                yield from until(lambda: len(D_) > 2 * c + k)
                _, _, Dm, he, _ = D_[2 * c + k]
                cs_ = slice(128 * c, 128 * c + 128)
                sb_ = yield from SBk.get()
                hs = mm(sb_.t[:, :], cT.t[:, k, cs_], qx.t[:, k, :, cs_], True, True, T_["hqx"], T_["lct"], sb_.free)
                yield [hs, he]
                Cm = yield from rCm.get()
                hC = dve(lambda e: e.tensor_tensor(Cm.t[:, :, :], sb_.t[:, :].rearrange("p (h s) -> p h s", h=4),
                         Dm.t[:, :, :], ALU.mult), he, hs, Cm.free, n=512)
                sb_.free, Dm.free = [hC], [hC]
                yield hC
                if k == 0:
                    o1[c] = yield from OB1.get()
                ob = o1[c]
                for hd in range(4):
                    hh = 4 * k + hd
                    h = mm(ob.t[:, 33 * hh:33 * hh + 33], Cm.t[:, hd, :], V.t[:, c, hh, :], True, True, hC, hV, ob.free)
                Cm.free = [h]
                return hs, h

            D_ = []

            def exps():
                for c in range(2):
                    for k in range(2):
                        yield from half(c, k)

            def sums():
                ob = yield from OB2.get()
                for k in range(2):
                    h = mm(ob.t[:, 132 * k:132 * k + 132], cb.t[:, 0, 128 * k:128 * k + 128],
                           wV.t[:, 4 * k:4 * k + 4, :], True, True, hW, T_["lc"], ob.free)
                wV.free = [h]
                yield h
                KV = yield from rKV.get()
                hKV = dve(lambda e, ob=ob: e.tensor_tensor(KV.t[:, :, :, :],
                          ob.t[:, 0:264].rearrange("p (k h d) -> p k h d", k=2, h=4),
                          hm4[:, :].unsqueeze(1).unsqueeze(3).to_broadcast([128, 2, 4, 33]), ALU.mult), h, KV.free, n=264)
                ob.free = [hKV]
                T_["kvst"] = hKV
                for k in range(2):
                    hs, hO1 = yield from rest(0, k)
                yield hO1
                spawn_tail(b, 0, hO1, o1[0], o1[0].t[:, 0:264].rearrange("p (h d) -> p h d", h=8))
                for k in range(2):
                    hs, hO1 = yield from rest(1, k)
                qx.free = [hs]
                ob = yield from OB2.get()
                for k in range(2):
                    h = mm(ob.t[:, 132 * k:132 * k + 132], qT.t[:, k, 128:256], KV.t[:, k, :, :], True, True, hKV, T_["hqT"], ob.free)
                KV.free, qT.free, V.free = [h], [h, T_["hqx"]], [hO1]
                cb.free, cT.free = [hO1, hKV, hV], [hs]
                yield h
                O = yield from rO.get()
                hO = dve(lambda e: e.tensor_tensor(O.t[:, :, :], ob.t[:, 0:264].rearrange("p (h d) -> p h d", h=8),
                         cols[:, 5, jc].unsqueeze(2).to_broadcast([128, 8, 33]), ALU.mult), h, O.free, newcol, n=264)
                ob.free = [hO]
                yield hO
                hO = dve(lambda e: e.tensor_tensor(O.t[:, :, :], O.t[:, :, :],
                         o1[1].t[:, 0:264].rearrange("p (h d) -> p h d", h=8), ALU.add), hO, hO1, n=264)
                o1[1].free = [hO]
                yield hO
                spawn_tail(b, 1, hO, O, O.t[:, :, :])
                mxu = G_.setdefault("mxu", [])
                mxu.append(D_[-1][4])
                if len(mxu) == 4:
                    G_["Mx"].free = mxu

            T_["sums"] = sums()
            yield from exps()

        def attend_sums(b):
            yield from until(lambda: "sums" in BT.get(b, {}))
            yield from BT[b]["sums"]

        def shared(p):
            yield from until(lambda: len(PR.get(p, {}).get("x1w", [])) == 4)
            R = PR[p]
            hh = yield from rhh.get()
            yield from until(lambda: ws_w)
            hl = yield from rhl.get()
            yield R["w"]
            yield from tables.get("gelu")
            ws, hb, mults = [], None, []
            for f in range(4):
                hb = []
                bks = []
                for m in range(2):
                    bk = yield from FB.get()
                    bks.append(bk)
                    n = 0
                    for a_, b_ in ((wsh, R["Hh"]), (wsh, R["Hl"]), (wsl, R["Hh"])):
                        for k in range(2):
                            h = mm(bk.t[:, :], a_[:, m, 512 * k + 128 * f:512 * k + 128 * f + 128], b_.t[:, k, :],
                                   n == 0, n == 5, R["w"], ws_w, bk.free)
                            n += 1
                        yield h
                    hb.append(h)
                gs = yield from rg.get()
                bg, bu = bks
                hg = act(lambda e, gs=gs, bg=bg: e.activation(gs.t[:, :], bg.t[:, :], ACT.Gelu), hb[0], gs.free, n=512)
                bg.free = [hg]
                if f == 3:
                    tables.put()
                yield [hg, hb[1]]
                gf = yield from rgf.get()
                h = dve(lambda e, gs=gs, bu=bu, gf=gf: e.tensor_tensor(gf.t[:, :], gs.t[:, :], bu.t[:, :], ALU.mult), hg, hb[1], gf.free, n=512)
                gs.free, bu.free = [h], [h]
                h1 = act(lambda e, gf=gf, f=f: e.copy(hh.t[:, f, :], gf.t[:, :]), h, hh.free, n=512)
                h2 = dve(lambda e, gf=gf, f=f: e.tensor_tensor(hl.t[:, f, :], gf.t[:, :], hh.t[:, f, :], ALU.subtract), h1, hl.free, n=512)
                gf.free = [h2]
                ws += [h1, h2]
            R["Hh"].free, R["Hl"].free = [hb[1], R["lh"]], [hb[1], R["lh"]]
            yield ws
            for tt in range(4):
                yb = yield from FB.get()
                n = 0
                for f in range(4):
                    for a_, b_ in ((hh, wsh), (hh, wsl), (hl, wsh)):
                        hy = mm(yb.t[:, 0:256], a_.t[:, f, 128 * tt:128 * tt + 128], b_[:, 2, 256 * f:256 * f + 256],
                                n == 0, n == 11, ws, yb.free)
                        n += 1
                    yield hy
                ys = yield from rys.get()
                xs = BT[2 * p + tt // 2]["x1"]
                h = dve(lambda e, ys=ys, yb=yb, xs=xs, tt=tt: e.tensor_tensor(ys.t[:, :], yb.t[:, 0:256], xs.t[:, tt % 2, :], ALU.add),
                        hy, ys.free, R["x1w"], n=256)
                yb.free = [h]
                if tt % 2:
                    xs.free = [h]
                r0 = 512 * p + 128 * tt
                ys.free = [store(dACC[r0:r0 + 128, :], ys.t[:, :], h)]
            hh.free, hl.free = [hy], [hy]

        def route(G8):
            yield from until(lambda: len(RT.get(G8, [])) == 16 and (G8 == 0 or "rt" in RT))
            yield from tables.get("exp")
            rt = RT.get("rt", [])
            l3 = lgt[:, :, :, :].rearrange("p c b e -> p (c b) e")
            h = dve(lambda e: e.tensor_reduce(sm1[:, :], l3, AX.X, ALU.max), RT[G8], rt, n=256)
            yield h
            h = dve(lambda e: e.tensor_tensor(l3, l3, sm1[:, :].unsqueeze(2).to_broadcast([128, 16, E0]), ALU.subtract), h, n=256)
            h = act(lambda e: e.activation(l3, l3, ACT.Exp), h, n=256)
            tables.put()
            yield h
            h = dve(lambda e: e.tensor_reduce(sm1[:, :], l3, AX.X, ALU.add), h, n=256)
            yield h
            h = dve(lambda e: e.reciprocal(sm1[:, :], sm1[:, :]), h)
            yield h
            h = dve(lambda e: e.tensor_tensor(l3, l3, sm1[:, :].unsqueeze(2).to_broadcast([128, 16, E0]), ALU.mult), h, n=256)
            yield h
            tb = yield from TB.get()
            for c in range(2):
                ht_ = tr(tb.t[:, 128 * c:128 * c + 128], lgt[:, c, :, :], ident[:, :], h, tb.free)
            RT["lgfree"] = [ht_]
            h = act(lambda e, tb=tb: e.copy(sc[:, :], tb.t[:, 0:256]), ht_, rt, n=256)
            tb.free = [h]
            yield h
            for rd in range(4):
                v8, i8 = vals[:, 8 * rd:8 * rd + 8], ix[:, 8 * rd:8 * rd + 8]
                a, bb = (sc, sc2) if rd % 2 == 0 else (sc2, sc)
                h = dve(lambda e, v8=v8, a=a: e.max(v8, a[:, :]), h, rt, n=256)
                yield h
                hi = dve(lambda e, v8=v8, a=a, i8=i8: e.max_index(i8, v8, a[:, :]), h, n=256)
                if rd < 3:
                    h = dve(lambda e, v8=v8, a=a, bb=bb: e.match_replace(bb[:, :], v8, a[:, :], -1.0), h, hi, n=256)
                    yield h
            hb = dve(lambda e: e.tensor_scalar(pint[:, 1:2], pint[:, 0:1], 4, 8, ALU.logical_shift_right, ALU.logical_shift_left), c_hm, c_sel, rt)
            hb = dve(lambda e: e.tensor_scalar(bof[:, :], pint[:, 1:2], float(2048 * G8), None, ALU.add), hb)
            h = dve(lambda e: e.tensor_scalar(ixf[:, :], ix[:, :], bof[:, 0:1], None, ALU.add), hi, hb)
            yield h
            tb = yield from TB.get()
            tr(tb.t[0:32, 0:128], ixf[:, :], ident[:, :], h, tb.free)
            h1 = tr(tb.t[0:32, 128:256], vals[:, :], ident[:, :], h)
            yield h1
            for bl in range(8):
                jj, bg = bl % 4, 2 * G8 + bl // 4
                ps = slice(32 * jj, 32 * jj + 32)
                dve(lambda e, ps=ps, bg=bg, bl=bl: e.tensor_copy(idxJ[ps, bg, :], tb.t[0:32, 16 * bl:16 * bl + 16]), h1)
                h = dve(lambda e, ps=ps, bg=bg, bl=bl: e.tensor_copy(wJ[ps, bg, :], tb.t[0:32, 128 + 16 * bl:128 + 16 * bl + 16]), h1)
            tb.free = [h]
            RT["rt"] = [h, h1]

        def seq(f, items):
            for i in items:
                yield from f(i)

        def tail_seq(c):
            for b in range(B):
                yield from tails(b, c)

        interleave([seq(attend, range(B)), seq(attend_sums, range(B)), tail_seq(0), tail_seq(1),
                    seq(group, range(4)), seq(prep, range(0, B, 2)), seq(prep, range(1, B, 2)), seq(expand, range(B)), seq(rows_, range(B)), later_loads(),
                    seq(route, range(2)), seq(shared, range(8))])
        P.barrier()
        M1.st.close()
        for s in banks:
            s.free = []

        M3 = Mem()
        W1 = M3.sb("W1", [128, E1, 2, H1])
        lw1 = []
        M2 = Mem()
        rraw = [M2.ring(f"wraw{m}", (2, 2, 1)[m], [128, 1024]) for m in range(3)]
        rwh = [M2.ring(f"wh{m}", 2, [128, 1024], FR) for m in range(3)]
        rwl = [M2.ring(f"wl{m}", 2, [128, 1024], FR) for m in range(3)]
        rxe = M2.ring("xe", 2, [128, 4, D])
        rxh = M2.ring("xeh", 2, [128, 2, 512], FR)
        rxl = M2.ring("xel", 2, [128, 2, 512], FR)
        rg = M2.ring("g2", 2, [128, 512])
        rgf = M2.ring("gf", 2, [128, 512])
        rhh = M2.ring("h2h", 2, [128, 4, 512], FR)
        rhl = M2.ring("h2l", 2, [128, 4, 512], FR)
        rye = M2.ring("ye", 2, [128, 4, D])
        GBK = Ring(banks[0:2])
        UBK = Ring(banks[2:4])
        TBK = Ring(banks[4:6])
        YBK = Ring(banks[6:8])
        scat = [None] * 4

        def w_load(x, m):
            raw = rraw[m].next()
            return raw, load(raw.t[:, :].rearrange("p (k f) -> p k f", k=4 if m == 2 else 2),
                             A[("Wg", "Wu", "Wd")[m]][x].rearrange("(k p) f -> p k f", p=128), raw.free)

        def w_split(m, ld_):
            raw, lw = ld_
            wh, wl = rwh[m].next(), rwl[m].next()
            h = act(lambda e: e.copy(wh.t[:, :], raw.t[:, :]), lw, wh.free)
            h2 = dve(lambda e: e.tensor_tensor(wl.t[:, :], raw.t[:, :], wh.t[:, :], ALU.subtract), h, wl.free)
            raw.free = [h, h2]
            return wh, wl, [h, h2]

        def e_gather(x):
            xe = rxe.next()
            return xe, [P.dma("gpsimd", "ga", 8, lambda e, bg=bg: e.indirect_dma_start(
                out=xe.t[:, bg, :], out_offset=None, in_=dH[:, :],
                in_offset=bass.IndirectOffsetOnAxis(ap=idxJ[:, bg, x:x + 1], axis=0)), xe.free) for bg in range(4)]

        def e_xslots(st):
            return st[0], st[1], rxh.next(), rxl.next(), []

        def e_xprep(st, bp):
            xe, ga, xh, xl, out_ = st
            tb = TBK.next()
            for k in range(2):
                h = tr(tb.t[:, 128 * k:128 * k + 128], xe.t[:, bp, 128 * k:128 * k + 128], ident[:, :], ga[bp], tb.free)
            ts_ = slice(128 * bp, 128 * bp + 128)
            tv = tb.t[:, 0:256].rearrange("p (k t) -> p k t", k=2)
            h1 = act(lambda e: e.copy(xh.t[:, :, ts_], tv), h, xh.free)
            h2 = dve(lambda e: e.tensor_tensor(xl.t[:, :, ts_], tv, xh.t[:, :, ts_], ALU.subtract), h1, xl.free)
            tb.free = [h2]
            out_ += [h1, h2]
            if bp == 3:
                xe.free = [h]

        def e_down(x, tt, hh, hl, hw_, w, ye):
            wh, wl, hw = w
            yb = YBK.next()
            n = 0
            for f in range(4):
                for a_, b_ in ((hh, wh), (hh, wl), (hl, wh)):
                    hy = mm(yb.t[:, 0:256], a_.t[:, f, 128 * tt:128 * tt + 128], b_.t[:, 256 * f:256 * f + 256],
                            n == 0, n == 11, hw_, hw, yb.free)
                    n += 1
            h = act(lambda e: e.activation(ye.t[:, tt, :], yb.t[:, 0:256], ACT.Copy, scale=wJ[:, tt, x:x + 1]), hy, ye.free)
            yb.free = [h]
            scat[tt] = P.dma("gpsimd", "sc", 8, lambda e: e.indirect_dma_start(
                out=dACC[:, :], out_offset=bass.IndirectOffsetOnAxis(ap=idxJ[:, tt, x:x + 1], axis=0),
                in_=ye.t[:, tt, :], in_offset=None, compute_op=ALU.add), h, scat[tt])
            return hy, scat[tt]

        gath = [e_gather(0), e_gather(1)]
        wload_ = {(0, m): w_load(0, m) for m in range(3)}
        ws_ = {(0, 0): w_split(0, wload_.pop((0, 0)))}
        xp = e_xslots(gath.pop(0))
        for bp in range(4):
            e_xprep(xp, bp)
        for m in (1, 2):
            ws_[(0, m)] = w_split(m, wload_.pop((0, m)))
        wload_.update({(1, m): w_load(1, m) for m in range(3)})
        prev = None
        for x in range(E0 + 1):
            if x < E0:
                _, _, xh, xl, hx = xp
                hh, hl = rhh.next(), rhl.next()
                hws = []
                if x + 1 < E0:
                    xn = e_xslots(gath.pop(0))
            if prev:
                ye = rye.next()
                dn = []
            for f in range(4):
                if x < E0:
                    fs = lambda k: slice(512 * k + 128 * f, 512 * k + 128 * f + 128)
                    hb = []
                    bks = (GBK.next(), UBK.next())
                    for m, bk in enumerate(bks):
                        wh, wl, hw = ws_[(x, m)]
                        n = 0
                        for a_, b_ in ((wh, xh), (wl, xh), (wh, xl)):
                            for k in range(2):
                                h = mm(bk.t[:, :], a_.t[:, fs(k)], b_.t[:, k, :], n == 0, n == 5, hx, hw, bk.free)
                                n += 1
                        hb.append(h)
                        if f == 3:
                            wh.free, wl.free = [h], [h]
                    gs, gf = rg.next(), rgf.next()
                    bgk, bu = bks
                    h = act(lambda e, gs=gs, bgk=bgk: e.activation(gs.t[:, :], bgk.t[:, :], ACT.Gelu), hb[0], gs.free)
                    bgk.free = [h]
                    h = dve(lambda e, gs=gs, bu=bu, gf=gf: e.tensor_tensor(gf.t[:, :], gs.t[:, :], bu.t[:, :], ALU.mult),
                            h, hb[1], gf.free)
                    gs.free, bu.free = [h], [h]
                    h1 = act(lambda e, gf=gf, f=f, hh=hh: e.copy(hh.t[:, f, :], gf.t[:, :]), h, hh.free)
                    h2 = dve(lambda e, gf=gf, f=f, hh=hh, hl=hl: e.tensor_tensor(hl.t[:, f, :], gf.t[:, :], hh.t[:, f, :], ALU.subtract),
                             h1, hl.free)
                    gf.free = [h2]
                    hws += [h1, h2]
                if prev:
                    dn.append(e_down(x - 1, f, *prev[0:2], prev[2], prev[3], ye))
                if x + 1 < E0:
                    for bp in ((0,), (1,), (2, 3), ())[f]:
                        e_xprep(xn, bp)
                    if f < 2:
                        ws_[(x + 1, f)] = w_split(f, wload_.pop((x + 1, f)))
                        if x + 2 < E0:
                            wload_[(x + 2, f)] = w_load(x + 2, f)
                    if f == 2 and x + 2 < E0:
                        gath.append(e_gather(x + 2))
                    if f == 3 and x % 2 == 0:
                        lw1.append(P.dma("sync", "lw", 4, lambda e, x=x: e.dma_start(
                            W1[:, x // 2, :, :], A["W1"][x // 2].rearrange("(k p) f -> p k f", p=128))))
            if prev:
                prev[0].free, prev[1].free = [dn[-1][0]], [dn[-1][0]]
                prev[3][0].free, prev[3][1].free = [dn[-1][0]], [dn[-1][0]]
                ye.free = [d[1] for d in dn]
            if x < E0:
                xh.free, xl.free = [hb[1]], [hb[1]]
                prev = (hh, hl, hws, ws_[(x, 2)])
                if x + 1 < E0:
                    ws_[(x + 1, 2)] = w_split(2, wload_.pop((x + 1, 2)))
                    if x + 2 < E0:
                        wload_[(x + 2, 2)] = w_load(x + 2, 2)
                    xp = xn
        P.barrier()
        M2.st.close()
        for s in banks:
            s.free = []

        M6 = Mem()
        W2 = M6.sb("W2", [128, E1, 8, D])
        te = M6.sb("te", [128, 2, TILES], I32)
        gam = M6.sb("gam", [128, D])
        bet = M6.sb("bet", [128, D])
        PRE = 2
        x3p = [Slot(M6.sb(f"x3p{b}", [128, 2, D])) for b in range(PRE)]
        M4 = Mem()
        small = M4.ring("sma", 8, [128, 2, 16])
        w1r = M4.sb("w1r", [128, 2, E1])
        bgr = M4.sb("bgr", [128, E1])
        b2sb = M4.sb("b2sb", [E1, D])
        ld_wr = load2(w1r[:, :, :], A["L1g"].rearrange("(k p) e -> p k e", p=128))
        ld_bg = load2(bgr[:, :], A["bg"].rearrange("(a n) -> a n", a=1).to_broadcast([128, E1]))
        ld_b2 = load2(b2sb[:, :], A["b2"])
        zer = M4.sb("zer", [128, 2, D])
        SLP = (E1 * REG + TS) // 128
        sli = M4.sb("sli", [128, SLP], I32)
        slz = M4.sb("slz", [128, SLP, 2])
        io8 = M4.sb("io8", [128, 8], I32)
        io8f = M4.sb("io8f", [128, 8])
        tok = M4.sb("tok", [128, NT], I32)
        run = M4.sb("run", [128, 2, 8])
        rx = M4.ring("x2", 5, [128, 2, D])
        rct = M4.ring("c3T", 3, [128, 2, S])
        rq = M4.ring("Q3", 4, [128, 2, D])
        rs = M4.ring("S3", 3, [128, 3, 128])
        rz = M4.ring("z3", 6, [128, 2, D])
        ren = M4.ring("en", 3, [128, 4, 2, 2])
        rzb = M4.ring("zb", 2, [128, 2, D])
        rzT = M4.ring("zT", 2, [128, 2, S])
        rlg = M4.ring("lg", 3, [128, 4, 8])
        rv8 = M4.ring("v8", 2, [128, 4, 8])
        ri8 = M4.ring("i8", 2, [128, 4, 8], U32)
        rrt = M4.ring("rt", 2, [128, 5, 4, 8])
        rpo = M4.ring("po", 3, [128, 4, 2], U32)
        rcb = M4.ring("cbT", 2, [8, 512])
        mask3 = M4.sb("mask3", [128, 3, 128])
        before = M4.sb("before", [128, NT + 1, 8])
        PB = Ring(banks)

        h0 = pool(lambda e: e.memset(zer[:, :, :], 0.0))
        hs0 = pool(lambda e: e.memset(slz[:, :, :], 0.0), n=100)
        hs1 = pool(lambda e: e.iota(sli[:, :], [[1, SLP]], base=0, channel_multiplier=SLP), n=100)
        hs1 = dve(lambda e: e.tensor_scalar(sli[:, :], sli[:, :], TS - 1, None, ALU.bitwise_and), hs1, n=SLP)
        hs1 = dve(lambda e: e.tensor_scalar(slz[:, :, 1:2].bitcast(I32), sli[:, :].unsqueeze(2), N, None, ALU.add), hs0, hs1, n=SLP)
        slinit = store2(dSL.rearrange("(p r) e -> p r e", p=128), slz[:, :, :], hs1)
        h1 = pool(lambda e: e.iota(io8[:, :], [[1, 8]], base=0, channel_multiplier=0))
        hio = dve(lambda e: e.tensor_copy(io8f[:, :], io8[:, :]), h1)
        htok = pool(lambda e: e.iota(tok[:, :], [[128, NT]], base=0, channel_multiplier=1))
        hmask = [dve(lambda e, m=m, t=t: e.tensor_copy(mask3[:, m, :], t[:, 0:128])) for m, t in ((0, tri), (1, ones), (2, tri))]
        sums = [dve(lambda e: e.memset(before[:, 0, :], 0.0))]
        for d_ in (dOUT, dZ):
            store2(d_[N:N + TS, :].rearrange("(c p) d -> p c d", p=128), zer[:, :, :], h0)
        ti = M4.sb("ti", [128, TILES], I32)
        hti = pool(lambda e: e.iota(ti[:, :], [[1, TILES]], base=0, channel_multiplier=0))
        xsd = []

        def norm3(src, dst, after, dst_free):
            sm = yield from small.get()
            s = sm.t
            h = [dve(lambda e, c=c: e.bn_stats(s[:, c, 0:6], src[:, c, 0:D]), after, sm.free, n=D) for c in range(2)]
            yield h
            h = [dve(lambda e, c=c: e.bn_aggr(s[:, c, 6:8], s[:, c, 0:6]), h) for c in range(2)]
            yield h
            h = dve(lambda e: e.tensor_scalar(s[:, :, 9:10], s[:, :, 7:8], EPS, None, ALU.add), h)
            yield h
            h = pool(lambda e: e.tensor_tensor(s[:, :, 8:9], s[:, :, 9:10],
                     mhalf[:, :].unsqueeze(1).to_broadcast([128, 2, 1]), ALU.pow), h, c_mh)
            yield h
            h2 = dve(lambda e: e.scalar_tensor_tensor(out=s[:, :, 10:11], in0=s[:, :, 6:7], scalar=-1.0, in1=s[:, :, 8:9],
                     op0=ALU.mult, op1=ALU.mult), h)
            yield h2
            h = [act(lambda e, c=c: e.activation(dst[:, c, 0:D], src[:, c, 0:D], ACT.Identity, scale=s[:, c, 8:9],
                     bias=s[:, c, 10:11]), h, h2, dst_free, n=2 * D) for c in range(2)]
            sm.free = [h]
            return h

        X3, Z3 = {}, {}

        def loads3(b):
            rows = slice(256 * b, 256 * b + 256)
            x = yield from rx.get()
            ct = yield from rct.get()
            lct = load(ct.t[:, :, :], A["ctxT"][:, rows].rearrange("(k p) t -> p k t", p=128), ct.free)
            lx = load(x.t[:, :, :], dACC[rows, :].rearrange("(c p) d -> p c d", p=128), x.free)
            X3[b] = x, ct, lx, lct

        def layer1(b):
            rows = slice(256 * b, 256 * b + 256)
            yield from until(lambda: b in X3)
            x, ct, lx, lct = X3.pop(b)
            yield lct
            sb_ = yield from PB.get()
            for k in range(2):
                h = mm(sb_.t[:, 0:256], ct.t[:, k, 0:128], ct.t[:, k, :], k == 0, k == 1, lct, sb_.free)
            for k in range(2):
                h = mm(sb_.t[:, 256:384], ct.t[:, k, 128:256], ct.t[:, k, 128:256], k == 0, k == 1)
            ct.free = [h]
            yield h
            s3 = yield from rs.get()
            h3 = dve(lambda e: e.tensor_tensor(s3.t[:, :, :], sb_.t[:, 0:384].rearrange("p (m s) -> p m s", m=3),
                     mask3[:, :, :], ALU.mult), h, s3.free, hmask, n=384)
            sb_.free = [h3]
            q = yield from rq.get()
            hq = yield from norm3(x.t, q.t, lx, q.free)
            yield hq
            qb = yield from PB.get()
            mm(qb.t[:, 0:256], s3.t[:, 0, :], q.t[:, 0, :], True, False, hq, h3, qb.free)
            mm(qb.t[:, 0:256], ident[:, :], q.t[:, 0, :], False, True)
            mm(qb.t[:, 256:512], s3.t[:, 1, :], q.t[:, 0, :], True, False)
            mm(qb.t[:, 256:512], s3.t[:, 2, :], q.t[:, 1, :], False, False)
            h = mm(qb.t[:, 256:512], ident[:, :], q.t[:, 1, :], False, True)
            s3.free, q.free = [h], [h]
            yield h
            h4 = dve(lambda e: e.tensor_tensor(x.t[:, :, :], x.t[:, :, :],
                     qb.t[:, :].rearrange("p (c d) -> p c d", c=2), ALU.add), h, hq, n=512)
            qb.free = [h4]
            yield h4
            s1 = store(dX3[rows, :].rearrange("(c p) d -> p c d", p=128), x.t[:, :, :], h4)
            z = yield from rz.get()
            hz = yield from norm3(x.t, z.t, h4, z.free)
            x.free = [s1, hz]
            yield hz
            tb = yield from PB.get()
            tv = tb.t[:, :].rearrange("p (k t) -> p k t", k=2)
            for k in range(2):
                for c in range(2):
                    h = tr(tv[:, k, 128 * c:128 * c + 128], z.t[:, c, 128 * k:128 * k + 128], ident[:, :], hz, tb.free)
            yield h
            zT = yield from rzT.get()
            hzt = act(lambda e: e.copy(zT.t[:, :, :], tv), h, zT.free, n=512)
            tb.free = [hzt]
            yield hzt
            lb = yield from PB.get()
            for c in range(2):
                for k in range(2):
                    hl = mm(lb.t[:, 8 * c:8 * c + 8], zT.t[:, k, 128 * c:128 * c + 128], w1r[:, k, :], k == 0, k == 1,
                            hzt, ld_wr, lb.free)
            zT.free = [hl]
            yield hl
            if ("lg", b // 2) not in Z3:
                Z3[("lg", b // 2)] = yield from rlg.get()
            lg = Z3[("lg", b // 2)]
            h = dve(lambda e: e.tensor_tensor(lg.t[:, 2 * (b % 2):2 * (b % 2) + 2, :], lb.t[:, 0:16].rearrange("p (c x) -> p c x", c=2),
                    bgr[:, :].unsqueeze(1).to_broadcast([128, 2, 8]), ALU.add), hl, ld_bg, lg.free, n=16)
            lb.free = [h]
            Z3[b] = z, hz, h

        def router1(p):
            yield from until(lambda: 2 * p in Z3 and 2 * p + 1 in Z3)
            lg = Z3[("lg", p)]
            zs, hz, hlg = zip(Z3[2 * p], Z3[2 * p + 1])
            v8 = yield from rv8.get()
            i8 = yield from ri8.get()
            rt = yield from rrt.get()
            i8f, oh, prd, cmb = (rt.t[:, m, :, :] for m in (0, slice(1, 3), 3, 4))
            yield hlg
            hm = [dve(lambda e, c=c: e.max(v8.t[:, c, :], lg.t[:, c, :]), hlg, v8.free) for c in range(4)]
            yield hm
            hi = [dve(lambda e, c=c: e.max_index(i8.t[:, c, :], v8.t[:, c, :], lg.t[:, c, :]), hm, i8.free) for c in range(4)]
            hd = dve(lambda e: e.tensor_tensor(i8f[:, :, 2:3], v8.t[:, :, 1:2], v8.t[:, :, 0:1], ALU.subtract), hm, rt.free)
            lg.free = hi
            yield hi
            h = dve(lambda e: e.tensor_copy(i8f[:, :, 0:2], i8.t[:, :, 0:2]), hi, hd)
            v8.free, i8.free = [hd, hi], [h]
            he = act(lambda e: e.activation(i8f[:, :, 3:4], i8f[:, :, 2:3], ACT.Exp), h, n=8)
            yield h
            ho = [dve(lambda e, k=k: e.tensor_tensor(oh[:, k, :, :], i8f[:, :, k:k + 1].to_broadcast([128, 4, 8]),
                  io8f[:, :].unsqueeze(1).to_broadcast([128, 4, 8]), ALU.is_equal), h, hio, n=32) for k in range(2)]
            yield ho
            hk = dve(lambda e: e.tensor_tensor(prd[:, :, :], oh[:, 0, :, :], oh[:, 1, :, :], ALU.add), ho, n=32)
            yield hk
            yield from until(lambda: len(sums) == 4 * p + 1)
            for i in range(4 * p, 4 * p + 4):
                h = dve(lambda e, i=i: e.tensor_tensor(before[:, i + 1, :], before[:, i, :], prd[:, i - 4 * p, :], ALU.add),
                        hk, sums[-1])
                sums.append(h)
                yield h
            rb = yield from PB.get()
            mm(rb.t[:, 0:32], stri[:, :], prd[:, :, :], True, False, hk, rb.free)
            hr = mm(rb.t[:, 0:32], ones[:, 0:128], before[:, 4 * p:4 * p + 4, :], False, True, h)
            yield he
            h = dve(lambda e: e.tensor_scalar(i8f[:, :, 4:5], i8f[:, :, 3:4], 1.0, None, ALU.add), he)
            yield h
            h = dve(lambda e: e.reciprocal(i8f[:, :, 4:5], i8f[:, :, 4:5]), h)
            yield h
            hw = dve(lambda e: e.tensor_tensor(i8f[:, :, 5:6], i8f[:, :, 3:4], i8f[:, :, 4:5], ALU.mult), h)
            yield [hw, hr]
            h = dve(lambda e: e.tensor_tensor(cmb[:, :, :], oh[:, 0, :, :], i8f[:, :, 4:5].to_broadcast([128, 4, 8]), ALU.mult), hw, n=32)
            h2 = dve(lambda e: e.tensor_tensor(prd[:, :, :], oh[:, 1, :, :], i8f[:, :, 5:6].to_broadcast([128, 4, 8]), ALU.mult), hw, hr, n=32)
            yield h2
            hc = dve(lambda e: e.tensor_tensor(cmb[:, :, :], cmb[:, :, :], prd[:, :, :], ALU.add), h, h2, n=32)
            yield hc
            cbk = yield from PB.get()
            for c in range(4):
                hct = tr(cbk.t[0:8, 128 * c:128 * c + 128], cmb[:, c, :], ident[:, :], hc, cbk.free)
            cb = yield from rcb.get()
            hcb = act(lambda e: e.copy(cb.t[:, :], cbk.t[0:8, :]), hct, cb.free, n=512)
            cbk.free = [hcb]
            h = dve(lambda e: e.scalar_tensor_tensor(out=prd[:, :, :], in0=io8f[:, :].unsqueeze(1).to_broadcast([128, 4, 8]),
                    scalar=float(REG), in1=rb.t[:, 0:32].rearrange("p (c x) -> p c x", c=4), op0=ALU.mult, op1=ALU.add), hr, hc, n=32)
            rb.free = [h]
            yield h
            h = dve(lambda e: e.tensor_tensor(oh[:, :, :, :], oh[:, :, :, :], prd[:, :, :].unsqueeze(1).to_broadcast([128, 2, 4, 8]),
                    ALU.mult), h, n=64)
            yield h
            h = [dve(lambda e, k=k: e.tensor_reduce(i8f[:, :, 6 + k], oh[:, k, :, :], AX.X, ALU.add), h, n=32) for k in range(2)]
            yield h
            po = yield from rpo.get()
            hp = dve(lambda e: e.tensor_copy(po.t[:, :, :], i8f[:, :, 6:8]), h, po.free)
            yield hp
            en = yield from ren.get()
            hws = [dve(lambda e: e.tensor_copy(en.t[:, :, :, 0], i8f[:, :, 4:6]), hw, en.free),
                   dve(lambda e: e.tensor_copy(en.t[:, :, :, 1].bitcast(I32), tok[:, 4 * p:4 * p + 4].unsqueeze(2).to_broadcast([128, 4, 2])),
                       htok, en.free)]
            yield hws
            SC[p] = en, po, hws, hp
            for j in range(2):
                z, b = zs[j], 2 * p + j
                sz = store(dZ[256 * b:256 * b + 256, :].rearrange("(c p) d -> p c d", p=128), z.t[:, :, :], hz)
                bb = yield from PB.get()
                for c in range(2):
                    hb = mm(bb.t[:, 256 * c:256 * c + 256], cb.t[:, 256 * j + 128 * c:256 * j + 128 * c + 128], b2sb[:, :], True, True,
                            hcb, ld_b2, bb.free)
                yield hb
                zb = yield from rzb.get()
                h = dve(lambda e, z=z, zb=zb, bb=bb: e.tensor_tensor(zb.t[:, :, :], z.t[:, :, 0:D],
                        bb.t[:, :].rearrange("p (c d) -> p c d", c=2), ALU.add), hb, zb.free, n=512)
                bb.free = [h]
                z.free = [sz, h]
                zb.free = [store(dOUT[256 * b:256 * b + 256, :].rearrange("(c p) d -> p c d", p=128), zb.t[:, :, :], h)]
            rt.free, cb.free = [hws, h], [hb]

        SC = {}

        def scatter3(p):
            yield from until(lambda: p in SC)
            en, po, hws, hp = SC[p]
            yield [hws, hp]
            ends = []
            for c in range(4):
                for k in range(2):
                    ends.append(P.dma("gpsimd", "sx", 8, lambda e, c=c, k=k: e.indirect_dma_start(
                        out=dSL[:, :], out_offset=bass.IndirectOffsetOnAxis(ap=po.t[:, c, k:k + 1], axis=0),
                        in_=en.t[:, c, k, :], in_offset=None), hws, hp, slinit))
                    yield float(P.time["gpsimd"])
            xsd.extend(ends)
            po.free, en.free = [ends], [ends]

        def wload():
            for x in range(E1):
                yield from until(lambda: len(Z3) > 2 * x + 1)
                lw1.append(P.dma("sync", "lw", 4, lambda e, x=x: e.dma_start(
                    W2[:, x, :, :], A["W2"][x].rearrange("(k p) f -> p k f", p=128))))

        NW = 4
        interleave([seq(loads3, range(B))] + [seq(layer1, range(w, B, NW)) for w in range(NW)]
                   + [seq(router1, range(w, B // 2, 2)) for w in range(2)] + [wload(), seq(scatter3, range(B // 2))])
        rb = PB.next()
        hr = mm(rb.t[:, 0:8], ones[:, 0:128], before[:, NT, :], True, True, sums[-1], rb.free)
        hrun = dve(lambda e: e.tensor_copy(run[:, 0, :], rb.t[:, 0:8]), hr)
        rb.free = [hrun]
        M5 = Mem()
        cn = M5.sb("cn", [128, 6, 8])
        cni = M5.sb("cni", [128, 8], I32)
        tf = M5.sb("tf", [128, 5, TILES])
        cmpt = M5.sb("cmpt", [128, TILES, 8])
        cnt = run[:, 0, :]
        h2 = dve(lambda e: e.tensor_scalar(cni[:, :], cnt, float(TS - 1), None, ALU.add), hrun)
        h2 = dve(lambda e: e.tensor_scalar(cni[:, :], cni[:, :], 8, None, ALU.arith_shift_right), h2)
        h2 = dve(lambda e: e.tensor_copy(cn[:, 0, :], cni[:, :]), h2)
        h2 = dve(lambda e: e.tensor_tensor_scan(cn[:, 1, :], ones[:, 0:8], cn[:, 0, :], 0.0, ALU.mult, ALU.add), h2)
        h = dve(lambda e: e.tensor_copy(tf[:, 0, :], ti[:, :]), hti)
        h = dve(lambda e: e.tensor_tensor(cmpt[:, :, :], tf[:, 0, :].unsqueeze(2).to_broadcast([128, TILES, 8]),
                cn[:, 1, :].unsqueeze(1).to_broadcast([128, TILES, 8]), ALU.is_ge), h, h2)
        h = dve(lambda e: e.tensor_reduce(tf[:, 1, :], cmpt[:, :, :], AX.X, ALU.add), h)
        h = dve(lambda e: e.tensor_tensor(cmpt[:, :, :], cmpt[:, :, :], cn[:, 0, :].unsqueeze(1).to_broadcast([128, TILES, 8]), ALU.mult), h)
        h = dve(lambda e: e.tensor_reduce(tf[:, 2, :], cmpt[:, :, :], AX.X, ALU.add), h)
        h = dve(lambda e: e.tensor_tensor(tf[:, 2, :], tf[:, 0, :], tf[:, 2, :], ALU.subtract), h)
        h = dve(lambda e: e.tensor_scalar(tf[:, 3, :], tf[:, 1, :], float(REG // TS), None, ALU.mult), h)
        h = dve(lambda e: e.tensor_tensor(tf[:, 2, :], tf[:, 2, :], tf[:, 3, :], ALU.add), h)
        h = dve(lambda e: e.tensor_scalar(tf[:, 4, :], tf[:, 1, :], 8.0, None, ALU.is_lt), h)
        h = dve(lambda e: e.tensor_tensor(te[:, 0, :], tf[:, 1, :], tf[:, 4, :], ALU.mult), h)
        h = dve(lambda e: e.tensor_scalar(tf[:, 3, :], tf[:, 4, :], -float(E1 * REG // TS), float(E1 * REG // TS), ALU.mult, ALU.add), h)
        h = dve(lambda e: e.tensor_tensor(tf[:, 2, :], tf[:, 2, :], tf[:, 4, :], ALU.mult), h)
        h = dve(lambda e: e.tensor_tensor(te[:, 1, :], tf[:, 2, :], tf[:, 3, :], ALU.add), h)
        P.barrier()
        M5.st.close()
        M4.st.close()
        for s in banks:
            s.free = []

        M7 = Mem()
        rxs = M7.ring("xs", 3, [128, 2, D])
        res_ = M7.ring("es", 6, [128, 2, 2])
        rxh = M7.ring("xh", 2, [128, 2, TS], FR)
        rxl = M7.ring("xl", 2, [128, 2, TS], FR)
        rgl = M7.ring("gl", 3, [128, 2, TS])
        rhh = M7.ring("hh", 2, [128, 4, TS], FR)
        rhl = M7.ring("hl", 2, [128, 4, TS], FR)
        rwh = M7.ring("wh", 3, [128, 1024], FR)
        rwl = M7.ring("wl", 3, [128, 1024], FR)
        rb1 = M7.ring("b1c", 6, [128, 8])
        ry = M7.ring("y1", 2, [128, 2, D])
        w1f = W1[:, :, :, :].rearrange("p x k f -> p (x k) f")
        w2f = W2[:, :, :, :].rearrange("p x k f -> p (x k f)")
        Tb = banks[0]
        Ab = Ring(banks[1:4])
        Yb = banks[4:8]
        regs = {}

        def expert(e, name, i):
            if regs.get(name, (None, None))[0] != i:
                regs[name] = (i, e.value_load(te[0:1, 0, i:i + 1], min_val=0, max_val=E1 - 1))
            return regs[name][1]

        def part(i, kind, half):
            wh, wl = rwh.next(), rwl.next()
            if kind == 1:
                def src(r):
                    return w1f[:, bass.ds(r * 2, 2), 512 * half:512 * half + 512]
                vh, vl = (w.t[:, :].rearrange("p (k f) -> p k f", k=2) for w in (wh, wl))
            else:
                def src(r):
                    return w2f[:, bass.ds(r * 2048 + 1024 * half, 1024)]
                vh, vl = wh.t[:, :], wl.t[:, :]
            who, name = HI[(kind, half)]
            h = who(lambda e: (e.copy if name == "a" else e.tensor_copy)(vh, src(expert(e, name, i))), wh.free)
            h2 = dve(lambda e: e.tensor_tensor(vl, src(expert(e, "v", i)), vh, ALU.subtract), h, wl.free)
            return wh, wl, vh, vl, [h, h2]

        HI = {(1, 0): (act, "a"), (1, 1): (act, "a"), (2, 0): (act, "a"), (2, 1): (dve, "v")}

        def s_load(i):
            es, b1c = res_.next(), rb1.next()

            def ldx(e):
                r = e.value_load(te[0:1, 1, i:i + 1], min_val=0, max_val=E1 * REG // TS)
                return e.dma_start(es.t[:, :, :], dSL.rearrange("(n c p) d -> n p c d", p=128, c=2)[bass.ds(r, 1), :, :, :]
                                   .rearrange("a p c d -> (a p) c d"))

            def ldb1(e):
                r = e.value_load(te[0:1, 0, i:i + 1], min_val=0, max_val=E1 - 1)
                return e.dma_start(b1c.t[:, :], A["b1"][bass.ds(r, 1), :, :].rearrange("a p c -> (a p) c"))
            return es, b1c, P.dma("sync", "lx", 4, ldx, es.free), P.dma("sync", "lb", 4, ldb1, b1c.free)

        def x_load(st):
            es, b1c, ls, lb = st
            xs = rxs.next()
            lx = [P.dma("gpsimd", "gz", 6, lambda e, c=c: e.indirect_dma_start(
                out=xs.t[:, c, :], out_offset=None, in_=dZ[:, :],
                in_offset=bass.IndirectOffsetOnAxis(ap=es.t[:, c, 1:2].bitcast(U32), axis=0)), ls, xs.free) for c in range(2)]
            return xs, es, b1c, lx, lb

        def x_prep(st):
            xs, es, b1c, lx, lb = st
            Tb.take()
            tv = Tb.t[:, :].rearrange("p (k t) -> p k t", k=2)
            for k in range(2):
                for c in range(2):
                    h = tr(tv[:, k, 128 * c:128 * c + 128], xs.t[:, c, 128 * k:128 * k + 128], ident[:, :], lx, Tb.free)
            xh, xl = rxh.next(), rxl.next()
            h1 = act(lambda e: e.copy(xh.t[:, :, :], tv), h, xh.free)
            h2 = dve(lambda e: e.tensor_tensor(xl.t[:, :, :], tv, xh.t[:, :, :], ALU.subtract), h1, xl.free)
            Tb.free, xs.free = [h2], [h]
            return xh, xl, b1c, lb, [h1, h2], es

        def up(i, x, half, w):
            xh, xl, b1c, lb, hx, es = x
            wh, wl, vh, vl, hw = w
            hh, hl = rhh.next(), rhl.next()
            out_ = []
            for q in range(2):
                ab = Ab.next()
                for c in range(2):
                    fs = slice(128 * (2 * q + c), 128 * (2 * q + c) + 128)
                    o = ab.t[:, TS * c:TS * c + TS]
                    n = 0
                    for ww, xx in ((vh, xh), (vh, xl), (vl, xh)):
                        for k in range(2):
                            h = mm(o, ww[:, k, fs], xx.t[:, k, :], n == 0, n == 5, hx, hw, ab.free)
                            n += 1
                gl = rgl.next()
                for c in range(2):
                    cc = 4 * half + 2 * q + c
                    ha = act(lambda e, c=c, cc=cc, gl=gl, ab=ab: e.activation(gl.t[:, c, :], ab.t[:, TS * c:TS * c + TS],
                             ACT.Gelu, bias=b1c.t[:, cc:cc + 1]), h, lb, gl.free)
                ab.free = [ha]
                qs = slice(2 * q, 2 * q + 2)
                h1 = act(lambda e, qs=qs, gl=gl: e.copy(hh.t[:, qs, :], gl.t[:, :, :]), ha, hh.free)
                h2 = dve(lambda e, qs=qs, gl=gl: e.tensor_tensor(hl.t[:, qs, :], gl.t[:, :, :], hh.t[:, qs, :], ALU.subtract),
                         h1, hl.free)
                gl.free = [h2]
                out_ += [h1, h2]
            wh.free, wl.free = [h], [h]
            if half == 1:
                xh.free, xl.free, b1c.free = [h], [h], [ha]
            return hh, hl, out_, es

        last = [None]

        def down(i, half, hp, w):
            hh, hl, hw_, es = hp
            wh, wl, vh, vl, hw = w
            for tt in range(2):
                yb = Yb[2 * (i % 2) + tt]
                if half == 0:
                    yb.take()
                n = 0
                for c in range(4):
                    for a_, b_ in ((hh, vh), (hh, vl), (hl, vh)):
                        h = mm(yb.t[:, 0:256], a_.t[:, c, 128 * tt:128 * tt + 128], b_[:, 256 * c:256 * c + 256],
                               half == 0 and n == 0, half == 1 and n == 11, hw_, hw, yb.free)
                        n += 1
            hh.free, hl.free, wh.free, wl.free = [h], [h], [h], [h]
            if half == 1:
                y = ry.next()
                sc = []
                for tt in range(2):
                    yb = Yb[2 * (i % 2) + tt]
                    h2 = dve(lambda e, tt=tt, yb=yb: e.tensor_scalar(y.t[:, tt, :], yb.t[:, 0:256], es.t[:, tt, 0:1], None,
                             ALU.mult), h, y.free)
                    yb.free = [h2]
                    sc.append(P.dma("gpsimd", "sy", 4, lambda e, tt=tt: e.indirect_dma_start(
                        out=dOUT[:, :], out_offset=bass.IndirectOffsetOnAxis(ap=es.t[:, tt, 1:2].bitcast(U32), axis=0),
                        in_=y.t[:, tt, :], in_offset=None, compute_op=ALU.add), h2, last[0]))
                y.free = last[0] = sc
                es.free = sc

        units = []
        for i in range(TILES):
            units.append((i, 1, 0))
            if i:
                units.append((i - 1, 2, 1))
            units += [(i, 1, 1), (i, 2, 0)]
        units.append((TILES - 1, 2, 1))
        wq_ = [part(*units[n]) for n in range(2)]
        sl_ = [s_load(i) for i in range(4)]
        xl_ = [x_load(s) for s in sl_[0:3]]
        x = x_prep(xl_.pop(0))
        hp = {}
        for n, (i, kind, half) in enumerate(units):
            if n + 2 < len(units):
                wq_.append(part(*units[n + 2]))
            if kind == 1:
                hp[(i, half)] = up(i, x, half, wq_[n])
                if half == 0:
                    xnext = x_prep(xl_.pop(0)) if i + 1 < TILES else None
                else:
                    x = xnext
            else:
                down(i, half, hp.pop((i, half)), wq_[n])
                if half == 1 and i + 3 < TILES:
                    xl_.append(x_load(sl_[i + 3]))
                    if i + 4 < TILES:
                        sl_.append(s_load(i + 4))
            wq_[n] = None
        ld_ga = load(gam[:, :], A["gamma"].rearrange("(a n) -> a n", a=1).to_broadcast([128, D]))
        ld_be = load(bet[:, :], A["beta"].rearrange("(a n) -> a n", a=1).to_broadcast([128, D]))
        for b in range(PRE):
            x3p[b].free = [load(x3p[b].t[:, :, :], dX3[256 * b:256 * b + 256, :].rearrange("(c p) d -> p c d", p=128))]
        P.barrier()
        M7.st.close()
        for s in banks:
            s.free = []

        M8 = Mem()
        small = M8.ring("smc", 8, [128, 2, 16])
        rz = M8.ring("zc", 12, [128, 2, D])
        rx = M8.ring("xc", 8, [128, 2, D])
        rn = M8.ring("nc", 5, [128, 2, D])
        ry = M8.ring("yc", 4, [128, 2, D])
        LD = {}

        def last_loads():
            for b in range(B):
                rows = slice(256 * b, 256 * b + 256)
                z = yield from rz.get()
                lz = load(z.t[:, :, :], dOUT[rows, :].rearrange("(c p) d -> p c d", p=128), z.free)
                if b < PRE:
                    x, lx = x3p[b], x3p[b].free
                else:
                    x = yield from rx.get()
                    lx = load(x.t[:, :, :], dX3[rows, :].rearrange("(c p) d -> p c d", p=128), x.free)
                LD[b] = z, x, lz, lx

        def last_norm(b):
            rows = slice(256 * b, 256 * b + 256)
            yield from until(lambda: b in LD)
            z, x, lz, lx = LD[b]
            n = yield from rn.get()
            yield lz
            hn = yield from norm3(z.t, n.t, lz, n.free)
            z.free = [hn]
            hb = pool(lambda e: e.tensor_tensor(x.t[:, :, :], x.t[:, :, :], bet[:, :].unsqueeze(1).to_broadcast([128, 2, D]), ALU.add),
                      lx, ld_be, n=300)
            yield hn
            y = yield from ry.get()
            h = dve(lambda e: e.tensor_tensor(n.t[:, :, :], n.t[:, :, :], gam[:, :].unsqueeze(1).to_broadcast([128, 2, D]), ALU.mult),
                    hn, ld_ga, n=512)
            yield h
            h = dve(lambda e: e.tensor_tensor(y.t[:, :, :], n.t[:, :, :], x.t[:, :, :], ALU.add), h, hb, y.free, n=512)
            n.free, x.free = [h], [h]
            y.free = [P.dma("sync", "out", 4, lambda e: e.dma_start(out[rows, :].rearrange("(c p) d -> p c d", p=128), y.t[:, :, :]), h)]

        interleave([last_loads()] + [seq(last_norm, range(w, B, 5)) for w in range(5)])
        M8.st.close()
        M6.st.close()
        M3.st.close()
        P.barrier()
        block = ctx.enter_context(nc.Block())
        P.emit(block)


STOP = 99


def kernel(**inputs):
    import concourse.bacc as _bacc
    from concourse.bass_utils import run_bass_kernel_spmd as _run

    i = {k: np.asarray(v) for k, v in inputs.items()}
    t = lambda a: np.ascontiguousarray(np.swapaxes(a, -1, -2))
    arrays = {
        "x": i["x"].reshape(N, D),
        "ctx": i["ctx_1024"].reshape(N, D),
        "ctxT": t(i["ctx_1024"].reshape(N, D)),
        "igate_w": t(i["L0_xattn_igate_w"]).reshape(6, 128, 8),
        "fgate_w": t(i["L0_xattn_fgate_w"]).reshape(6, 128, 8),
        "igate_b": i["L0_xattn_igate_b"],
        "fgate_b": i["L0_xattn_fgate_b"],
        "ln_scale": i["L0_xattn_ln_scale"],
        "gate_w": t(i["L0_ffn_gate_w"]),
        "Wg": t(i["L0_ffn_Wg"]), "Wu": t(i["L0_ffn_Wu"]), "Wd": t(i["L0_ffn_Wd"]),
        "Ws_g": t(i["L0_ffn_Ws_g"]), "Ws_u": t(i["L0_ffn_Ws_u"]), "Ws_d": t(i["L0_ffn_Ws_d"]),
        "L1g": i["L1_ffn_Wg"], "bg": i["L1_ffn_bg"],
        "W1": i["L1_ffn_W1"], "b1": t(i["L1_ffn_b1"].reshape(E1, 8, 128)),
        "W2": i["L1_ffn_W2"], "b2": i["L1_ffn_b2"],
        "gamma": i["L1_ffn_gamma"], "beta": i["L1_ffn_beta"],
    }
    nc = _bacc.Bacc("TRN2", target_bir_lowering=False, num_devices=1)
    maps, aps = {}, {}
    for name, a in arrays.items():
        a = np.ascontiguousarray(a)
        maps["in_" + name] = a
        aps[name] = nc.dram_tensor("in_" + name, a.shape, mybir.dt.from_np(a.dtype), kind="ExternalInput").ap()
    out = nc.dram_tensor("out_0", [N, D], FP, kind="ExternalOutput").ap()
    build(nc, aps, out, STOP)
    r = _run(nc, [maps], core_ids=[0])
    return r.results[0]["out_0"].reshape(B, S, D)
```
